# Optimizing a Trainium2 kernel written in Bass

```python
import numpy as np
import jax
import jax.numpy as jnp

def _softmax(x, axis=-1):
    return jax.nn.softmax(x, axis=axis)

def _gelu(x):
    return jax.nn.gelu(x, approximate=True)

def _silu(x):
    return jax.nn.silu(x)

def _sigmoid(x):
    return jax.nn.sigmoid(x)

def _layernorm(x, axis=-1, eps=1e-05):
    m = jnp.mean(x, axis=axis, keepdims=True)
    v = jnp.var(x, axis=axis, keepdims=True)
    return (x - m) / jnp.sqrt(v + eps)

def _scatter_add(tgt, idx, src, axis=0):
    return tgt.at[idx].add(src)

def _segment_sum(src, seg, n):
    return jax.ops.segment_sum(src, seg, n)
kernel_name = 'mk_vit_tower_postln_d2_tok_img1024_r4_203a34'

def setup_inputs(seed: int=0):
    np.random.seed(seed)
    _w = jnp.asarray

    def _rec_inputs():
        import jax
        import jax.numpy as jnp
        _rk = jax.random.key(seed)
        x = 7.22013e-05 + 1.00017 * jax.random.normal(jax.random.fold_in(_rk, 1), (4, 1, 512, 256), jnp.float32)
        return x
    x = _rec_inputs()

    def _L0_tok_setup():
        import jax, jax.numpy as jnp
        import numpy as np
        import math
        EMBED_DIM = 256
        NUM_HEADS = 16
        HEAD_DIM = EMBED_DIM // NUM_HEADS
        INPUT_DIM = 256
        key = jax.random.key(seed)
        k_x, k_wqkv, k_wout = jax.random.split(key, 3)
        x = jax.random.normal(k_x, (4, 1, 512, INPUT_DIM), dtype=jnp.float32)

        def xavier(k, shape):
            fan_out, fan_in = shape
            bound = math.sqrt(6.0 / (fan_in + fan_out))
            return jax.random.uniform(k, shape, jnp.float32, -bound, bound)
        w_qkv = xavier(k_wqkv, (3 * EMBED_DIM, INPUT_DIM))
        b_qkv = jnp.zeros((3 * EMBED_DIM,), jnp.float32)
        w_out = xavier(k_wout, (EMBED_DIM, EMBED_DIM))
        b_out = jnp.zeros((EMBED_DIM,), jnp.float32)
        return {'x': x, 'w_qkv': w_qkv, 'b_qkv': b_qkv, 'w_out': w_out, 'b_out': b_out}
    _L0_tok_all = _L0_tok_setup()
    _L0_tok_in = {k: v for k, v in _L0_tok_all.items() if k in ('w_qkv', 'b_qkv', 'w_out', 'b_out')}
    del _L0_tok_all

    def _L0_attn_setup():
        import jax, jax.numpy as jnp
        import numpy as np
        import math
        N_HEAD = 16
        ROPE_BASE = 10000.0

        def _rope(x):
            S, d = (x.shape[1], x.shape[-1])
            inv_freq = 1.0 / ROPE_BASE ** (jnp.arange(0, d, 2, dtype=jnp.float32) / d)
            t = jnp.arange(S, dtype=jnp.float32)
            freqs = jnp.einsum('i,j->ij', t, inv_freq)
            emb = jnp.concatenate([freqs, freqs], axis=-1)
            cos = jnp.cos(emb)[None, :, None, :]
            sin = jnp.sin(emb)[None, :, None, :]
            x1, x2 = jnp.split(x, 2, axis=-1)
            x_rot = jnp.concatenate([-x2, x1], axis=-1)
            return x * cos + x_rot * sin
        key = jax.random.key(seed)
        ks = jax.random.split(key, 6)
        B, S, D = (2, 512, 256)
        x = jax.random.normal(ks[0], (B, S, D), dtype=jnp.float32)
        w = lambda k: jax.random.normal(k, (D, D), dtype=jnp.float32) * 0.02
        return {'x': x, 'wq': w(ks[1]), 'wk': w(ks[2]), 'wv': w(ks[3]), 'wg': w(ks[4]), 'wo': w(ks[5])}
    _L0_attn_all = _L0_attn_setup()
    _L0_attn_in = {k: v for k, v in _L0_attn_all.items() if k in ('wq', 'wk', 'wv', 'wg', 'wo')}
    del _L0_attn_all

    def _L0_ffn_setup():
        import jax, jax.numpy as jnp
        import numpy as np
        ALPHA = 1.702
        LIMIT = 7.0
        TOP_K = 2
        key = jax.random.key(seed)
        ks = jax.random.split(key, 4)
        B, S, H, E, I = (2, 256, 256, 8, 512)
        return {'hidden_states': jax.random.normal(ks[0], (B, S, H), jnp.float32), 'router_weight': jax.random.normal(ks[1], (E, H), jnp.float32), 'router_bias': jnp.zeros((E,), jnp.float32), 'gate_up_proj': jax.random.normal(ks[2], (E, H, 2 * I), jnp.float32) * 0.02, 'gate_up_bias': jnp.zeros((E, 2 * I), jnp.float32), 'down_proj': jax.random.normal(ks[3], (E, I, H), jnp.float32) * 0.02, 'down_bias': jnp.zeros((E, H), jnp.float32)}
    _L0_ffn_all = _L0_ffn_setup()
    _L0_ffn_in = {k: v for k, v in _L0_ffn_all.items() if k in ('router_weight', 'router_bias', 'gate_up_proj', 'gate_up_bias', 'down_proj', 'down_bias')}
    del _L0_ffn_all

    def _L1_attn_setup():
        import jax, jax.numpy as jnp
        import numpy as np
        D = 256
        H = 16
        HD = D // H
        EPS = 1e-06

        def _rmsnorm(x, w):
            xf = x.astype(jnp.float32)
            var = jnp.mean(xf * xf, axis=-1, keepdims=True)
            return (w * (xf * jax.lax.rsqrt(var + EPS))).astype(x.dtype)
        key = jax.random.key(seed)
        ks = jax.random.split(key, 10)
        B, N = (2, 512)
        s = 0.02
        return {'x': jax.random.normal(ks[0], (B, N, D), jnp.float32), 'Wq': jax.random.normal(ks[1], (D, D + H), jnp.float32) * s, 'bq': jnp.zeros((D + H,), jnp.float32), 'Wk': jax.random.normal(ks[2], (D, D), jnp.float32) * s, 'bk': jnp.zeros((D,), jnp.float32), 'Wv': jax.random.normal(ks[3], (D, D), jnp.float32) * s, 'bv': jnp.zeros((D,), jnp.float32), 'Wo': jax.random.normal(ks[4], (D, D), jnp.float32) * s, 'bo': jnp.zeros((D,), jnp.float32), 'qn_w': jnp.ones((HD,), jnp.float32), 'kn_w': jnp.ones((HD,), jnp.float32)}
    _L1_attn_all = _L1_attn_setup()
    _L1_attn_in = {k: v for k, v in _L1_attn_all.items() if k in ('Wq', 'bq', 'Wk', 'bk', 'Wv', 'bv', 'Wo', 'bo', 'qn_w', 'kn_w')}
    del _L1_attn_all

    def _L1_ffn_setup():
        import jax, jax.numpy as jnp
        import numpy as np
        BS, SLEN, DIM = (1, 512, 256)
        NUM_EXPERTS, TOP_K = (8, 2)
        HID = 352

        def _masked_grouped_mm(x, w, onehot):
            g = jnp.einsum('tk,gnk->tgn', x, w, preferred_element_type=jnp.float32)
            return jnp.einsum('tgn,tg->tn', g, onehot)

        def moe_forward(x, gate_w, expert_bias, w_up, w_down, shared_w_up, shared_w_down):
            bs, slen, dim = x.shape
            xf = x.reshape(-1, dim)
            scores = jax.nn.sigmoid((xf @ gate_w.T).astype(jnp.float32))
            biased = scores + expert_bias
            _, sel = jax.lax.top_k(biased, TOP_K)
            top_scores = jnp.take_along_axis(scores, sel, axis=-1)
            flat_sel = sel.reshape(-1)
            counts = jnp.bincount(flat_sel, length=NUM_EXPERTS)
            order = jnp.argsort(flat_sel, stable=True)
            scores_sorted = top_scores.reshape(-1)[order]
            token_ids = order // TOP_K
            routed_in = (xf[token_ids] * scores_sorted[:, None]).astype(x.dtype)
            seg = jnp.repeat(jnp.arange(NUM_EXPERTS), counts, total_repeat_length=flat_sel.shape[0])
            onehot = jax.nn.one_hot(seg, NUM_EXPERTS, dtype=jnp.float32)
            h = _masked_grouped_mm(routed_in.astype(jnp.bfloat16), w_up.astype(jnp.bfloat16), onehot)
            h = jnp.square(jax.nn.relu(h.astype(jnp.bfloat16)))
            routed_out = _masked_grouped_mm(h.astype(jnp.bfloat16), w_down.astype(jnp.bfloat16), onehot)
            routed_out = routed_out.astype(jnp.bfloat16).astype(x.dtype)
            hs = jnp.square(jax.nn.relu(xf @ shared_w_up.T))
            shared_out = hs @ shared_w_down.T
            combined = jnp.zeros((flat_sel.shape[0], dim), routed_out.dtype).at[order].set(routed_out)
            out = combined.reshape(-1, TOP_K, dim).sum(axis=1) + shared_out
            return out.reshape(bs, slen, dim)
        key = jax.random.key(seed)
        k = jax.random.split(key, 6)
        s = 0.02
        return {'x': jax.random.normal(k[0], (BS, SLEN, DIM), jnp.float32), 'gate_w': jax.random.normal(k[1], (NUM_EXPERTS, DIM), jnp.float32) * s, 'expert_bias': jnp.zeros((NUM_EXPERTS,), jnp.float32), 'w_up': jax.random.normal(k[2], (NUM_EXPERTS, HID, DIM), jnp.float32) * s, 'w_down': jax.random.normal(k[3], (NUM_EXPERTS, DIM, HID), jnp.float32) * s, 'shared_w_up': jax.random.normal(k[4], (HID, DIM), jnp.float32) * s, 'shared_w_down': jax.random.normal(k[5], (DIM, HID), jnp.float32) * s}
    _L1_ffn_all = _L1_ffn_setup()
    _L1_ffn_in = {k: v for k, v in _L1_ffn_all.items() if k in ('gate_w', 'expert_bias', 'w_up', 'w_down', 'shared_w_up', 'shared_w_down')}
    del _L1_ffn_all
    return {'x': x, 'L0_tok_w_qkv': _L0_tok_in['w_qkv'], 'L0_tok_b_qkv': _L0_tok_in['b_qkv'], 'L0_tok_w_out': _L0_tok_in['w_out'], 'L0_tok_b_out': _L0_tok_in['b_out'], 'L0_attn_wq': _L0_attn_in['wq'], 'L0_attn_wk': _L0_attn_in['wk'], 'L0_attn_wv': _L0_attn_in['wv'], 'L0_attn_wg': _L0_attn_in['wg'], 'L0_attn_wo': _L0_attn_in['wo'], 'L0_ffn_router_weight': _L0_ffn_in['router_weight'], 'L0_ffn_router_bias': _L0_ffn_in['router_bias'], 'L0_ffn_gate_up_proj': _L0_ffn_in['gate_up_proj'], 'L0_ffn_gate_up_bias': _L0_ffn_in['gate_up_bias'], 'L0_ffn_down_proj': _L0_ffn_in['down_proj'], 'L0_ffn_down_bias': _L0_ffn_in['down_bias'], 'L1_attn_Wq': _L1_attn_in['Wq'], 'L1_attn_bq': _L1_attn_in['bq'], 'L1_attn_Wk': _L1_attn_in['Wk'], 'L1_attn_bk': _L1_attn_in['bk'], 'L1_attn_Wv': _L1_attn_in['Wv'], 'L1_attn_bv': _L1_attn_in['bv'], 'L1_attn_Wo': _L1_attn_in['Wo'], 'L1_attn_bo': _L1_attn_in['bo'], 'L1_attn_qn_w': _L1_attn_in['qn_w'], 'L1_attn_kn_w': _L1_attn_in['kn_w'], 'L1_ffn_gate_w': _L1_ffn_in['gate_w'], 'L1_ffn_expert_bias': _L1_ffn_in['expert_bias'], 'L1_ffn_w_up': _L1_ffn_in['w_up'], 'L1_ffn_w_down': _L1_ffn_in['w_down'], 'L1_ffn_shared_w_up': _L1_ffn_in['shared_w_up'], 'L1_ffn_shared_w_down': _L1_ffn_in['shared_w_down']}

def reference(x, L0_tok_w_qkv, L0_tok_b_qkv, L0_tok_w_out, L0_tok_b_out, L0_attn_wq, L0_attn_wk, L0_attn_wv, L0_attn_wg, L0_attn_wo, L0_ffn_router_weight, L0_ffn_router_bias, L0_ffn_gate_up_proj, L0_ffn_gate_up_bias, L0_ffn_down_proj, L0_ffn_down_bias, L1_attn_Wq, L1_attn_bq, L1_attn_Wk, L1_attn_bk, L1_attn_Wv, L1_attn_bv, L1_attn_Wo, L1_attn_bo, L1_attn_qn_w, L1_attn_kn_w, L1_ffn_gate_w, L1_ffn_expert_bias, L1_ffn_w_up, L1_ffn_w_down, L1_ffn_shared_w_up, L1_ffn_shared_w_down):
    import jax
    import jax.numpy as jnp

    def _L0_tok_ref(x, w_qkv, b_qkv, w_out, b_out):
        import jax, jax.numpy as jnp
        import numpy as np
        import math
        EMBED_DIM = 256
        NUM_HEADS = 16
        HEAD_DIM = EMBED_DIM // NUM_HEADS
        INPUT_DIM = 256
        B, y, S, _ = x.shape
        qkv = jnp.einsum('bysd,ed->byse', x, w_qkv) + b_qkv
        qkv = qkv.reshape(B, S, NUM_HEADS, 3 * HEAD_DIM).transpose(0, 2, 1, 3)
        q, k, v = jnp.split(qkv, 3, axis=-1)
        logits = jnp.einsum('bhqd,bhkd->bhqk', q, k) / math.sqrt(HEAD_DIM)
        attn = jax.nn.softmax(logits, axis=-1)
        vals = jnp.einsum('bhqk,bhkd->bhqd', attn, v)
        vals = vals.transpose(0, 2, 1, 3).reshape(B, S, EMBED_DIM)
        return jnp.einsum('bse,oe->bso', vals, w_out) + b_out

    def _L0_attn_ref(x, wq, wk, wv, wg, wo):
        import jax, jax.numpy as jnp
        import numpy as np
        import math
        N_HEAD = 16
        ROPE_BASE = 10000.0

        def _rope(x):
            S, d = (x.shape[1], x.shape[-1])
            inv_freq = 1.0 / ROPE_BASE ** (jnp.arange(0, d, 2, dtype=jnp.float32) / d)
            t = jnp.arange(S, dtype=jnp.float32)
            freqs = jnp.einsum('i,j->ij', t, inv_freq)
            emb = jnp.concatenate([freqs, freqs], axis=-1)
            cos = jnp.cos(emb)[None, :, None, :]
            sin = jnp.sin(emb)[None, :, None, :]
            x1, x2 = jnp.split(x, 2, axis=-1)
            x_rot = jnp.concatenate([-x2, x1], axis=-1)
            return x * cos + x_rot * sin
        B, S, D = x.shape
        H = N_HEAD
        Dh = D // H
        q = (x @ wq.T).reshape(B, S, H, Dh)
        k = (x @ wk.T).reshape(B, S, H, Dh)
        v = (x @ wv.T).reshape(B, S, H, Dh)
        q = _rope(q)
        k = _rope(k)
        q = q.transpose(0, 2, 1, 3)
        k = k.transpose(0, 2, 1, 3)
        v = v.transpose(0, 2, 1, 3)
        idx = jnp.arange(S)
        d_mask = jnp.tril(idx[:, None] - idx[None, :]).astype(jnp.float32)
        gamma = 1.0 - jnp.exp2(-5.0 - jnp.arange(H, dtype=jnp.float32))
        causal = jnp.tril(jnp.ones((S, S), dtype=jnp.float32))
        decay_matrix = jnp.power(gamma[:, None, None], d_mask) * causal
        retention = jnp.einsum('bhsd,bhtd->bhst', q, k) / math.sqrt(Dh)
        retention = retention * decay_matrix[None]
        out = jnp.einsum('bhst,bhtd->bhsd', retention, v)
        out = out.transpose(0, 2, 1, 3).reshape(B, S, D)
        g = jax.nn.silu(x @ wg.T)
        return out * g @ wo.T

    def _L0_ffn_ref(hidden_states, router_weight, router_bias, gate_up_proj, gate_up_bias, down_proj, down_bias):
        import jax, jax.numpy as jnp
        import numpy as np
        ALPHA = 1.702
        LIMIT = 7.0
        TOP_K = 2
        B, S, H = hidden_states.shape
        E, _, two_I = gate_up_proj.shape
        I = two_I // 2
        flat = hidden_states.reshape(B * S, H)
        logits = flat @ router_weight.T + router_bias
        scores = jax.nn.softmax(logits, axis=-1)
        topk_w, topk_idx = jax.lax.top_k(scores, TOP_K)
        gu = jnp.einsum('th,ehn->ten', flat, gate_up_proj) + gate_up_bias
        gate = jnp.minimum(gu[..., :I], LIMIT)
        up = jnp.clip(gu[..., I:], -LIMIT, LIMIT)
        glu = gate * jax.nn.sigmoid(gate * ALPHA)
        act = (up + 1.0) * glu
        down = jnp.einsum('tei,eih->teh', act, down_proj) + down_bias
        gathered = jnp.take_along_axis(down, topk_idx[:, :, None], axis=1)
        out = (gathered * topk_w[:, :, None]).sum(axis=1)
        return out.reshape(B, S, H)

    def _L1_attn_ref(x, Wq, bq, Wk, bk, Wv, bv, Wo, bo, qn_w, kn_w):
        import jax, jax.numpy as jnp
        import numpy as np
        D = 256
        H = 16
        HD = D // H
        EPS = 1e-06

        def _rmsnorm(x, w):
            xf = x.astype(jnp.float32)
            var = jnp.mean(xf * xf, axis=-1, keepdims=True)
            return (w * (xf * jax.lax.rsqrt(var + EPS))).astype(x.dtype)
        B, N, _ = x.shape
        qg = x @ Wq + bq
        Q, gate = (qg[..., :D], qg[..., D:])
        K = x @ Wk + bk
        V = x @ Wv + bv
        Q = Q.reshape(B, N, H, HD).transpose(0, 2, 1, 3)
        K = K.reshape(B, N, H, HD).transpose(0, 2, 1, 3)
        V = V.reshape(B, N, H, HD).transpose(0, 2, 1, 3)
        Q = _rmsnorm(Q, qn_w)
        K = _rmsnorm(K, kn_w)
        scores = jnp.einsum('bhqd,bhkd->bhqk', Q, K) / jnp.sqrt(jnp.float32(HD))
        attn = jax.nn.softmax(scores.astype(jnp.float32), axis=-1).astype(Q.dtype)
        out = jnp.einsum('bhqk,bhkd->bhqd', attn, V)
        out = out.transpose(0, 2, 1, 3)
        out = out * jax.nn.sigmoid(gate)[..., None]
        out = out.reshape(B, N, D)
        return out @ Wo + bo

    def _L1_ffn_ref(x, gate_w, expert_bias, w_up, w_down, shared_w_up, shared_w_down):
        import jax, jax.numpy as jnp
        import numpy as np
        BS, SLEN, DIM = (1, 512, 256)
        NUM_EXPERTS, TOP_K = (8, 2)
        HID = 352

        def _masked_grouped_mm(x, w, onehot):
            g = jnp.einsum('tk,gnk->tgn', x, w, preferred_element_type=jnp.float32)
            return jnp.einsum('tgn,tg->tn', g, onehot)

        def moe_forward(x, gate_w, expert_bias, w_up, w_down, shared_w_up, shared_w_down):
            bs, slen, dim = x.shape
            xf = x.reshape(-1, dim)
            scores = jax.nn.sigmoid((xf @ gate_w.T).astype(jnp.float32))
            biased = scores + expert_bias
            _, sel = jax.lax.top_k(biased, TOP_K)
            top_scores = jnp.take_along_axis(scores, sel, axis=-1)
            flat_sel = sel.reshape(-1)
            counts = jnp.bincount(flat_sel, length=NUM_EXPERTS)
            order = jnp.argsort(flat_sel, stable=True)
            scores_sorted = top_scores.reshape(-1)[order]
            token_ids = order // TOP_K
            routed_in = (xf[token_ids] * scores_sorted[:, None]).astype(x.dtype)
            seg = jnp.repeat(jnp.arange(NUM_EXPERTS), counts, total_repeat_length=flat_sel.shape[0])
            onehot = jax.nn.one_hot(seg, NUM_EXPERTS, dtype=jnp.float32)
            h = _masked_grouped_mm(routed_in.astype(jnp.bfloat16), w_up.astype(jnp.bfloat16), onehot)
            h = jnp.square(jax.nn.relu(h.astype(jnp.bfloat16)))
            routed_out = _masked_grouped_mm(h.astype(jnp.bfloat16), w_down.astype(jnp.bfloat16), onehot)
            routed_out = routed_out.astype(jnp.bfloat16).astype(x.dtype)
            hs = jnp.square(jax.nn.relu(xf @ shared_w_up.T))
            shared_out = hs @ shared_w_down.T
            combined = jnp.zeros((flat_sel.shape[0], dim), routed_out.dtype).at[order].set(routed_out)
            out = combined.reshape(-1, TOP_K, dim).sum(axis=1) + shared_out
            return out.reshape(bs, slen, dim)
        return moe_forward(x, gate_w, expert_bias, w_up, w_down, shared_w_up, shared_w_down)
    h = _L0_tok_ref(x, L0_tok_w_qkv, L0_tok_b_qkv, L0_tok_w_out, L0_tok_b_out)
    h = _layernorm(h + _L0_attn_ref(h, L0_attn_wq, L0_attn_wk, L0_attn_wv, L0_attn_wg, L0_attn_wo), axis=-1)
    h = _layernorm(h + _L0_ffn_ref(h, L0_ffn_router_weight, L0_ffn_router_bias, L0_ffn_gate_up_proj, L0_ffn_gate_up_bias, L0_ffn_down_proj, L0_ffn_down_bias), axis=-1)
    h = _layernorm(h + _L1_attn_ref(h, L1_attn_Wq, L1_attn_bq, L1_attn_Wk, L1_attn_bk, L1_attn_Wv, L1_attn_bv, L1_attn_Wo, L1_attn_bo, L1_attn_qn_w, L1_attn_kn_w), axis=-1)
    h = _layernorm(h + _L1_ffn_ref(h, L1_ffn_gate_w, L1_ffn_expert_bias, L1_ffn_w_up, L1_ffn_w_down, L1_ffn_shared_w_up, L1_ffn_shared_w_down), axis=-1)
    return h

_drawn_inputs = setup_inputs


def setup_inputs(seed=0):
    import zlib

    import numpy as np

    out = dict(_drawn_inputs(seed))
    spreads = {'L0_tok_b_qkv': (0.0, 0.1),
     'L0_tok_b_out': (0.0, 0.1),
     'L0_ffn_router_bias': (0.0, 2.0),
     'L0_ffn_gate_up_bias': (0.0, 0.295),
     'L0_ffn_down_bias': (0.0, 0.1),
     'L1_attn_bq': (0.0, 0.8),
     'L1_attn_bk': (0.0, 2.0),
     'L1_attn_bv': (0.0, 0.45),
     'L1_attn_bo': (0.0, 0.1),
     'L1_attn_qn_w': (1.0, 0.6),
     'L1_attn_kn_w': (1.0, 0.6),
     'L1_ffn_expert_bias': (0.0, 0.585)}
    factors = {'L0_attn_wq': 8.0,
     'L0_attn_wk': 8.0,
     'L0_attn_wv': 8.0,
     'L0_attn_wg': 8.0,
     'L0_attn_wo': 8.0,
     'L1_attn_Wq': 6.396,
     'L1_attn_Wk': 8.0,
     'L1_ffn_gate_w': 3.656,
     'L1_ffn_w_up': 3.146,
     'L1_ffn_w_down': 3.091}
    for name, (base, spread) in spreads.items():
        noise = np.random.default_rng([zlib.crc32(name.encode()), seed]).standard_normal(out[name].shape)
        drawn = base * np.exp(spread * noise) if base else spread * noise
        out[name] = jnp.asarray(drawn.astype(out[name].dtype))
    for name, factor in factors.items():
        out[name] = (out[name] * factor).astype(out[name].dtype)
    return out
```

```python
from contextlib import ExitStack

import numpy as np

import concourse.bass as bass
from concourse import mybir

F32 = mybir.dt.float32
BF16 = mybir.dt.bfloat16
I32 = mybir.dt.int32
U32 = mybir.dt.uint32
ALU = mybir.AluOpType
ACT = mybir.ActivationFunctionType
AX_X = mybir.AxisListType.X

P = 128
B = 4
S = 512
D = 256
H = 16
HD = D // H
KD = D // P
TT = S // P
NT = B * TT
HG = H // 4
Q_PART = (0, 0, 0, 1, 1, 2)
K_PART = (0, 1, 2, 0, 1, 0)
SK = HD * len(Q_PART)
E = 8
FI = 512
LIMIT = 7.0
HID = 352
HIDP = 384
NS = 40
ZCOLS = 1280
LN_EPS = 1e-5
RMS_EPS = 1e-6
TURN_AT = 3
MAX_LAG = 5


class Chain:

    def __init__(self, eng, sem):
        self.eng, self.sem, self.n = eng, sem, 0

    def mark(self, ins):
        ins.then_inc(self.sem, 1)
        self.n += 1
        return self.n

    def wait(self, n=None):
        self.eng.wait_ge(self.sem, self.n if n is None else n)



def max_heads(h):
    steps = H - MAX_LAG
    return range(H * (h - MAX_LAG) // steps, H * (h - MAX_LAG + 1) // steps) if h >= MAX_LAG else ()


def semaphores(nc, ctx, prefix):
    taken = []

    def sem(name):
        taken.append(nc.alloc_semaphore(prefix + name))
        return taken[-1]

    def give_back():
        nc.clear_and_free_semaphores(taken)
        nc.all_engine_barrier()

    ctx.callback(give_back)
    return sem


def spread(ap, shape):
    return ap.broadcast_to(shape)


def attention(nc, kind, env, dram):
    P_SLOTS = 6 if kind != "ret" else 5
    tok, ret, rmsn = kind == "tok", kind == "ret", kind == "rms"
    softmax = not ret
    htok, ident = env["htok"], env["ident"]
    scratch = dram["scratch"]
    RU_PROJ = 4 if tok else KD + TT + 4
    RU_MAX = H * TT + 1 if softmax else 0
    RU_V = 2 if tok else TT
    RU = RU_PROJ + RU_MAX + RU_V
    OU = HG + TT + KD + 2
    NW = {"tok": 768, "ret": 1024, "rms": 784}[kind]
    WV = NW - 512
    PCOLS = TT * S if softmax else TT * S - P * (1 + 2 + 3)

    with ExitStack() as ctx:
        def sb(name, shape, dt=F32):
            return ctx.enter_context(nc.sbuf_tensor(f"{kind}_{name}", shape, dt))

        def ps(name, shape, dt=F32):
            return ctx.enter_context(nc.psum_tensor(f"{kind}_{name}", shape, dt))

        sem = semaphores(nc, ctx, f"{kind}_")

        w_in = sb("w_in", [P, KD, NW])
        w_o = sb("w_o", [P, KD, D])
        loads = [(w_in[:, :, :], dram[f"{kind}_w_in"].rearrange("(k p) n -> p k n", p=P)),
                 (w_o[:, :, :], dram[f"{kind}_w_o"].rearrange("(k p) n -> p k n", p=P))]
        if softmax:
            bias_o = sb("bias_o", [P, D])
            loads.append((bias_o[:, :], dram[f"{kind}_b_o"].partition_broadcast(P)))
            rowmax = sb("rowmax", [P, H * TT])
            negm = sb("negm", [H * TT, 2, P])
            mparts = sb("mparts", [H * TT, 3, P], BF16)
            rden = sb("rden", [P, TT, H])
        if tok:
            bias_qk = sb("bias_qk", [P, 4])
            bias_v = sb("bias_v", [P, D])
            loads += [(bias_qk[:, :], dram["tok_b_qk"]), (bias_v[:, :], dram["tok_b_v"].partition_broadcast(P))]
        if rmsn:
            bias_in = sb("bias_in", [P, NW])
            norm_w = sb("norm_w", [P, 2, HD])
            ssq = sb("ssq", [P, 32])
            rms = sb("rms", [P, 32])
            gate = sb("gate", [P, 2, TT, H])
            graw = sb("graw", [P, H])
            loads += [(bias_in[:, :], dram["rms_b_in"].partition_broadcast(P)),
                      (norm_w[:, :, :].rearrange("p k d -> p (k d)"), dram["rms_norm_w"].partition_broadcast(P))]
        if ret:
            decay = sb("decay", [P, H, S])
            cos = sb("cos", [P, TT, 8])
            sin = sb("sin", [P, TT, 8])
            gate = sb("gate", [P, 2, TT, D])
            tmp2 = sb("tmp2", [P, S])
            loads += [(decay[:, :, :].rearrange("p h n -> p (h n)"), dram["decay"]),
                      (cos[:, :, :], dram["cos"].rearrange("(t p) r -> p t r", p=P)),
                      (sin[:, :, :], dram["sin"].rearrange("(t p) r -> p t r", p=P))]
        if not tok:
            stats = sb("stats", [P, 6])
            mv = sb("mv", [P, NT, 2])
            veps = sb("veps", [P, NT])
            rstd = sb("rstd", [P, NT])
            half = sb("half", [P, 32])
            qk = sb("qk", [P, S])
            tmp = sb("tmp", [P, S])
        ht = sb("ht", [P, 2 if tok else 1, KD, S])
        qf = sb("qf", [P, 2, S])
        rest = sb("rest", [P, S])
        parts = sb("parts", [P, 2, 3, S], BF16)
        qs = sb("qs", [SK + 3, 2, H, S], BF16)
        ks = sb("ks", [SK + 3, 2, H, S], BF16)
        v = sb("v", [P, TT, H, 32])
        prob = sb("prob", [P, P_SLOTS, PCOLS])
        ot = sb("ot", [P, HG, S])
        rot = ot
        otok = sb("otok", [P, TT, D])
        ot2 = sb("ot2", [P, KD, S])

        ring = ps("ring", [P, 2, S])
        score = ps("score", [P, 2, 2, S])
        outps = ps("outps", [P, 2, S])

        weights_in = sem("weights_in")
        x_in = [sem(f"x_in{i}") for i in range(2)]
        key_ones = sem("key_ones")
        rstd_ready = sem("rstd_ready")
        consts_set = sem("consts_set")
        ring_filled = sem("ring_filled")
        ht_ready = sem("ht_ready")
        qk_ready = sem("qk_ready")
        qk_used = sem("qk_used")
        sq_ready = sem("sq_ready")
        ssq_ready = sem("ssq_ready")
        rot_ready = sem("rot_ready")
        qf_ready = sem("qf_ready")
        qf_used = sem("qf_used")
        parts_ready = sem("parts_ready")
        parts_saved = [sem(f"parts_saved{i}") for i in range(2)]
        stacked = [sem(f"stacked{i}") for i in range(2)]
        max_done = sem("max_done")
        negm_ready = sem("negm_ready")
        mparts_ready = sem("mparts_ready")
        maxrows_in = [sem(f"maxrows_in{i}") for i in range(2)]
        score_filled = sem("score_filled")
        prob_ready = sem("prob_ready")
        v_ready = sem("v_ready")
        graw_ready = sem("graw_ready")
        gexp_ready = sem("gexp_ready")
        gate_ready = sem("gate_ready")
        out_filled = sem("out_filled")
        ot_ready = sem("ot_ready")
        rden_ready = sem("rden_ready")
        otok_ready = sem("otok_ready")
        ot2_ready = sem("ot2_ready")
        y_ready = sem("y_ready")
        stats_ready = sem("stats_ready")
        pool_step = sem("pool_step")
        dve_step = sem("dve_step")

        def ring_use(b, u):
            return u % 2, b * RU + u + 1

        def ring_release(b, u):
            if tok and u < RU_PROJ:
                return qf_ready, 4 * b + u + 1
            if not tok and u < KD:
                return ht_ready, KD * b + u + 1
            if not tok and u < KD + TT:
                return qk_ready, TT * b + u - KD + 1
            if u < RU_PROJ:
                return qf_ready, 4 * b + u - KD - TT + 1
            if u < RU_PROJ + RU_MAX - 1:
                return max_done, H * TT * b + u - RU_PROJ + 1
            if u < RU_PROJ + RU_MAX:
                return negm_ready, b + 1
            n = RU_V * b + u - RU_PROJ - RU_MAX + 1
            return (v_ready, n) if tok else (gate_ready, n) if ret else (graw_ready, n)

        def out_use(b, u):
            return 1 if u < HG else (u - HG) % 2, b * OU + u + 1

        def out_release(b, u):
            if u < HG:
                return ot_ready, HG * b + u + 1
            if u < HG + TT:
                return otok_ready, TT * b + u - HG + 1
            if u < HG + TT + KD:
                return ot2_ready, KD * b + u - HG - TT + 1
            return y_ready, 2 * b + u - HG - TT - KD + 1

        def kt_cols(kt):
            return (0, kt * S) if softmax else (kt * P, kt * S - P * (kt * (kt - 1) // 2))

        def slot_free(eng, b, h):
            old = H * b + h - P_SLOTS
            if old >= 0:
                eng.wait_ge(out_filled, OU * (old // H) + (old % H) // 4 + 1)

        block = ctx.enter_context(nc.Block())

        @block.sync
        def _(sp):
            for dst, src in loads:
                sp.dma_start(dst, src).then_inc(weights_in, 16)

            def load_x(b):
                if b >= 2:
                    sp.wait_ge(ring_filled, (b - 1) * RU)
                sp.dma_start(ht[:, b % 2, :, :],
                             dram["x"].rearrange("(k p) n -> p k n", p=P)[:, :, b * S:(b + 1) * S]).then_inc(x_in[b % 2], 16)

            def stack(b):
                for f in range(4):
                    side, heads = f // 2, slice(H // 2 * (f % 2), H // 2 * (f % 2) + H // 2)
                    sp.wait_ge(parts_ready, 4 * b + f + 1)
                    for g, part in enumerate(K_PART if side else Q_PART):
                        sp.dma_start(scratch[b, side, HD * g:HD * g + HD, heads, :].rearrange("d h n -> h d n"),
                                     parts[:, f % 2, part, :]).then_inc(parts_saved[f % 2], 16)
                    sp.wait_ge(parts_saved[f % 2], 16 * 6 * (2 * b + side + 1))
                    if b >= 2:
                        sp.wait_ge(score_filled, 2 * H * (b - 1))
                    sp.dma_start((ks if side else qs)[0:SK, b % 2, heads, :].rearrange("p h n -> p (h n)"),
                                 scratch[b, side, :, heads, :].rearrange("p h n -> p (h n)")
                                 ).then_inc(stacked[b % 2], 16)

            def max_rows(b):
                sp.wait_ge(mparts_ready, b + 1)
                for j in range(3):
                    sp.dma_start(qs[SK + j:SK + j + 1, b % 2, :, :].rearrange("o h (t q) -> o (h t) q", q=P),
                                 mparts[:, j, :]).then_inc(maxrows_in[b % 2], 16)

            if tok:
                load_x(0)
            for hook in env.get(f"{kind}_dmas", ()):
                hook(sp)
            for b in range(B):
                if tok and b + 1 < B:
                    load_x(b + 1)
                stack(b)
                if softmax:
                    max_rows(b)

        @block.gpsimd
        def _(pool):
            chain = Chain(pool, pool_step)
            pool.memset(v[:, :, :, HD:32], 1.0).then_inc(consts_set, 1)
            if not tok:
                pool.memset(half[:, :], -0.5).then_inc(consts_set, 1)
                pool.wait_ge(consts_set, 2)
                pool.wait_ge(weights_in, 16 * len(loads))

            def rope(b):
                for t in range(TT):
                    n = TT * b + t
                    pool.wait_ge(qk_ready, n + 1)
                    eights = lambda a: a.rearrange("p (a r) -> p a r", r=8)
                    c = spread(cos[:, t, :].rearrange("p (a r) -> p a r", a=1), [P, 64, 8])
                    s = spread(sin[:, t, :].rearrange("p (a r) -> p a r", a=1), [P, 64, 8])
                    chain.mark(pool.tensor_tensor(eights(tmp[:, :]), eights(qk[:, :]), c, ALU.mult))
                    pool.tensor_tensor(eights(tmp2[:, :]), eights(qk[:, :]), s, ALU.mult).then_inc(qk_used, 1)
                    pool.wait_ge(qk_used, n + 1)
                    chain.wait()
                    halves = lambda a: a.rearrange("p (h s r) -> p h s r", s=2, r=8)
                    a, z, r = halves(tmp[:, :]), halves(tmp2[:, :]), halves(rot[:, t, :])
                    if b and t == 0:
                        if b >= 2:
                            pool.wait_ge(out_filled, OU * (b - 2) + HG + TT)
                    chain.mark(pool.tensor_tensor(r[:, :, 0, :], a[:, :, 0, :], z[:, :, 1, :], ALU.subtract))
                    pool.tensor_tensor(r[:, :, 1, :], a[:, :, 1, :], z[:, :, 0, :], ALU.add).then_inc(rot_ready, 1)
                    pool.wait_ge(rot_ready, n + 1)
                    chain.wait()

            def rmsnorm(b):
                for t in range(TT):
                    n = TT * b + t
                    pool.wait_ge(qk_ready, n + 1)
                    pool.tensor_tensor(tmp[:, :], qk[:, :], qk[:, :], ALU.mult).then_inc(sq_ready, 1)
                    pool.wait_ge(ssq_ready, n + 1)
                    chain.mark(pool.tensor_scalar(ssq[:, :], ssq[:, :], 1.0 / HD, RMS_EPS, ALU.mult, ALU.add))
                    chain.wait()
                    chain.mark(pool.tensor_tensor(rms[:, :], ssq[:, :], half[:, :], ALU.pow))
                    chain.wait()
                    heads = lambda a: a.rearrange("p (a d) -> p a d", d=HD)
                    pool.tensor_tensor(heads(tmp[:, :]), heads(qk[:, :]),
                                       spread(rms[:, :].rearrange("p (a o) -> p a o", o=1), [P, 32, HD]),
                                       ALU.mult).then_inc(qk_used, 1)
                    pool.wait_ge(qk_used, n + 1)
                    if b >= 2 and t == 0:
                        pool.wait_ge(out_filled, OU * (b - 2) + HG + TT)
                    for i in range(2):
                        w = spread(norm_w[:, i:i + 1, :], [P, H, HD])
                        last = pool.tensor_tensor(heads(rot[:, t, D * i:D * i + D]), heads(tmp[:, D * i:D * i + D]), w,
                                                  ALU.mult)
                        if i == 0:
                            chain.mark(last)
                    last.then_inc(rot_ready, 1)
                    pool.wait_ge(rot_ready, n + 1)
                    chain.wait()

            def split(b):
                for f in range(4):
                    n = 4 * b + f
                    pool.wait_ge(qf_ready, n + 1)
                    if n >= 2:
                        pool.wait_ge(parts_saved[f % 2], 16 * 6 * (n // 2))
                    part = parts[:, f % 2, :, :]
                    chain.mark(pool.tensor_copy(part[:, 0, :], qf[:, f % 2, :]))
                    chain.wait()
                    pool.tensor_tensor(rest[:, :], qf[:, f % 2, :], part[:, 0, :], ALU.subtract).then_inc(qf_used, 1)
                    pool.wait_ge(qf_used, n + 1)
                    chain.mark(pool.tensor_copy(part[:, 1, :], rest[:, :]))
                    chain.wait()
                    pool.tensor_tensor(part[:, 2, :], rest[:, :], part[:, 1, :], ALU.subtract).then_inc(parts_ready, 1)
                    pool.wait_ge(parts_ready, n + 1)

            def split_max(b):
                pool.wait_ge(negm_ready, b + 1)
                if b:
                    pool.wait_ge(maxrows_in[(b - 1) % 2], 48 * ((b - 1) // 2 + 1))
                a, r = negm[:, 0, :], negm[:, 1, :]
                chain.mark(pool.tensor_copy(mparts[:, 0, :], a))
                chain.wait()
                chain.mark(pool.tensor_tensor(r, a, mparts[:, 0, :], ALU.subtract))
                chain.wait()
                chain.mark(pool.tensor_copy(mparts[:, 1, :], r))
                chain.wait()
                pool.tensor_tensor(mparts[:, 2, :], r, mparts[:, 1, :], ALU.subtract).then_inc(mparts_ready, 1)
                pool.wait_ge(mparts_ready, b + 1)

            def gates(b):
                for t in range(TT):
                    n = TT * b + t
                    pool.wait_ge(gexp_ready, n + 1)
                    pool.tensor_scalar(gate[:, b % 2, t, :], gate[:, b % 2, t, :], 1.0, None,
                                       ALU.add).then_inc(gate_ready, 1)

            for b in range(B):
                if ret:
                    rope(b)
                if rmsn:
                    rmsnorm(b)
                split(b)
                if softmax:
                    split_max(b)
                if rmsn:
                    gates(b)
            if not tok:
                pool.wait_ge(stats_ready, NT)
                chain.mark(pool.tensor_scalar(veps[:, :], mv[:, :, 1], 1.0, LN_EPS, ALU.mult, ALU.add))
                chain.wait()
                pool.tensor_tensor(rstd[:, :], veps[:, :], half[:, 0:NT], ALU.pow).then_inc(rstd_ready, 1)
                pool.wait_ge(rstd_ready, 1)
                for n in range(1, NT, 2):
                    pool.tensor_scalar(htok[:, n, :], htok[:, n, :], mv[:, n, 0:1], rstd[:, n:n + 1],
                                       ALU.subtract, ALU.mult)

        @block.tensor
        def _(pe):
            pe.wait_ge(weights_in, 16 * len(loads))

            def use_ring(b, u):
                bank, _ = ring_use(b, u)
                if u >= 2:
                    pe.wait_ge(*ring_release(b, u - 2))
                elif b:
                    last = RU - 1 if (RU - 1) % 2 == bank else RU - 2
                    pe.wait_ge(*ring_release(b - 1, last))
                return ring[:, bank, :]

            def use_out(b, u):
                bank, _ = out_use(b, u)
                if 0 < u < HG:
                    pe.wait_ge(*out_release(b, u - 1))
                elif u == 0 and b:
                    pe.wait_ge(*out_release(b - 1, OU - 1))
                elif u == HG and b:
                    pe.wait_ge(*out_release(b - 1, OU - 2))
                elif u == HG + 1:
                    pe.wait_ge(*out_release(b, HG - 1))
                elif u > HG + 1:
                    pe.wait_ge(*out_release(b, u - 2))
                return outps[:, bank, :]

            def project(b):
                if tok:
                    pe.wait_ge(x_in[b % 2], 16 * (b // 2 + 1))
                    for f in range(4):
                        dst = use_ring(b, f)
                        for k in range(KD):
                            mm = pe.matmul(dst, w_in[:, k, P * f:P * f + P], ht[:, b % 2, k, :],
                                           start=(k == 0), stop=(k == KD - 1))
                        mm.then_inc(ring_filled, 1)
                    return
                for k in range(KD):
                    dst = use_ring(b, k)
                    for t in range(TT):
                        mm = pe.transpose(dst[:, P * t:P * t + P], htok[:, TT * b + t, P * k:P * k + P], ident[:, :])
                    mm.then_inc(ring_filled, 1)
                pe.wait_ge(ht_ready, KD * (b + 1))
                for t in range(TT):
                    dst = use_ring(b, KD + t)
                    for k in range(KD):
                        mm = pe.matmul(dst, ht[:, 0, k, P * t:P * t + P], w_in[:, k, 0:512],
                                       start=(k == 0), stop=(k == KD - 1))
                    mm.then_inc(ring_filled, 1)

            def turn_qk(b):
                pe.wait_ge(rot_ready, TT * (b + 1))
                for f in range(4):
                    dst = use_ring(b, KD + TT + f)
                    for t in range(TT):
                        mm = pe.transpose(dst[:, P * t:P * t + P], rot[:, t, P * f:P * f + P], ident[:, :])
                    mm.then_inc(ring_filled, 1)

            def project_v(b):
                for u in range(RU_V):
                    dst = use_ring(b, RU_PROJ + RU_MAX + u)
                    per = TT // RU_V
                    for i in range(per):
                        t = per * u + i
                        for k in range(KD):
                            mm = pe.matmul(dst[:, WV * i:WV * i + WV],
                                           ht[:, b % 2 if tok else 0, k, P * t:P * t + P],
                                           w_in[:, k, 512:NW], start=(k == 0), stop=(k == KD - 1))
                    mm.then_inc(ring_filled, 1)

            def row_max(b, h):
                if h == 0:
                    pe.wait_ge(stacked[b % 2], 16 * 4 * (b // 2 + 1))
                for t in range(TT):
                    dst = use_ring(b, RU_PROJ + TT * h + t)
                    pe.matmul(dst, qs[0:SK, b % 2, h, P * t:P * t + P], ks[0:SK, b % 2, h, :],
                              start=True, stop=True).then_inc(ring_filled, 1)

            def turn_max(b):
                dst = use_ring(b, RU_PROJ + H * TT)
                pe.wait_ge(max_done, H * TT * (b + 1))
                pe.transpose(dst[0:H * TT, 0:P], rowmax[:, :], ident[:, :]).then_inc(ring_filled, 1)

            def scores(b, h):
                rows = SK + 3 if softmax else SK
                if h == 0:
                    pe.wait_ge(stacked[b % 2], 16 * 4 * (b // 2 + 1))
                    if softmax:
                        pe.wait_ge(key_ones, 1)
                        pe.wait_ge(maxrows_in[b % 2], 48 * (b // 2 + 1))
                for p in range(2):
                    n = 2 * (H * b + h) + p
                    if n >= 2:
                        pe.wait_ge(prob_ready, n - 1)
                    for i in range(2):
                        kt = 2 * p + i
                        q0, _ = kt_cols(kt)
                        mm = pe.matmul(score[:, n % 2, i, q0:S], ks[0:rows, b % 2, h, P * kt:P * kt + P],
                                       qs[0:rows, b % 2, h, q0:S], start=True, stop=True)
                    mm.then_inc(score_filled, 1)

            def values(b, g):
                dst = use_out(b, g)
                pe.wait_ge(prob_ready, 2 * (H * b + 4 * g + 4))
                if g == 0:
                    pe.wait_ge(v_ready, RU_V * (b + 1))
                    pe.wait_ge(consts_set, 1)
                for kt in range(TT):
                    q0, at = kt_cols(kt)
                    for j in range(4):
                        h = 4 * g + j
                        mm = pe.matmul(dst[32 * j:32 * j + 32, q0:S], v[:, kt, h, :],
                                       prob[:, (H * b + h) % P_SLOTS, at:at + S - q0],
                                       start=(kt == 0), stop=(kt == TT - 1), tile_position=(0, 32 * j))
                mm.then_inc(out_filled, 1)

            def output(b):
                pe.wait_ge(ot_ready, HG * (b + 1))
                for t in range(TT):
                    dst = use_out(b, HG + t)
                    for g in range(HG):
                        mm = pe.transpose(dst[:, P * g:P * g + P], ot[:, g, P * t:P * t + P], ident[:, :])
                    mm.then_inc(out_filled, 1)
                pe.wait_ge(otok_ready, TT * (b + 1))
                for k in range(KD):
                    dst = use_out(b, HG + TT + k)
                    for t in range(TT):
                        mm = pe.transpose(dst[:, P * t:P * t + P], otok[:, t, P * k:P * k + P], ident[:, :])
                    mm.then_inc(out_filled, 1)
                pe.wait_ge(ot2_ready, KD * (b + 1))
                for u in range(2):
                    dst = use_out(b, HG + TT + KD + u)
                    for i in range(2):
                        t = 2 * u + i
                        for k in range(KD):
                            mm = pe.matmul(dst[:, D * i:D * i + D], ot2[:, k, P * t:P * t + P], w_o[:, k, :],
                                           start=(k == 0), stop=(k == KD - 1))
                    mm.then_inc(out_filled, 1)

            project(0)
            if not tok:
                turn_qk(0)
            if softmax:
                for h in range(H):
                    row_max(0, h)
                turn_max(0)
            project_v(0)
            for b in range(B):
                more = b + 1 < B
                if more:
                    project(b + 1)
                for h in range(H):
                    scores(b, h)
                    if more and not tok and h == TURN_AT:
                        turn_qk(b + 1)
                    if softmax and more:
                        for hh in max_heads(h):
                            row_max(b + 1, hh)
                    if h % 4 == 1 and h > 4:
                        values(b, h // 4 - 1)
                values(b, HG - 1)
                if softmax and more:
                    turn_max(b + 1)
                output(b)
                if more:
                    project_v(b + 1)

        @block.scalar
        def _(act):
            act.wait_ge(weights_in, 16 * len(loads))

            def take_ht(b):
                for k in range(KD):
                    bank, filled = ring_use(b, k)
                    act.wait_ge(ring_filled, filled)
                    act.activation(ht[:, 0, k, :], ring[:, bank, :], ACT.Copy).then_inc(ht_ready, 1)

            def take_qk(b):
                for t in range(TT):
                    bank, filled = ring_use(b, KD + t)
                    act.wait_ge(ring_filled, filled)
                    n = TT * b + t
                    if n:
                        act.wait_ge(qk_used, n)
                    act.activation(qk[:, :], ring[:, bank, :], ACT.Copy).then_inc(qk_ready, 1)

            def take_qf(b):
                for f in range(4):
                    bank, filled = ring_use(b, f if tok else KD + TT + f)
                    n = 4 * b + f
                    act.wait_ge(ring_filled, filled)
                    if n >= 2:
                        act.wait_ge(qf_used, n - 1)
                    if tok:
                        act.activation(qf[:, f % 2, :], ring[:, bank, :], ACT.Identity,
                                       bias=bias_qk[:, f:f + 1]).then_inc(qf_ready, 1)
                    else:
                        act.activation(qf[:, f % 2, :], ring[:, bank, :], ACT.Copy).then_inc(qf_ready, 1)

            def probs(b, h):
                for p in range(2):
                    n = 2 * (H * b + h) + p
                    act.wait_ge(score_filled, n + 1)
                    if p == 0:
                        slot_free(act, b, h)
                    act.activation(prob[:, (H * b + h) % P_SLOTS, 2 * p * S:2 * (p + 1) * S],
                                   score[:, n % 2, :, :].rearrange("p i n -> p (i n)"), ACT.Exp,
                                   scale=HD ** -0.5).then_inc(prob_ready, 1)

            def take_values(b, g):
                bank, filled = out_use(b, g)
                act.wait_ge(out_filled, filled)
                if g == 0 and not tok and b + 1 < B:
                    act.wait_ge(ring_filled, ring_use(b + 1, RU_PROJ - 1)[1])
                act.activation(ot[:, g, :], outps[:, bank, :], ACT.Copy).then_inc(ot_ready, 1)

            def take_ot2(b):
                for k in range(KD):
                    bank, filled = out_use(b, HG + TT + k)
                    act.wait_ge(out_filled, filled)
                    act.activation(ot2[:, k, :], outps[:, bank, :], ACT.Copy).then_inc(ot2_ready, 1)

            def take_gate(b):
                for t in range(TT):
                    n = TT * b + t
                    if ret:
                        bank, filled = ring_use(b, RU_PROJ + RU_MAX + t)
                        act.wait_ge(ring_filled, filled)
                        if b and t == 0:
                            act.wait_ge(out_filled, OU * (b - 1) + HG)
                        act.activation(v[:, t, :, 0:HD],
                                       ring[:, bank, 0:D].rearrange("p (h d) -> p h d", d=HD),
                                       ACT.Copy).then_inc(v_ready, 1)
                        if b >= 2:
                            act.wait_ge(otok_ready, TT * (b - 1))
                        act.activation(gate[:, b % 2, t, :], ring[:, bank, D:2 * D], ACT.Silu).then_inc(gate_ready, 1)
                    else:
                        act.wait_ge(graw_ready, n + 1)
                        if b >= 2:
                            act.wait_ge(otok_ready, TT * (b - 1))
                        act.activation(gate[:, b % 2, t, :], graw[:, :], ACT.Exp, scale=-1.0).then_inc(gexp_ready, 1)

            def project_in(b):
                if not tok:
                    take_ht(b)
                if ret:
                    take_qk(b)
                if tok:
                    take_qf(b)

            project_in(0)
            if not tok:
                take_qf(0)
            if not tok:
                take_gate(0)
            for b in range(B):
                more = b + 1 < B
                if more:
                    project_in(b + 1)
                for h in range(H):
                    if softmax:
                        probs(b, h)
                    if more and not tok and h == TURN_AT:
                        take_qf(b + 1)
                    if h % 4 == 1 and h > 4:
                        take_values(b, h // 4 - 1)
                take_values(b, HG - 1)
                take_ot2(b)
                if more and not tok:
                    take_gate(b + 1)

        @block.vector
        def _(dve):
            chain = Chain(dve, dve_step)
            if softmax:
                dve.memset(ks[SK:SK + 3, :, :, :].rearrange("p b h n -> p (b h n)").bitcast(I32),
                           0x3F803F80).then_inc(key_ones, 1)
            dve.wait_ge(weights_in, 16 * len(loads))

            def take_qk(b):
                for t in range(TT):
                    n = TT * b + t
                    bank, filled = ring_use(b, KD + t)
                    dve.wait_ge(ring_filled, filled)
                    if n:
                        dve.wait_ge(qk_used, n)
                    dve.tensor_tensor(qk[:, :], ring[:, bank, :], bias_in[:, 0:512], ALU.add).then_inc(qk_ready, 1)
                    dve.wait_ge(sq_ready, n + 1)
                    dve.tensor_reduce(ssq[:, :], tmp[:, :].rearrange("p (a d) -> p a d", d=HD), AX_X,
                                      ALU.add).then_inc(ssq_ready, 1)

            def row_max(b, h):
                for t in range(TT):
                    bank, filled = ring_use(b, RU_PROJ + TT * h + t)
                    dve.wait_ge(ring_filled, filled)
                    dve.reduce_max(rowmax[:, TT * h + t:TT * h + t + 1], ring[:, bank, :], AX_X).then_inc(max_done, 1)

            def take_max(b):
                bank, filled = ring_use(b, RU_PROJ + H * TT)
                dve.wait_ge(ring_filled, filled)
                if b:
                    dve.wait_ge(mparts_ready, b)
                dve.tensor_scalar(negm[:, 0, :], ring[0:H * TT, bank, 0:P], -1.0, None, ALU.mult).then_inc(negm_ready, 1)

            def take_v(b):
                for u in range(RU_V):
                    bank, filled = ring_use(b, RU_PROJ + RU_MAX + u)
                    dve.wait_ge(ring_filled, filled)
                    if b and u == 0:
                        dve.wait_ge(out_filled, OU * (b - 1) + HG)
                    if tok:
                        for i in range(2):
                            last = dve.tensor_tensor(
                                v[:, 2 * u + i, :, 0:HD],
                                ring[:, bank, D * i:D * i + D].rearrange("p (h d) -> p h d", d=HD),
                                bias_v[:, :].rearrange("p (h d) -> p h d", d=HD), ALU.add)
                        last.then_inc(v_ready, 1)
                    else:
                        dve.tensor_tensor(v[:, u, :, 0:HD],
                                          ring[:, bank, 0:D].rearrange("p (h d) -> p h d", d=HD),
                                          bias_in[:, 512:512 + D].rearrange("p (h d) -> p h d", d=HD),
                                          ALU.add).then_inc(v_ready, 1)
                        n = TT * b + u
                        if n:
                            dve.wait_ge(gexp_ready, n)
                        dve.tensor_tensor(graw[:, :], ring[:, bank, D:D + H], bias_in[:, 512 + D:NW],
                                          ALU.add).then_inc(graw_ready, 1)

            def decays(b, h):
                for p in range(2):
                    n = 2 * (H * b + h) + p
                    dve.wait_ge(score_filled, n + 1)
                    if p == 0:
                        slot_free(dve, b, h)
                    for i in range(2):
                        q0, at = kt_cols(2 * p + i)
                        last = dve.tensor_tensor(prob[:, (H * b + h) % P_SLOTS, at:at + S - q0],
                                                 score[:, n % 2, i, q0:S], decay[:, h, 0:S - q0], ALU.mult)
                    last.then_inc(prob_ready, 1)

            def take_out(b):
                for t in range(TT):
                    bank, filled = out_use(b, HG + t)
                    n = TT * b + t
                    dve.wait_ge(out_filled, filled)
                    o = outps[:, bank, :].rearrange("p (h e) -> p h e", e=32)
                    if ret:
                        dve.wait_ge(gate_ready, n + 1)
                        dve.tensor_tensor(otok[:, t, :].rearrange("p (h d) -> p h d", d=HD), o[:, :, 0:HD],
                                          gate[:, b % 2, t, :].rearrange("p (h d) -> p h d", d=HD),
                                          ALU.mult).then_inc(otok_ready, 1)
                        continue
                    r = rden[:, t, :]
                    if rmsn:
                        dve.wait_ge(gate_ready, n + 1)
                        chain.mark(dve.tensor_tensor(r, o[:, :, HD], gate[:, b % 2, t, :], ALU.mult))
                        chain.wait()
                        dve.reciprocal(r, r).then_inc(rden_ready, 1)
                    else:
                        dve.reciprocal(r, o[:, :, HD]).then_inc(rden_ready, 1)
                    dve.wait_ge(rden_ready, n + 1)
                    dve.tensor_tensor(otok[:, t, :].rearrange("p (h d) -> p h d", d=HD), o[:, :, 0:HD],
                                      spread(r.rearrange("p (h o) -> p h o", o=1), [P, H, HD]),
                                      ALU.mult).then_inc(otok_ready, 1)

            def take_y(b):
                for u in range(2):
                    bank, filled = out_use(b, HG + TT + KD + u)
                    dve.wait_ge(out_filled, filled)
                    n = TT * b + 2 * u
                    y = htok[:, n:n + 2, :]
                    o = outps[:, bank, :].rearrange("p (i d) -> p i d", d=D)
                    if tok:
                        dve.tensor_tensor(y, o, spread(bias_o[:, :].rearrange("p (i d) -> p i d", i=1), [P, 2, D]),
                                          ALU.add).then_inc(y_ready, 1)
                        continue
                    dve.tensor_tensor(y, y, o, ALU.add).then_inc(y_ready, 1)
                    dve.wait_ge(y_ready, 2 * b + u + 1)
                    if rmsn:
                        chain.mark(dve.tensor_tensor(
                            y, y, spread(bias_o[:, :].rearrange("p (i d) -> p i d", i=1), [P, 2, D]), ALU.add))
                        chain.wait()
                    for i in range(2):
                        chain.mark(dve.bn_stats(stats[:, :], htok[:, n + i, :]))
                        chain.wait()
                        dve.bn_aggr(mv[:, n + i, :], stats[:, :]).then_inc(stats_ready, 1)
                        dve.wait_ge(stats_ready, n + i + 1)

            if rmsn:
                take_qk(0)
            if softmax:
                for h in range(H):
                    row_max(0, h)
                take_max(0)
                take_v(0)
            for b in range(B):
                more = b + 1 < B
                if rmsn and more:
                    take_qk(b + 1)
                for h in range(H):
                    if ret:
                        decays(b, h)
                    if softmax and more:
                        for hh in max_heads(h):
                            row_max(b + 1, hh)
                if softmax and more:
                    take_max(b + 1)
                take_out(b)
                take_y(b)
                if softmax and more:
                    take_v(b + 1)
            if not tok:
                dve.wait_ge(rstd_ready, 1)
                for n in range(0, NT, 2):
                    dve.tensor_scalar(htok[:, n, :], htok[:, n, :], mv[:, n, 0:1], rstd[:, n:n + 1],
                                      ALU.subtract, ALU.mult)


def layernorm_rows(pool, chain, mv, veps, rstd, half, rstd_ready):
    chain.mark(pool.tensor_scalar(veps[:, :], mv[:, :, 1], 1.0, LN_EPS, ALU.mult, ALU.add))
    chain.wait()
    pool.tensor_tensor(rstd[:, :], veps[:, :], half[:, 0:NT], ALU.pow).then_inc(rstd_ready, 1)


def moe(nc, layer, env, dram):
    first = layer == 0
    htok, ident = env["htok"], env["ident"]
    rows_in, rows_out = dram[f"slots{layer}"], dram[f"results{layer}"]
    XT = F32 if first else BF16

    with ExitStack() as outer:
        def sbo(name, shape, dt=F32):
            return outer.enter_context(nc.sbuf_tensor(f"m{layer}_{name}", shape, dt))

        slot = sbo("slot", [P, NT, 2], I32)
        weight = sbo("weight", [P, NT, 2])
        expert = sbo("expert", [P, NS], I32)
        if first:
            w_gu = sbo("w_gu", [P, KD, E, 2 * FI])
            w_dn = sbo("w_dn", [P, FI // P, E, D])
            b_gu = sbo("b_gu", [P, E, 2 * FI])
            b_dn = sbo("b_dn", [P, E, D])
        else:
            w_up = sbo("w_up", [P, E, KD, HIDP], BF16)
            w_dn = sbo("w_dn", [P, E, HIDP // P, D], BF16)

        with ExitStack() as ctx:
            def sb(name, shape, dt=F32):
                return ctx.enter_context(nc.sbuf_tensor(f"r{layer}_{name}", shape, dt))

            def ps(name, shape, dt=F32):
                return ctx.enter_context(nc.psum_tensor(f"r{layer}_{name}", shape, dt))

            sem = semaphores(nc, ctx, f"r{layer}_")

            hT = sb("hT", [P, KD, NT * P])
            rw = sb("rw", [P, KD, E])
            rb = sb("rb", [P, E])
            iota = sb("iota", [P, NS])
            before = sb("before", [P, P])
            ones = sb("ones", [P, P])
            upto = sb("upto", [P, E, E])
            logit = sb("logit", [P, NT, E])
            score = sb("score", [P, NT, E])
            choice = sb("choice", [P, NT, E]) if not first else score
            top = sb("top", [P, NT])
            total = sb("total", [P, NT])
            max8 = sb("max8", [P, NT, 8])
            idx8 = sb("idx8", [P, NT, 8], U32)
            idxf = sb("idxf", [P, 2, NT])
            pick = sb("pick", [P, 2, NT, E])
            both = sb("both", [P, NT, E])
            prod = sb("prod", [P, 2, NT, E])
            count = sb("count", [P, E])
            count_i = sb("count_i", [P, E], I32)
            tiles_i = sb("tiles_i", [P, E], I32)
            tiles = sb("tiles", [P, E])
            tri = sb("tri", [P, E, E])
            upto_e = sb("upto_e", [P, E])
            base = sb("base", [P, E])
            place = sb("place", [P, NT, E])
            slotf = sb("slotf", [P, 2, NT])
            cmp = sb("cmp", [P, NS, E])
            expf = sb("expf", [P, NS])
            turned = ps("turned", [P, 2, S])
            small = ps("small", [P, S])
            places = ps("places", [P, S])
            counts = small[:, 2 * NT * E:2 * NT * E + E]
            loads = [(rw[:, :, :], dram[f"r{layer}_w"].rearrange("(k p) e -> p k e", p=P)),
                     (rb[:, :], dram[f"r{layer}_b"].partition_broadcast(P)),
                     (iota[:, :], dram["iota"].partition_broadcast(P)),
                     (before[:, :], dram["before"]),
                     (upto[:, :, :].rearrange("p a b -> p (a b)"), dram["upto"].partition_broadcast(P))]
            if first:
                late = [(w_gu[:, :, e, :], dram["m0_w_gu"][e].rearrange("(k p) n -> p k n", p=P)) for e in range(E)]
                late += [(w_dn[:, :, e, :], dram["m0_w_dn"][e].rearrange("(k p) n -> p k n", p=P)) for e in range(E)]
                late += [(b_gu[:, e, :], dram["m0_b_gu"][e].partition_broadcast(P)) for e in range(E)]
                late += [(b_dn[:, e, :], dram["m0_b_dn"][e].partition_broadcast(P)) for e in range(E)]
            else:
                s_up = sb("s_up", [P, KD, HIDP])
                s_dn = sb("s_dn", [P, HIDP // P, D])
                raw = sb("raw", [P, 2, KD * HIDP])
                hid = sb("hid", [P, 2, HIDP // P, S])
                scaled = sb("scaled", [P, NT, 2, D], BF16)
                shup = ps("shup", [P, 2, S])
                shdn = ps("shdn", [P, 2, S])
                loads += [(s_up[:, :, :], dram["s_up"].rearrange("(k p) n -> p k n", p=P)),
                          (s_dn[:, :, :], dram["s_dn"].rearrange("(k p) n -> p k n", p=P))]
                late = []

            loaded = sem("loaded")
            weights_in = sem("weights_in")
            ones_set = sem("ones_set")
            turned_filled = sem("turned_filled")
            ht_ready = sem("ht_ready")
            logits_filled = sem("logits_filled")
            logits_ready = sem("logits_ready")
            exp_ready = sem("exp_ready")
            both_ready = sem("both_ready")
            places_filled = sem("places_filled")
            slots_ready = sem("slots_ready")
            sent = sem("sent")
            dve_step = sem("dve_step")
            raw_in = [sem(f"raw_in{i}") for i in range(2)]
            cast_done = sem("cast_done")
            up_filled = sem("up_filled")
            relu_ready = sem("relu_ready")
            hid_ready = sem("hid_ready")
            dn_filled = sem("dn_filled")
            dn_read = sem("dn_read")
            scaled_ready = sem("scaled_ready")
            HC = HIDP // P

            block = ctx.enter_context(nc.Block())

            @block.sync
            def _(sp):
                for dst, src in loads:
                    sp.dma_start(dst, src).then_inc(loaded, 16)
                for dst, src in late:
                    sp.dma_start(dst, src).then_inc(weights_in, 16)
                if not first:
                    for i in range(2 * E):
                        e, up = i // 2, i % 2 == 0
                        if i >= 2:
                            sp.wait_ge(cast_done, i - 1)
                        n = KD * HIDP if up else HC * D
                        src = dram["m1_w_up" if up else "m1_w_dn"][e].rearrange("(k p) n -> p k n", p=P)
                        sp.dma_start(raw[:, i % 2, 0:n].rearrange("p (k n) -> p k n", k=KD if up else HC),
                                     src).then_inc(raw_in[i % 2], 16)
                else:
                    sp.wait_ge(weights_in, 16 * len(late))

            @block.tensor
            def _(pe):
                pe.wait_ge(loaded, 16 * len(loads))
                for b in range(B):
                    for k in range(KD):
                        u = KD * b + k
                        if u >= 2:
                            pe.wait_ge(ht_ready, u - 1)
                        for t in range(TT):
                            mm = pe.transpose(turned[:, u % 2, P * t:P * t + P], htok[:, TT * b + t, P * k:P * k + P],
                                              ident[:, :])
                        mm.then_inc(turned_filled, 1)
                    if b:
                        logits(pe, b - 1) if False else None
                pe.wait_ge(ht_ready, KD * B)
                for n in range(NT):
                    for k in range(KD):
                        mm = pe.matmul(small[:, E * n:E * n + E], hT[:, k, P * n:P * n + P], rw[:, k, :],
                                       start=(k == 0), stop=(k == KD - 1))
                mm.then_inc(logits_filled, 1)

                def shared_up(b):
                    for c in range(HC):
                        u = HC * b + c
                        if u >= 2:
                            pe.wait_ge(relu_ready, u - 1)
                        for k in range(KD):
                            mm = pe.matmul(shup[:, u % 2, :], s_up[:, k, P * c:P * c + P],
                                           hT[:, k, S * b:S * b + S], start=(k == 0), stop=(k == KD - 1))
                        mm.then_inc(up_filled, 1)

                def shared_down(b):
                    pe.wait_ge(hid_ready, HC * (b + 1))
                    for i in range(2):
                        u = 2 * b + i
                        if u >= 2:
                            pe.wait_ge(dn_read, u - 1)
                        for t in range(2):
                            for c in range(HC):
                                mm = pe.matmul(shdn[:, u % 2, D * t:D * t + D],
                                               hid[:, b % 2, c, P * (2 * i + t):P * (2 * i + t) + P],
                                               s_dn[:, c, :], start=(c == 0), stop=(c == HC - 1))
                        mm.then_inc(dn_filled, 1)

                if not first:
                    shared_up(0)
                pe.wait_ge(both_ready, 1)
                pe.wait_ge(ones_set, 1)
                flat = both[:, :, :].rearrange("p n e -> p (n e)")
                pe.matmul(places[:, 0:NT * E], before[:, :], flat, start=True, stop=False)
                for n in range(NT - 1):
                    rest = NT - 1 - n
                    pe.matmul(places[:, E * (n + 1):NT * E].rearrange("p (n e) -> p n e", e=E), ones[:, :],
                              spread(both[:, n:n + 1, :], [P, rest, E]), start=False, stop=(n == NT - 2))
                for n in range(NT):
                    mm = pe.matmul(counts, ones[:, :], both[:, n, :], start=(n == 0), stop=(n == NT - 1))
                mm.then_inc(places_filled, 1)
                if not first:
                    for b in range(B):
                        if b + 1 < B:
                            shared_up(b + 1)
                        shared_down(b)

            @block.scalar
            def _(act):
                for u in range(KD * B):
                    act.wait_ge(turned_filled, u + 1)
                    b, k = u // KD, u % KD
                    act.activation(hT[:, k, S * b:S * b + S], turned[:, u % 2, :], ACT.Copy).then_inc(ht_ready, 1)
                act.wait_ge(logits_ready, 1)
                act.activation(score[:, :, :].rearrange("p n e -> p (n e)"),
                               logit[:, :, :].rearrange("p n e -> p (n e)"),
                               ACT.Exp if first else ACT.Sigmoid).then_inc(exp_ready, 1)
                if not first:
                    def cast(i):
                        e, up = i // 2, i % 2 == 0
                        n = KD * HIDP if up else HC * D
                        act.wait_ge(raw_in[i % 2], 16 * (i // 2 + 1))
                        dst = (w_up if up else w_dn)[:, e, :, :].rearrange("p k n -> p (k n)")
                        act.activation(dst, raw[:, i % 2, 0:n], ACT.Copy).then_inc(cast_done, 1)

                    for u in range(HC * B):
                        b, c = u // HC, u % HC
                        act.wait_ge(up_filled, u + 1)
                        if b >= 2 and c == 0:
                            act.wait_ge(dn_filled, 2 * (b - 1))
                        act.activation(hid[:, b % 2, c, :], shup[:, u % 2, :], ACT.Relu).then_inc(relu_ready, 1)
                        cast(u)
                    for i in range(HC * B, 2 * E):
                        cast(i)

            @block.gpsimd
            def _(pool):
                pool.memset(ones[:, :], 1.0).then_inc(ones_set, 1)
                if not first:
                    for u in range(HC * B):
                        b, c = u // HC, u % HC
                        pool.wait_ge(relu_ready, u + 1)
                        pool.tensor_tensor(hid[:, b % 2, c, :], hid[:, b % 2, c, :], hid[:, b % 2, c, :],
                                           ALU.mult).then_inc(hid_ready, 1)
                pool.wait_ge(slots_ready, 1)
                pool.wait_ge(*env["slots_cleared"][layer])
                if not first:
                    pool.wait_ge(scaled_ready, 1)
                for n in range(NT):
                    for k in range(2):
                        src = htok[:, n, :] if first else scaled[:, n, k, :]
                        pool.indirect_dma_start(rows_in, bass.IndirectOffsetOnAxis(ap=slot[:, n, k:k + 1], axis=0),
                                                src, None).then_inc(sent, 16)
                pool.wait_ge(sent, 16 * 2 * NT)

            @block.vector
            def _(dve):
                chain = Chain(dve, dve_step)

                def then(ins):
                    chain.mark(ins)
                    chain.wait()

                def over_tiles(ap):
                    return spread(ap.rearrange("p (n e) -> p n e", n=1), [P, NT, E])

                def over_experts(ap, n=NT):
                    return spread(ap.rearrange("p (n e) -> p n e", e=1), [P, n, E])

                dve.wait_ge(loaded, 16 * len(loads))
                dve.wait_ge(logits_filled, 1)
                lg = small[:, 0:NT * E].rearrange("p (n e) -> p n e", e=E)
                if first:
                    then(dve.tensor_tensor(logit[:, :, :], lg, over_tiles(rb[:, :]), ALU.add))
                    then(dve.tensor_reduce(top[:, :], logit[:, :, :], AX_X, ALU.max))
                    dve.tensor_tensor(logit[:, :, :], logit[:, :, :], over_experts(top[:, :]),
                                      ALU.subtract).then_inc(logits_ready, 1)
                    dve.wait_ge(exp_ready, 1)
                    then(dve.tensor_reduce(total[:, :], score[:, :, :], AX_X, ALU.add))
                    then(dve.reciprocal(total[:, :], total[:, :]))
                    then(dve.tensor_tensor(score[:, :, :], score[:, :, :], over_experts(total[:, :]), ALU.mult))
                else:
                    dve.tensor_copy(logit[:, :, :], lg).then_inc(logits_ready, 1)
                    dve.wait_ge(exp_ready, 1)
                    then(dve.tensor_tensor(choice[:, :, :], score[:, :, :], over_tiles(rb[:, :]), ALU.add))
                for n in range(NT):
                    chain.mark(dve.max(max8[:, n, :], choice[:, n, :]))
                chain.wait()
                for n in range(NT):
                    chain.mark(dve.max_index(idx8[:, n, :], max8[:, n, :], choice[:, n, :]))
                chain.wait()
                for k in range(2):
                    chain.mark(dve.tensor_copy(idxf[:, k, :], idx8[:, :, k]))
                chain.wait()
                for k in range(2):
                    chain.mark(dve.tensor_tensor(pick[:, k, :, :], over_tiles(iota[:, 0:E]),
                                                 over_experts(idxf[:, k, :]), ALU.is_equal))
                chain.wait()
                dve.tensor_tensor(both[:, :, :], pick[:, 0, :, :], pick[:, 1, :, :], ALU.add).then_inc(both_ready, 1)
                for k in range(2):
                    chain.mark(dve.tensor_tensor(prod[:, k, :, :], pick[:, k, :, :], score[:, :, :], ALU.mult))
                chain.wait()
                for k in range(2):
                    chain.mark(dve.tensor_reduce(weight[:, :, k], prod[:, k, :, :], AX_X, ALU.add))
                chain.wait()
                dve.wait_ge(places_filled, 1)
                then(dve.tensor_scalar(count_i[:, :], counts, float(P - 1), None, ALU.add))
                then(dve.tensor_scalar(tiles_i[:, :], count_i[:, :], 7, None, ALU.logical_shift_right))
                then(dve.tensor_copy(tiles[:, :], tiles_i[:, :]))
                then(dve.tensor_tensor(tri[:, :, :], upto[:, :, :],
                                       spread(tiles[:, :].rearrange("p (a b) -> p a b", a=1), [P, E, E]), ALU.mult))
                then(dve.tensor_reduce(upto_e[:, :], tri[:, :, :], AX_X, ALU.add))
                then(dve.tensor_tensor(base[:, :], upto_e[:, :], tiles[:, :], ALU.subtract))
                then(dve.tensor_scalar(base[:, :], base[:, :], float(P), None, ALU.mult))
                then(dve.tensor_tensor(place[:, :, :], places[:, 0:NT * E].rearrange("p (n e) -> p n e", e=E),
                                       over_tiles(base[:, :]), ALU.add))
                for k in range(2):
                    chain.mark(dve.tensor_tensor(prod[:, k, :, :], pick[:, k, :, :], place[:, :, :], ALU.mult))
                chain.wait()
                for k in range(2):
                    chain.mark(dve.tensor_reduce(slotf[:, k, :], prod[:, k, :, :], AX_X, ALU.add))
                chain.wait()
                dve.tensor_copy(slot[:, :, :].rearrange("p n k -> p k n"), slotf[:, :, :]).then_inc(slots_ready, 1)
                if not first:
                    for n in range(NT):
                        for k in range(2):
                            last = dve.tensor_scalar(scaled[:, n, k, :], htok[:, n, :], weight[:, n, k:k + 1], None,
                                                     ALU.mult)
                    last.then_inc(scaled_ready, 1)
                then(dve.tensor_tensor(cmp[:, :, :],
                                       spread(upto_e[:, :].rearrange("p (n e) -> p n e", n=1), [P, NS, E]),
                                       over_experts(iota[:, :], NS), ALU.is_le))
                then(dve.tensor_reduce(expf[:, :], cmp[:, :, :], AX_X, ALU.add))
                then(dve.tensor_scalar(expert[:, :], expf[:, :], float(E - 1), None, ALU.min))
                if not first:
                    dve.wait_ge(scaled_ready, 1)
                    for u in range(2 * B):
                        dve.wait_ge(dn_filled, u + 1)
                        y = htok[:, 2 * u:2 * u + 2, :]
                        dve.tensor_tensor(y, y, shdn[:, u % 2, :].rearrange("p (i d) -> p i d", d=D),
                                          ALU.add).then_inc(dn_read, 1)

        with ExitStack() as ctx:
            def sb(name, shape, dt=F32):
                return ctx.enter_context(nc.sbuf_tensor(f"t{layer}_{name}", shape, dt))

            def ps(name, shape, dt=F32):
                return ctx.enter_context(nc.psum_tensor(f"t{layer}_{name}", shape, dt))

            sem = semaphores(nc, ctx, f"t{layer}_")

            (tiles_first if first else tiles_second)(nc, env, sb, ps, sem, ctx, dict(
                rows_in=rows_in, rows_out=rows_out, expert=expert, w_dn=w_dn,
                **(dict(w_gu=w_gu, b_gu=b_gu, b_dn=b_dn) if first else dict(w_up=w_up))))

        with ExitStack() as ctx:
            def sb(name, shape, dt=F32):
                return ctx.enter_context(nc.sbuf_tensor(f"c{layer}_{name}", shape, dt))

            sem = semaphores(nc, ctx, f"c{layer}_")

            got = sb("got", [P, NT, 2, D], XT)
            stats = sb("stats", [P, 6])
            mv = sb("mv", [P, NT, 2])
            veps = sb("veps", [P, NT])
            rstd = sb("rstd", [P, NT])
            half = sb("half", [P, NT])
            GRP = 4
            fetched = [sem(f"fetched{i}") for i in range(NT // GRP)]
            half_set = sem("half_set")
            pool_step = sem("pool_step")
            dve_step = sem("dve_step")
            stats_ready = sem("stats_ready")
            rstd_ready = sem("rstd_ready")
            normed = [sem(f"normed{i}") for i in range(2)]
            stored = sem("stored")
            block = ctx.enter_context(nc.Block())

            @block.gpsimd
            def _(pool):
                chain = Chain(pool, pool_step)
                pool.memset(half[:, :], -0.5).then_inc(half_set, 1)
                for n in range(NT):
                    for k in range(2):
                        pool.indirect_dma_start(got[:, n, k, :], None, rows_out,
                                                bass.IndirectOffsetOnAxis(ap=slot[:, n, k:k + 1], axis=0)
                                                ).then_inc(fetched[n // GRP], 16)
                pool.wait_ge(half_set, 1)
                pool.wait_ge(stats_ready, NT)
                layernorm_rows(pool, chain, mv, veps, rstd, half, rstd_ready)
                pool.wait_ge(rstd_ready, 1)
                for n in range(1, NT, 2):
                    pool.tensor_scalar(htok[:, n, :], htok[:, n, :], mv[:, n, 0:1], rstd[:, n:n + 1],
                                       ALU.subtract, ALU.mult).then_inc(normed[1], 1)

            @block.vector
            def _(dve):
                chain = Chain(dve, dve_step)
                for n in range(NT):
                    if n % GRP == 0:
                        dve.wait_ge(fetched[n // GRP], 16 * 2 * GRP)
                    y = htok[:, n, :]
                    for k in range(2):
                        if first:
                            chain.mark(dve.scalar_tensor_tensor(out=y, in0=got[:, n, k, :],
                                                                scalar=weight[:, n, k:k + 1], in1=y,
                                                                op0=ALU.mult, op1=ALU.add))
                        else:
                            chain.mark(dve.tensor_tensor(y, y, got[:, n, k, :], ALU.add))
                        chain.wait()
                    chain.mark(dve.bn_stats(stats[:, :], y))
                    chain.wait()
                    dve.bn_aggr(mv[:, n, :], stats[:, :]).then_inc(stats_ready, 1)
                    dve.wait_ge(stats_ready, n + 1)
                dve.wait_ge(rstd_ready, 1)
                for n in range(0, NT, 2):
                    dve.tensor_scalar(htok[:, n, :], htok[:, n, :], mv[:, n, 0:1], rstd[:, n:n + 1],
                                      ALU.subtract, ALU.mult).then_inc(normed[0], 1)

            if not first:
                @block.sync
                def _(sp):
                    out = dram["out"].rearrange("(t p) d -> p t d", p=P)
                    for n in range(0, NT, 4):
                        for s in normed:
                            sp.wait_ge(s, n // 2 + 2)
                        sp.dma_start(out[:, n:n + 4, :], htok[:, n:n + 4, :]).then_inc(stored, 16)
                    sp.wait_ge(stored, 16 * (NT // 4))


def in_steps(eng, first, last, step, unroll=2):
    turns = (last - first) // unroll
    if turns > 1:
        with eng.Fori(0, turns) as i:
            for d in range(unroll):
                step(i * unroll + (first + d), (first + d) % unroll)
    else:
        turns = 0
    for j in range(first + unroll * turns, last):
        step(j, j % unroll)


def tiles_first(nc, env, sb, ps, sem, ctx, t):
    ident, expert = env["ident"], t["expert"]
    KF = FI // P
    xin = sb("xin", [P, 2, D])
    xT = sb("xT", [P, 2, KD, P])
    g = sb("g", [P, 2, FI])
    u = sb("u", [P, 2, FI])
    sig = sb("sig", [P, 2, FI])
    act_t = sb("act", [P, 2, FI])
    aT = sb("aT", [P, 2, KF, P])
    y = sb("y", [P, 2, D])
    x_ps = ps("x_ps", [P, 2 * KD, P])
    g_ps = ps("g_ps", [P, 2, FI])
    u_ps = ps("u_ps", [P, 2, FI])
    a_ps = ps("a_ps", [P, KF, P])
    y_ps = ps("y_ps", [P, 2 * D])

    x_in = [sem(f"x_in{i}") for i in range(2)]
    x_turned = sem("x_turned")
    xT_ready = sem("xT_ready")
    g_filled = sem("g_filled")
    u_filled = sem("u_filled")
    g_ready = sem("g_ready")
    u_ready = sem("u_ready")
    g_min = sem("g_min")
    u_clip = sem("u_clip")
    sig_ready = sem("sig_ready")
    glu_ready = sem("glu_ready")
    a_ready = sem("a_ready")
    a_turned = sem("a_turned")
    aT_ready = sem("aT_ready")
    y_filled = sem("y_filled")
    y_ready = sem("y_ready")
    y_saved = [sem(f"y_saved{i}") for i in range(2)]
    block = ctx.enter_context(nc.Block())

    def of_expert(eng, j):
        return eng.value_load(expert[0:1, bass.ds(j, 1)], min_val=0, max_val=E - 1)

    @block.sync
    def _(sp):
        def rows(ap, j):
            return ap[bass.ds(j * P, P), :]

        def load(j, q):
            sp.dma_start(xin[:, q, :], rows(t["rows_in"], j)).then_inc(x_in[q], 16)

        def step(j, q):
            sp.wait_ge(x_turned, j - 1)
            load(j, q)

        load(0, 0)
        load(1, 1)
        in_steps(sp, 2, NS, step)
        for s in y_saved:
            sp.wait_ge(s, 16 * (NS // 2))

    @block.tensor
    def _(pe):
        def turn_x(j, q, early=False):
            pe.wait_ge(x_in[q], 8 * (j - q) + 16)
            if not early:
                pe.wait_ge(xT_ready, j)
            for k in range(KD):
                mm = pe.transpose(x_ps[:, k, :], xin[:, q, P * k:P * k + P], ident[:, :])
            mm.then_inc(x_turned, 1)

        def gate(j, q, early=False):
            e = of_expert(pe, j)
            pe.wait_ge(xT_ready, j + 1)
            if not early:
                pe.wait_ge(g_ready, j - 1)
            for k in range(KD):
                mm = pe.matmul(g_ps[:, q, :], xT[:, q, k, :],
                               t["w_gu"][:, k, bass.ds(e, 1), 0:FI].rearrange("p o n -> p (o n)"),
                               start=(k == 0), stop=(k == KD - 1))
            mm.then_inc(g_filled, 1)
            return e

        def up(j, q, e, early=False):
            if not early:
                pe.wait_ge(u_ready, j - 1)
            for k in range(KD):
                mm = pe.matmul(u_ps[:, q, :], xT[:, q, k, :],
                               t["w_gu"][:, k, bass.ds(e, 1), FI:2 * FI].rearrange("p o n -> p (o n)"),
                               start=(k == 0), stop=(k == KD - 1))
            mm.then_inc(u_filled, 1)

        def turn_a(j, q, early=False):
            pe.wait_ge(a_ready, j + 1)
            if not early:
                pe.wait_ge(aT_ready, j)
            for k in range(KF):
                mm = pe.transpose(a_ps[:, k, :], act_t[:, q, P * k:P * k + P], ident[:, :])
            mm.then_inc(a_turned, 1)

        def down(j, q, early=False):
            e = of_expert(pe, j)
            pe.wait_ge(aT_ready, j + 1)
            if not early:
                pe.wait_ge(y_ready, j)
            for k in range(KF):
                mm = pe.matmul(y_ps[:, 0:D], aT[:, q, k, :],
                               t["w_dn"][:, k, bass.ds(e, 1), :].rearrange("p o n -> p (o n)"),
                               start=(k == 0), stop=(k == KF - 1))
            mm.then_inc(y_filled, 1)

        def step(j, q):
            e = gate(j + 1, 1 - q)
            down(j - 1, 1 - q)
            up(j + 1, 1 - q, e)
            turn_a(j, q)
            turn_x(j + 2, q)

        turn_x(0, 0, True)
        turn_x(1, 1)
        up(0, 0, gate(0, 0, True), True)
        e = gate(1, 1, True)
        up(1, 1, e, True)
        turn_a(0, 0, True)
        turn_x(2, 0)
        for j in (1, 2):
            e = gate(j + 1, 1 - j % 2)
            down(j - 1, 1 - j % 2, j == 1)
            up(j + 1, 1 - j % 2, e)
            turn_a(j, j % 2)
            turn_x(j + 2, j % 2)
        in_steps(pe, 3, NS - 2, step)
        e = gate(NS - 1, 1)
        down(NS - 3, 1)
        up(NS - 1, 1, e)
        turn_a(NS - 2, 0)
        down(NS - 2, 0)
        turn_a(NS - 1, 1)
        down(NS - 1, 1)

    @block.scalar
    def _(act):
        def take_x(j, q):
            act.wait_ge(x_turned, j + 1)
            act.activation(xT[:, q, :, :], x_ps[:, 0:KD, :], ACT.Copy).then_inc(xT_ready, 1)

        def sigmoid(j, q):
            act.wait_ge(g_min, j + 1)
            act.activation(sig[:, q, :], g[:, q, :], ACT.Sigmoid, scale=1.702).then_inc(sig_ready, 1)

        def take_a(j, q):
            act.wait_ge(a_turned, j + 1)
            act.activation(aT[:, q, :, :], a_ps[:, :, :], ACT.Copy).then_inc(aT_ready, 1)

        def save(j, q):
            act.wait_ge(y_ready, j + 1)
            act.dma_start(t["rows_out"][bass.ds(j * P, P), :], y[:, q, :]).then_inc(y_saved[q], 16)

        def step(j, q):
            sigmoid(j, q)
            take_a(j - 1, 1 - q)
            take_x(j + 1, 1 - q)
            save(j - 3, 1 - q)

        take_x(0, 0)
        take_x(1, 1)
        sigmoid(0, 0)
        sigmoid(1, 1)
        take_a(0, 0)
        take_x(2, 0)
        sigmoid(2, 0)
        take_a(1, 1)
        take_x(3, 1)
        in_steps(act, 3, NS - 1, step)
        sigmoid(NS - 1, 1)
        take_a(NS - 2, 0)
        take_a(NS - 1, 1)
        for j in range(NS - 4, NS):
            save(j, j % 2)

    @block.gpsimd
    def _(pool):
        def step(j, q):
            pool.wait_ge(sig_ready, j + 1)
            pool.tensor_tensor(sig[:, q, :], sig[:, q, :], g[:, q, :], ALU.mult).then_inc(glu_ready, 1)

        in_steps(pool, 0, NS, step)

    @block.vector
    def _(dve):
        def hidden(j, q, early=False):
            e = of_expert(dve, j)
            dve.wait_ge(g_filled, j + 1)
            dve.tensor_tensor(g[:, q, :], g_ps[:, q, :],
                              t["b_gu"][:, bass.ds(e, 1), 0:FI].rearrange("p o n -> p (o n)"),
                              ALU.add).then_inc(g_ready, 1)
            dve.wait_ge(g_ready, j + 1)
            dve.tensor_scalar(g[:, q, :], g[:, q, :], LIMIT, None, ALU.min).then_inc(g_min, 1)
            dve.wait_ge(u_filled, j + 1)
            dve.tensor_tensor(u[:, q, :], u_ps[:, q, :],
                              t["b_gu"][:, bass.ds(e, 1), FI:2 * FI].rearrange("p o n -> p (o n)"),
                              ALU.add).then_inc(u_ready, 1)
            dve.wait_ge(u_ready, j + 1)
            dve.tensor_scalar(u[:, q, :], u[:, q, :], LIMIT, -LIMIT, ALU.min, ALU.max).then_inc(u_clip, 1)
            dve.wait_ge(u_clip, j + 1)
            dve.wait_ge(glu_ready, j + 1)
            if not early:
                dve.wait_ge(a_turned, j - 1)
            dve.scalar_tensor_tensor(out=act_t[:, q, :], in0=u[:, q, :], scalar=1.0, in1=sig[:, q, :],
                                     op0=ALU.add, op1=ALU.mult).then_inc(a_ready, 1)

        def result(j, q, early=False):
            e = of_expert(dve, j)
            dve.wait_ge(y_filled, j + 1)
            if not early:
                dve.wait_ge(y_saved[q], 8 * (j - q))
            dve.tensor_tensor(y[:, q, :], y_ps[:, 0:D],
                              t["b_dn"][:, bass.ds(e, 1), :].rearrange("p o n -> p (o n)"),
                              ALU.add).then_inc(y_ready, 1)

        def step(j, q):
            hidden(j, q)
            result(j - 2, q)

        hidden(0, 0, True)
        hidden(1, 1, True)
        for j in (2, 3):
            hidden(j, j % 2)
            result(j - 2, j % 2, True)
        in_steps(dve, 4, NS, step)
        result(NS - 2, 0)
        result(NS - 1, 1)


def tiles_second(nc, env, sb, ps, sem, ctx, t):
    expert, ident = t["expert"], env["ident_bf"]
    HC = HIDP // P
    DEEP = 4
    xin = sb("xin", [P, DEEP, D], BF16)
    xT = sb("xT", [P, 2, KD, P], BF16)
    h = sb("h", [P, 2, HC, P], BF16)
    hsq = sb("hsq", [P, 2, HC, P], BF16)
    y = sb("y", [P, DEEP, D], BF16)
    x_ps = [ps(f"x_ps{i}", [P, 2 * S], BF16) for i in range(2)]
    h_ps = [ps(f"h_ps{i}", [P, 512]) for i in range(2)]
    y_ps = [ps(f"y_ps{i}", [P, 512]) for i in range(2)]
    x_in = [sem(f"x_in{i}") for i in range(DEEP)]
    x_turned = sem("x_turned")
    xT_ready = sem("xT_ready")
    h_filled = sem("h_filled")
    h_ready = sem("h_ready")
    hsq_ready = sem("hsq_ready")
    y_filled = sem("y_filled")
    y_ready = sem("y_ready")
    y_saved = [sem(f"y_saved{i}") for i in range(DEEP)]
    block = ctx.enter_context(nc.Block())

    @block.sync
    def _(sp):
        def rows(ap, j):
            return ap[bass.ds(j * P, P), :]

        def load(j, q):
            sp.dma_start(xin[:, q, :], rows(t["rows_in"], j)).then_inc(x_in[q], 16)

        def step(j, q):
            sp.wait_ge(x_turned, j - DEEP + 1)
            load(j, q)

        for j in range(DEEP):
            load(j, j)
        in_steps(sp, DEEP, NS, step, DEEP)
        for s in y_saved:
            sp.wait_ge(s, 16 * (NS // DEEP))

    @block.tensor
    def _(pe):
        def turn_x(j, q, early=False):
            pe.wait_ge(x_in[q], 16 // DEEP * (j - q) + 16)
            if not early:
                pe.wait_ge(xT_ready, j - 1)
            for k in range(KD):
                mm = pe.transpose(x_ps[q % 2][:, P * k:P * k + P], xin[:, q, P * k:P * k + P], ident[:, :])
            mm.then_inc(x_turned, 1)

        def up(j, q, early=False):
            e = pe.value_load(expert[0:1, bass.ds(j, 1)], min_val=0, max_val=E - 1)
            pe.wait_ge(xT_ready, j + 1)
            if not early:
                pe.wait_ge(h_ready, j - 1)
            for c in range(HC):
                for k in range(KD):
                    mm = pe.matmul(h_ps[q % 2][:, P * c:P * c + P],
                                   t["w_up"][:, bass.ds(e, 1), k, P * c:P * c + P].rearrange("p o n -> p (o n)"),
                                   xT[:, q % 2, k, :], start=(k == 0), stop=(k == KD - 1))
            mm.then_inc(h_filled, 1)
            return e

        def down(j, q, early=False):
            e = pe.value_load(expert[0:1, bass.ds(j, 1)], min_val=0, max_val=E - 1)
            pe.wait_ge(hsq_ready, j + 1)
            if not early:
                pe.wait_ge(y_ready, j - 1)
            for c in range(HC):
                mm = pe.matmul(y_ps[q % 2][:, 0:D], hsq[:, q % 2, c, :],
                               t["w_dn"][:, bass.ds(e, 1), c, :].rearrange("p o n -> p (o n)"),
                               start=(c == 0), stop=(c == HC - 1))
            mm.then_inc(y_filled, 1)

        def step(j, q):
            turn_x(j + 2, (q + 2) % DEEP)
            up(j + 1, (q + 1) % DEEP)
            down(j, q)

        turn_x(0, 0, True)
        turn_x(1, 1, True)
        up(0, 0, True)
        turn_x(2, 2)
        up(1, 1, True)
        down(0, 0, True)
        turn_x(3, 3)
        up(2, 2)
        down(1, 1, True)
        in_steps(pe, 2, NS - 2, step, DEEP)
        up(NS - 1, DEEP - 1)
        down(NS - 2, DEEP - 2)
        down(NS - 1, DEEP - 1)

    @block.scalar
    def _(act):
        def take_x(j, q):
            act.wait_ge(x_turned, j + 1)
            act.activation(xT[:, q % 2, :, :], x_ps[q % 2][:, 0:D].rearrange("p (k n) -> p k n", k=KD), ACT.Copy).then_inc(xT_ready, 1)

        def relu(j, q, early=False):
            act.wait_ge(h_filled, j + 1)
            if not early:
                act.wait_ge(hsq_ready, j - 1)
            act.activation(h[:, q % 2, :, :].rearrange("p c n -> p (c n)"), h_ps[q % 2][:, 0:HIDP],
                           ACT.Relu).then_inc(h_ready, 1)

        def save(j, q):
            act.wait_ge(y_ready, j + 1)
            act.dma_start(t["rows_out"][bass.ds(j * P, P), :], y[:, q, :]).then_inc(y_saved[q], 16)

        def step(j, q):
            take_x(j, q)
            relu(j - 1, (q - 1) % DEEP)
            save(j - 3, (q - 3) % DEEP)

        take_x(0, 0)
        take_x(1, 1)
        relu(0, 0, True)
        take_x(2, 2)
        relu(1, 1, True)
        in_steps(act, 3, NS, step, DEEP)
        relu(NS - 1, DEEP - 1)
        for j in range(NS - 3, NS):
            save(j, j % DEEP)

    @block.gpsimd
    def _(pool):
        def square(j, q, early=False):
            pool.wait_ge(h_ready, j + 1)
            if not early:
                pool.wait_ge(y_filled, j - 1)
            pool.tensor_tensor(hsq[:, q % 2, :, :], h[:, q % 2, :, :], h[:, q % 2, :, :], ALU.mult).then_inc(hsq_ready, 1)

        square(0, 0, True)
        square(1, 1, True)
        in_steps(pool, 2, NS, square, DEEP)

    @block.vector
    def _(dve):
        def result(j, q, early=False):
            dve.wait_ge(y_filled, j + 1)
            if not early:
                dve.wait_ge(y_saved[q], 16 // DEEP * (j - q))
            dve.tensor_copy(y[:, q, :], y_ps[q % 2][:, 0:D]).then_inc(y_ready, 1)

        for j in range(DEEP):
            result(j, j, True)
        in_steps(dve, DEEP, NS, result, DEEP)


def rope_tables():
    inv = (1.0 / np.float32(10000.0) ** (np.arange(0, HD, 2, dtype=np.float32) / np.float32(HD))).astype(np.float32)
    angle = np.arange(S, dtype=np.float32)[:, None] * inv[None, :]
    return np.cos(angle).astype(np.float32), np.sin(angle).astype(np.float32)


def decay_table():
    gamma = 1.0 - 2.0 ** (-5.0 - np.arange(H))
    dist = np.arange(S)[None, :] - np.arange(P)[:, None]
    table = np.where(dist[:, None, :] >= 0, gamma[None, :, None] ** np.maximum(dist, 0)[:, None, :], 0.0)
    return np.ascontiguousarray((table * HD ** -0.5).astype(np.float32).reshape(P, H * S))


def vit_tower(nc, dram):
    with ExitStack() as ctx:
        htok = ctx.enter_context(nc.sbuf_tensor("htok", [P, NT, D], F32))
        ident = ctx.enter_context(nc.sbuf_tensor("ident", [P, P], F32))
        ident_bf = ctx.enter_context(nc.sbuf_tensor("ident_bf", [P, P], BF16))
        zeros = ctx.enter_context(nc.sbuf_tensor("zeros", [P, ZCOLS], F32))
        tables_in = ctx.enter_context(nc.semaphore("tables_in"))
        tables_cast = ctx.enter_context(nc.semaphore("tables_cast"))
        cleared = [ctx.enter_context(nc.semaphore(f"cleared{i}")) for i in range(2)]

        def clear_slots(sp):
            for layer, dt in ((0, F32), (1, BF16)):
                per = ZCOLS * (1 if layer == 0 else 2)
                flat = dram[f"slots{layer}"].rearrange("(p r) d -> p (r d)", p=P)
                src = zeros[:, :] if layer == 0 else zeros[:, :].bitcast(BF16)
                for c in range(NS * D // per):
                    sp.dma_start(flat[:, c * per:(c + 1) * per], src).then_inc(cleared[layer], 16)

        env = dict(htok=htok, ident=ident, ident_bf=ident_bf, ret_dmas=(clear_slots,),
                   slots_cleared=[(cleared[0], 16 * (NS * D // ZCOLS)), (cleared[1], 16 * (NS * D // (2 * ZCOLS)))])
        with nc.Block() as block:
            @block.sync
            def _(sp):
                sp.dma_start(ident[:, :], dram["ident"]).then_inc(tables_in, 16)

            @block.vector
            def _(dve):
                dve.memset(zeros[:, :], 0.0).then_inc(tables_cast, 1)
                dve.wait_ge(tables_in, 16)
                dve.tensor_copy(ident_bf[:, :], ident[:, :]).then_inc(tables_cast, 1)

        attention(nc, "tok", env, dram)
        attention(nc, "ret", env, dram)
        moe(nc, 0, env, dram)
        attention(nc, "rms", env, dram)
        moe(nc, 1, env, dram)


def kernel(**inputs):
    import numpy as _np
    import concourse.bacc as _bacc
    from concourse import mybir as _mybir
    from concourse.bass_utils import run_bass_kernel_spmd as _run

    I = {k: _np.asarray(a) for k, a in inputs.items()}
    w_qkv = I["L0_tok_w_qkv"].reshape(H, 3, HD, D).transpose(1, 0, 2, 3).reshape(3 * D, D).T
    b_qkv = I["L0_tok_b_qkv"].reshape(H, 3, HD).transpose(1, 0, 2).reshape(3 * D)
    cos, sin = rope_tables()

    def wide(a, axis):
        pad = [(0, 0)] * a.ndim
        pad[axis] = (0, HIDP - HID)
        return _np.pad(a, pad)

    arrays = {
        "x": I["x"].reshape(B * S, D).T,
        "tok_w_in": w_qkv,
        "tok_b_qk": b_qkv[:2 * D].reshape(4, P).T,
        "tok_b_v": b_qkv[2 * D:],
        "tok_w_o": I["L0_tok_w_out"].T,
        "tok_b_o": I["L0_tok_b_out"],
        "ret_w_in": _np.concatenate([I["L0_attn_wq"].T, I["L0_attn_wk"].T, I["L0_attn_wv"].T, I["L0_attn_wg"].T], 1),
        "ret_w_o": I["L0_attn_wo"].T,
        "r0_w": I["L0_ffn_router_weight"].T,
        "r0_b": I["L0_ffn_router_bias"],
        "m0_w_gu": I["L0_ffn_gate_up_proj"],
        "m0_w_dn": I["L0_ffn_down_proj"],
        "m0_b_gu": I["L0_ffn_gate_up_bias"],
        "m0_b_dn": I["L0_ffn_down_bias"],
        "rms_w_in": _np.concatenate([I["L1_attn_Wq"][:, :D], I["L1_attn_Wk"], I["L1_attn_Wv"], I["L1_attn_Wq"][:, D:]], 1),
        "rms_b_in": _np.concatenate([I["L1_attn_bq"][:D], I["L1_attn_bk"], I["L1_attn_bv"], I["L1_attn_bq"][D:]]),
        "rms_norm_w": _np.concatenate([I["L1_attn_qn_w"], I["L1_attn_kn_w"]]),
        "rms_w_o": I["L1_attn_Wo"],
        "rms_b_o": I["L1_attn_bo"],
        "r1_w": I["L1_ffn_gate_w"].T,
        "r1_b": I["L1_ffn_expert_bias"],
        "m1_w_up": wide(I["L1_ffn_w_up"].transpose(0, 2, 1), 2),
        "m1_w_dn": wide(I["L1_ffn_w_down"].transpose(0, 2, 1), 1),
        "s_up": wide(I["L1_ffn_shared_w_up"].T, 1),
        "s_dn": wide(I["L1_ffn_shared_w_down"].T, 0),
        "cos": cos,
        "sin": sin,
        "decay": decay_table(),
        "ident": _np.eye(P, dtype=_np.float32),
        "iota": _np.arange(NS, dtype=_np.float32),
        "before": _np.triu(_np.ones((P, P), _np.float32), 1),
        "upto": _np.tril(_np.ones((E, E), _np.float32)).reshape(E * E),
    }
    nc = _bacc.Bacc("TRN2", target_bir_lowering=False, num_devices=1)
    arrays = {f"in_{k}": _np.ascontiguousarray(a) for k, a in arrays.items()}
    dram = {k[3:]: nc.dram_tensor(k, a.shape, _mybir.dt.from_np(a.dtype), kind="ExternalInput").ap()
            for k, a in arrays.items()}
    dram["out"] = nc.dram_tensor("out_0", (B * S, D), F32, kind="ExternalOutput").ap()
    dram["scratch"] = nc.dram_tensor("scratch", (B, 2, SK, H, S), BF16, kind="Internal").ap()
    for layer, dt in ((0, F32), (1, BF16)):
        dram[f"slots{layer}"] = nc.dram_tensor(f"slots{layer}", (NS * P, D), dt, kind="Internal").ap()
        dram[f"results{layer}"] = nc.dram_tensor(f"results{layer}", (NS * P, D), dt, kind="Internal").ap()
    vit_tower(nc, dram)
    r = _run(nc, [arrays], core_ids=[0])
    return r.results[0]["out_0"].reshape(B, S, D)
```

```python
from contextlib import ExitStack

import numpy as np

import concourse.bass as bass
from concourse import mybir

F32 = mybir.dt.float32
BF16 = mybir.dt.bfloat16
I32 = mybir.dt.int32
U32 = mybir.dt.uint32
ALU = mybir.AluOpType
ACT = mybir.ActivationFunctionType
AX_X = mybir.AxisListType.X

P = 128
B = 4
S = 512
D = 256
H = 16
HD = D // H
KD = D // P
TT = S // P
NT = B * TT
HG = H // 4
Q_PART = (0, 0, 0, 1, 1, 2)
K_PART = (0, 1, 2, 0, 1, 0)
SK = HD * len(Q_PART)
E = 8
FI = 512
LIMIT = 7.0
HID = 352
HIDP = 384
NS = 40
ZCOLS = 1280
LN_EPS = 1e-5
RMS_EPS = 1e-6


class Chain:

    def __init__(self, eng, sem):
        self.eng, self.sem, self.n = eng, sem, 0

    def mark(self, ins):
        ins.then_inc(self.sem, 1)
        self.n += 1
        return self.n

    def wait(self, n=None):
        self.eng.wait_ge(self.sem, self.n if n is None else n)



def semaphores(nc, ctx, prefix):
    taken = []

    def sem(name):
        taken.append(nc.alloc_semaphore(prefix + name))
        return taken[-1]

    def give_back():
        nc.clear_and_free_semaphores(taken)
        nc.all_engine_barrier()

    ctx.callback(give_back)
    return sem


def spread(ap, shape):
    return ap.broadcast_to(shape)



def attention_order(kind):
    softmax = kind != "ret"
    if kind == "tok":
        prepare = [(3, "qk", 0), (5, "qk", 2), (7, "qk", 1), (9, "qk", 3)]
    else:
        prepare = [(3, "turn_h", 0), (3, "turn_h", 1)] + [(4 + t, "rows", t) for t in range(TT)]
        if kind == "rms":
            prepare += [(5 + t, "square", t) for t in range(TT)] + [(8, "norm", 0)]
        prepare += [(9 + i, "qk", f) for i, f in enumerate((0, 2, 1, 3))]
    prepare += [(h + 1, "split", f) for h, what, f in prepare if what == "qk"]
    prepare = sorted(prepare, key=lambda x: x[0])
    finish = [(2 + t, "turn_o", t) for t in range(TT)] + [(7 + k, "turn_back", k) for k in range(KD)]
    finish += [(10 + u, "project_o", u) for u in range(2)]

    items = [(what, 0, i) for _, what, i in prepare]
    for h in range(H):
        if softmax:
            items.append(("row_max", 0, h))
            if h % 8 == 7:
                items.append(("turn_max", 0, h // 8))
        items += [(what, 1, i) for at, what, i in prepare if at == h]
    items += [("values_in", 0, t) for t in range(TT)]
    for b in range(B):
        for h in range(H):
            items.append(("scores", b, h))
            if softmax and b + 1 < B:
                items.append(("row_max", b + 1, h))
                if h % 8 == 7:
                    items.append(("turn_max", b + 1, h // 8))
            if b:
                items += [(what, b - 1, i) for at, what, i in finish if at == h]
            if h >= 4 and h % 4 < 2:
                items.append(("values", b, 2 * (h // 4 - 1) + h % 4))
            elif b and h < 2:
                items.append(("values", b - 1, 2 * (HG - 1) + h))
            if b and h in (1, 2):
                items += [("values_in", b, t) for t in (2 * h - 2, 2 * h - 1)]
            if b + 2 < B:
                items += [(what, b + 2, i) for at, what, i in prepare if at == h]
    items += [("values", B - 1, 2 * (HG - 1)), ("values", B - 1, 2 * HG - 1)]
    items += [(what, B - 1, i) for _, what, i in finish]
    return items


def attention(nc, kind, env, dram):
    tok, ret, rmsn = kind == "tok", kind == "ret", kind == "rms"
    softmax = not ret
    htok, ident = env["htok"], env["ident"]
    scratch = dram["scratch"]
    NW = {"tok": 768, "ret": 1024, "rms": 784}[kind]
    WV = NW - 512
    P_SLOTS = 6
    PCOLS = TT * S if softmax else TT * S - P * (1 + 2 + 3)
    order = attention_order(kind)

    ring_items = [x for x in order if x[0] in ("turn_h", "rows", "qk", "row_max", "turn_max", "values_in")]
    ring_uses = [(w, b, i, t) for w, b, i in ring_items for t in (range(TT) if w == "row_max" else (0,))]
    ring_at = {use: n for n, use in enumerate(ring_uses)}
    out_uses = [x for x in order if x[0] in ("turn_o", "turn_back", "project_o")]
    out_at = {use: n for n, use in enumerate(out_uses)}
    counts = {}
    nth = {}
    for x in order:
        nth[x] = counts.get(x[0], 0)
        counts[x[0]] = nth[x] + 1

    with ExitStack() as ctx:
        def sb(name, shape, dt=F32):
            return ctx.enter_context(nc.sbuf_tensor(f"{kind}_{name}", shape, dt))

        def ps(name, shape, dt=F32):
            return ctx.enter_context(nc.psum_tensor(f"{kind}_{name}", shape, dt))

        sem = semaphores(nc, ctx, f"{kind}_")

        w_in = sb("w_in", [P, KD, NW])
        w_o = sb("w_o", [P, KD, D])
        loads = [(w_in[:, :, :], dram[f"{kind}_w_in"].rearrange("(k p) n -> p k n", p=P)),
                 (w_o[:, :, :], dram[f"{kind}_w_o"].rearrange("(k p) n -> p k n", p=P))]
        if softmax:
            bias_o = sb("bias_o", [P, D])
            loads.append((bias_o[:, :], dram[f"{kind}_b_o"].partition_broadcast(P)))
            rowmax = sb("rowmax", [P, H * TT])
            negm = sb("negm", [H * TT // 2, 2, P])
            mparts = sb("mparts", [H * TT // 2, 3, P], BF16)
            rden = sb("rden", [P, TT, H])
        if tok:
            bias_qk = sb("bias_qk", [P, 4])
            bias_v = sb("bias_v", [P, D])
            loads += [(bias_qk[:, :], dram["tok_b_qk"]), (bias_v[:, :], dram["tok_b_v"].partition_broadcast(P))]
        if rmsn:
            bias_in = sb("bias_in", [P, NW])
            norm_w = sb("norm_w", [P, 2])
            ssq = sb("ssq", [P, TT, 32])
            rms = sb("rms", [P, TT, 32])
            squares = sb("squares", [P, 2, S])
            gate = sb("gate", [P, 2, TT, H])
            graw = sb("graw", [P, H])
            loads += [(bias_in[:, :], dram["rms_b_in"].partition_broadcast(P)), (norm_w[:, :], dram["rms_norm_w"])]
        if ret:
            causal = sb("causal", [P, P])
            cos = sb("cos", [P, TT, 32, 8])
            sin = sb("sin", [P, TT, 32, 8])
            gate = sb("gate", [P, 2, TT, D])
            xcos = sb("xcos", [P, S])
            xsin = sb("xsin", [P, S])
            loads += [(causal[:, :], dram["causal"]),
                      (cos[:, :, :, :].rearrange("p t a r -> p t (a r)"), dram["cos"].rearrange("(t p) r -> p t r", p=P)),
                      (sin[:, :, :, :].rearrange("p t a r -> p t (a r)"), dram["sin"].rearrange("(t p) r -> p t r", p=P))]
        if not tok:
            stats = sb("stats", [P, 6])
            mv = sb("mv", [P, NT, 2])
            veps = sb("veps", [P, NT])
            rstd = sb("rstd", [P, NT])
            half = sb("half", [P, TT * 32])
            rot = sb("rot", [P, TT, S])
        ht = sb("ht", [P, 2, KD, S])
        left = sb("left", [P, 2, S])
        parts = sb("parts", [P, 2, 3, S], BF16)
        qs = sb("qs", [SK + 3, 2, H, S], BF16)
        ks = sb("ks", [SK + 3, 2, H, S], BF16)
        v = sb("v", [P, TT, H, 32])
        prob = sb("prob", [P, P_SLOTS, PCOLS])
        ot = sb("ot", [P, HG, S])
        otok = sb("otok", [P, TT, D])
        ot2 = sb("ot2", [P, KD, S])

        ring = ps("ring", [P, 2, S])
        score = ps("score", [P, 2, 2, S])
        valps = ps("valps", [P, S])
        outps = ps("outps", [P, S])

        weights_in = sem("weights_in")
        x_in = [sem(f"x_in{i}") for i in range(2)]
        ones_set = sem("ones_set")
        half_set = sem("half_set")
        key_ones = sem("key_ones")
        ring_filled = sem("ring_filled")
        ht_ready = sem("ht_ready")
        rows_ready = sem("rows_ready")
        turned_ready = sem("turned_ready")
        squares_ready = sem("squares_ready")
        ssq_ready = sem("ssq_ready")
        rms_ready = sem("rms_ready")
        rot_ready = sem("rot_ready")
        part0_ready = sem("part0_ready")
        left_ready = sem("left_ready")
        part1_ready = sem("part1_ready")
        parts_ready = sem("parts_ready")
        parts_saved = [sem(f"parts_saved{i}") for i in range(2)]
        stacked = [sem(f"stacked{i}") for i in range(4)]
        max_done = sem("max_done")
        negm_ready = sem("negm_ready")
        mparts_ready = sem("mparts_ready")
        maxrows_in = [sem(f"maxrows_in{i}") for i in range(2)]
        score_filled = sem("score_filled")
        prob_ready = sem("prob_ready")
        prob_diag = sem("prob_diag")
        v_ready = sem("v_ready")
        graw_ready = sem("graw_ready")
        gexp_ready = sem("gexp_ready")
        gate_ready = sem("gate_ready")
        val_filled = sem("val_filled")
        ot_ready = sem("ot_ready")
        out_filled = sem("out_filled")
        rden_step = sem("rden_step")
        otok_ready = sem("otok_ready")
        ot2_ready = sem("ot2_ready")
        y_ready = sem("y_ready")
        stats_ready = sem("stats_ready")
        rstd_ready = sem("rstd_ready")
        pool_step = sem("pool_step")
        dve_step = sem("dve_step")

        def ring_release(use):
            what, b, i, t = use
            n = nth[what, b, i]
            if what == "row_max":
                return max_done, TT * n + t + 1
            if what == "values_in":
                return (graw_ready if rmsn else gate_ready if ret else v_ready), n + 1
            return {"turn_h": ht_ready, "rows": rows_ready, "qk": left_ready, "turn_max": negm_ready}[what], n + 1

        def ring_view(what, b, i, t=0):
            n = ring_at[what, b, i, t]
            return ring[:, n % 2, :], n + 1

        def out_release(use):
            what = use[0]
            return {"turn_o": otok_ready, "turn_back": ot2_ready, "project_o": y_ready}[what], nth[use] + 1

        def stack_ready(b, h):
            return stacked[2 * (b % 2) + h // 8], 32 * (b // 2 + 1)

        DIAG = [(kt, kt, 1, P * kt) for kt in range(TT)]
        OFF = [(0, 1, 3, 0), (2, 3, 1, 3 * P), (1, 2, 2, 0)]

        block = ctx.enter_context(nc.Block())

        @block.sync
        def _(sp):
            for dst, src in loads:
                sp.dma_start(dst, src).then_inc(weights_in, 16)
            for hook in env.get(f"{kind}_dmas", ()):
                hook(sp)

            def load_x(b):
                if b >= 2:
                    sp.wait_ge(ring_filled, ring_at["values_in", b - 2, TT - 1, 0] + 1)
                sp.dma_start(ht[:, b % 2, :, :],
                             dram["x"].rearrange("(k p) n -> p k n", p=P)[:, :, b * S:(b + 1) * S]).then_inc(x_in[b % 2], 16)

            def save_parts(b, f):
                n = nth["split", b, f]
                heads = slice(8 * (f % 2), 8 * (f % 2) + 8)
                sp.wait_ge(parts_ready, n + 1)
                for g, part in enumerate(K_PART if f // 2 else Q_PART):
                    sp.dma_start(scratch[b, f // 2, HD * g:HD * g + HD, heads, :].rearrange("d h n -> h d n"),
                                 parts[:, n % 2, part, :]).then_inc(parts_saved[n % 2], 16)

            def stack(b, f):
                n = nth["split", b, f]
                heads = slice(8 * (f % 2), 8 * (f % 2) + 8)
                sp.wait_ge(parts_saved[n % 2], 96 * (n // 2 + 1))
                if b >= 2:
                    sp.wait_ge(score_filled, 2 * (H * (b - 2) + 8 * (f % 2) + 8))
                sp.dma_start((ks if f // 2 else qs)[0:SK, b % 2, heads, :].rearrange("p h n -> p (h n)"),
                             scratch[b, f // 2, :, heads, :].rearrange("p h n -> p (h n)")
                             ).then_inc(stacked[2 * (b % 2) + f % 2], 16)

            def max_rows(b, i):
                sp.wait_ge(mparts_ready, 2 * b + i + 1)
                for j in range(3):
                    sp.dma_start(qs[SK + j:SK + j + 1, b % 2, 8 * i:8 * i + 8, :].rearrange("o h (t q) -> o (h t) q", q=P),
                                 mparts[:, j, :]).then_inc(maxrows_in[i], 16)

            late = []
            for what, b, i in order:
                if what == "qk" and tok and i == 0:
                    if b < 2:
                        load_x(b)
                if what == "values_in" and tok and i == TT - 1 and b + 2 < B:
                    load_x(b + 2)
                if what == "split":
                    save_parts(b, i)
                    if i == 2:
                        stack(b, 0)
                        stack(b, 2)
                    if i == 3:
                        if b < 2:
                            stack(b, 1)
                            stack(b, 3)
                        else:
                            late.append(b)
                if what == "turn_max":
                    max_rows(b, i)
                if what == "scores" and i == 0 and late:
                    bb = late.pop()
                    stack(bb, 1)
                    stack(bb, 3)

        @block.gpsimd
        def _(pool):
            chain = Chain(pool, pool_step)
            pool.memset(v[:, :, :, HD:32], 1.0).then_inc(ones_set, 1)
            if not tok:
                pool.memset(half[:, :], -0.5).then_inc(half_set, 1)
                pool.wait_ge(half_set, 1)
            for what, b, i in order:
                n = nth[what, b, i]
                if what == "rows" and ret:
                    pool.wait_ge(rows_ready, n + 1)
                    if i == 0 and b:
                        pool.wait_ge(ring_filled, ring_at["qk", b - 1, 3, 0] + 1)
                    halves = lambda a: a.rearrange("p (h s r) -> p h s r", s=2, r=8)
                    a, z, r = halves(xcos[:, :]), halves(xsin[:, :]), halves(rot[:, i, :])
                    chain.mark(pool.tensor_tensor(r[:, :, 0, :], a[:, :, 0, :], z[:, :, 1, :], ALU.subtract))
                    pool.tensor_tensor(r[:, :, 1, :], a[:, :, 1, :], z[:, :, 0, :], ALU.add).then_inc(rot_ready, 1)
                    chain.wait()
                    pool.wait_ge(rot_ready, n + 1)
                if what == "norm":
                    pool.wait_ge(ssq_ready, TT * (b + 1))
                    chain.mark(pool.tensor_scalar(ssq[:, :, :], ssq[:, :, :], 1.0 / HD, RMS_EPS, ALU.mult, ALU.add))
                    chain.wait()
                    pool.tensor_tensor(rms[:, :, :].rearrange("p t a -> p (t a)"),
                                       ssq[:, :, :].rearrange("p t a -> p (t a)"), half[:, :],
                                       ALU.pow).then_inc(rms_ready, 1)
                if what == "split":
                    pool.wait_ge(part1_ready, n + 1)
                    pool.tensor_tensor(parts[:, n % 2, 2, :], left[:, n % 2, :], parts[:, n % 2, 1, :],
                                       ALU.subtract).then_inc(parts_ready, 1)
                if what == "turn_max":
                    pool.wait_ge(negm_ready, n + 1)
                    if n:
                        pool.wait_ge(maxrows_in[(n - 1) % 2], 48 * ((n - 1) // 2 + 1))
                    a, r = negm[:, 0, :], negm[:, 1, :]
                    chain.mark(pool.tensor_copy(mparts[:, 0, :], a))
                    chain.wait()
                    chain.mark(pool.tensor_tensor(r, a, mparts[:, 0, :], ALU.subtract))
                    chain.wait()
                    chain.mark(pool.tensor_copy(mparts[:, 1, :], r))
                    chain.wait()
                    pool.tensor_tensor(mparts[:, 2, :], r, mparts[:, 1, :], ALU.subtract).then_inc(mparts_ready, 1)
                    pool.wait_ge(mparts_ready, n + 1)
                if what == "values_in" and rmsn:
                    pool.wait_ge(gexp_ready, n + 1)
                    pool.tensor_scalar(gate[:, b % 2, i, :], gate[:, b % 2, i, :], 1.0, None,
                                       ALU.add).then_inc(gate_ready, 1)
            if not tok:
                pool.wait_ge(stats_ready, NT)
                chain.mark(pool.tensor_scalar(veps[:, :], mv[:, :, 1], 1.0, LN_EPS, ALU.mult, ALU.add))
                chain.wait()
                pool.tensor_tensor(rstd[:, :], veps[:, :], half[:, 0:NT], ALU.pow).then_inc(rstd_ready, 1)
                pool.wait_ge(rstd_ready, 1)
                for n in range(2, NT, 3):
                    pool.tensor_scalar(htok[:, n, :], htok[:, n, :], mv[:, n, 0:1], rstd[:, n:n + 1],
                                       ALU.subtract, ALU.mult)

        @block.tensor
        def _(pe):
            pe.wait_ge(weights_in, 16 * len(loads))

            def use_ring(what, b, i, t=0):
                n = ring_at[what, b, i, t]
                if n >= 2:
                    pe.wait_ge(*ring_release(ring_uses[n - 2]))
                return ring[:, n % 2, :]

            def use_out(what, b, i):
                n = out_at[what, b, i]
                if n:
                    pe.wait_ge(*out_release(out_uses[n - 1]))
                return outps[:, :]

            def turn_h(b, k):
                dst = use_ring("turn_h", b, k)
                for t in range(TT):
                    mm = pe.transpose(dst[:, P * t:P * t + P], htok[:, TT * b + t, P * k:P * k + P], ident[:, :])
                mm.then_inc(ring_filled, 1)

            def rows(b, t):
                if t == 0:
                    pe.wait_ge(ht_ready, KD * (b + 1))
                dst = use_ring("rows", b, t)
                for k in range(KD):
                    mm = pe.matmul(dst, ht[:, b % 2, k, P * t:P * t + P], w_in[:, k, 0:512],
                                   start=(k == 0), stop=(k == KD - 1))
                mm.then_inc(ring_filled, 1)

            def qk(b, f):
                if tok:
                    if f == 0:
                        pe.wait_ge(x_in[b % 2], 16 * (b // 2 + 1))
                    dst = use_ring("qk", b, f)
                    for k in range(KD):
                        mm = pe.matmul(dst, w_in[:, k, P * f:P * f + P], ht[:, b % 2, k, :],
                                       start=(k == 0), stop=(k == KD - 1))
                else:
                    if f == 0:
                        pe.wait_ge(rot_ready, TT * (b + 1))
                    dst = use_ring("qk", b, f)
                    for t in range(TT):
                        mm = pe.transpose(dst[:, P * t:P * t + P], rot[:, t, P * f:P * f + P], ident[:, :])
                mm.then_inc(ring_filled, 1)

            def values_in(b, t):
                dst = use_ring("values_in", b, t)
                for k in range(KD):
                    mm = pe.matmul(dst[:, 0:WV], ht[:, b % 2, k, P * t:P * t + P], w_in[:, k, 512:NW],
                                   start=(k == 0), stop=(k == KD - 1))
                mm.then_inc(ring_filled, 1)

            def row_max(b, h):
                if h % 8 == 0:
                    pe.wait_ge(*stack_ready(b, h))
                for t in range(TT):
                    dst = use_ring("row_max", b, h, t)
                    pe.matmul(dst, qs[0:SK, b % 2, h, P * t:P * t + P], ks[0:SK, b % 2, h, :],
                              start=True, stop=True).then_inc(ring_filled, 1)

            def turn_max(b, i):
                dst = use_ring("turn_max", b, i)
                pe.wait_ge(max_done, TT * (H * b + 8 * i + 8))
                pe.transpose(dst[0:H * TT // 2, 0:P], rowmax[:, 8 * TT * i:8 * TT * i + 8 * TT],
                             ident[:, :]).then_inc(ring_filled, 1)

            def scores(b, h):
                if h % 8 == 0:
                    pe.wait_ge(*stack_ready(b, h))
                    if softmax:
                        pe.wait_ge(maxrows_in[h // 8], 48 * (b + 1))
                        if h == 0 and b == 0:
                            pe.wait_ge(key_ones, 1)
                for p in range(2):
                    n = 2 * (H * b + h) + p
                    if softmax:
                        if n >= 2:
                            pe.wait_ge(prob_ready, n - 1)
                        for i in range(2):
                            kt = 2 * p + i
                            mm = pe.matmul(score[:, n % 2, i, :], ks[0:SK + 3, b % 2, h, P * kt:P * kt + P],
                                           qs[0:SK + 3, b % 2, h, :], start=True, stop=True)
                        mm.then_inc(score_filled, 1)
                        continue
                    if p == 0:
                        hh = H * b + h
                        if hh:
                            pe.wait_ge(prob_diag, hh)
                        for kt, qt, nq, at in DIAG:
                            mm = pe.matmul(score[:, 0, 0, at:at + P * nq], ks[0:SK, b % 2, h, P * kt:P * kt + P],
                                           qs[0:SK, b % 2, h, P * qt:P * (qt + nq)], start=True, stop=True)
                    else:
                        if hh:
                            pe.wait_ge(prob_ready, hh)
                        for j, (kt, qt, nq, at) in enumerate(OFF):
                            mm = pe.matmul(score[:, 1, j // 2, at:at + P * nq], ks[0:SK, b % 2, h, P * kt:P * kt + P],
                                           qs[0:SK, b % 2, h, P * qt:P * (qt + nq)], start=True, stop=True)
                    mm.then_inc(score_filled, 1)

            def values(b, i):
                g, piece = i // 2, i % 2
                if piece == 0:
                    hh = H * b + 4 * g + 4
                    pe.wait_ge(prob_ready, 2 * hh if softmax else hh)
                    if ret:
                        pe.wait_ge(prob_diag, hh)
                    if b + g:
                        pe.wait_ge(ot_ready, HG * b + g)
                    if g == 0:
                        pe.wait_ge(v_ready, TT * (b + 1))
                        pe.wait_ge(ones_set, 1)
                if softmax:
                    blocks = [(kt, 0, TT, S * kt) for kt in (2 * piece, 2 * piece + 1)]
                else:
                    off = [(kt, qt, nq, S + S * (j // 2) + at) for j, (kt, qt, nq, at) in enumerate(OFF)]
                    blocks = [off[0], DIAG[0], off[2]] if piece == 0 else [off[1]] + DIAG[1:]
                for n, (kt, qt, nq, at) in enumerate(blocks):
                    for j in range(4):
                        h = 4 * g + j
                        mm = pe.matmul(valps[32 * j:32 * j + 32, P * qt:P * (qt + nq)], v[:, kt, h, :],
                                       prob[:, (H * b + h) % P_SLOTS, at:at + P * nq],
                                       start=(piece == 0 and n == 0), stop=(piece == 1 and n == len(blocks) - 1),
                                       tile_position=(0, 32 * j), skip_group_check=not softmax)
                mm.then_inc(val_filled, 1)

            def turn_o(b, t):
                if t == 0:
                    pe.wait_ge(ot_ready, HG * (b + 1))
                dst = use_out("turn_o", b, t)
                for g in range(HG):
                    mm = pe.transpose(dst[:, P * g:P * g + P], ot[:, g, P * t:P * t + P], ident[:, :])
                mm.then_inc(out_filled, 1)

            def turn_back(b, k):
                if k == 0:
                    pe.wait_ge(otok_ready, TT * (b + 1))
                dst = use_out("turn_back", b, k)
                for t in range(TT):
                    mm = pe.transpose(dst[:, P * t:P * t + P], otok[:, t, P * k:P * k + P], ident[:, :])
                mm.then_inc(out_filled, 1)

            def project_o(b, u):
                if u == 0:
                    pe.wait_ge(ot2_ready, KD * (b + 1))
                dst = use_out("project_o", b, u)
                for i in range(2):
                    t = 2 * u + i
                    for k in range(KD):
                        mm = pe.matmul(dst[:, D * i:D * i + D], ot2[:, k, P * t:P * t + P], w_o[:, k, :],
                                       start=(k == 0), stop=(k == KD - 1))
                mm.then_inc(out_filled, 1)

            work = dict(turn_h=turn_h, rows=rows, qk=qk, values_in=values_in, row_max=row_max, turn_max=turn_max,
                        scores=scores, values=values, turn_o=turn_o, turn_back=turn_back, project_o=project_o)
            for what, b, i in order:
                if what in work:
                    work[what](b, i)

        @block.scalar
        def _(act):
            act.wait_ge(weights_in, 16 * len(loads))
            for what, b, i in order:
                n = nth[what, b, i]
                if what == "turn_h":
                    src, filled = ring_view(what, b, i)
                    act.wait_ge(ring_filled, filled)
                    if b >= 2 and i == 0:
                        act.wait_ge(ring_filled, ring_at["values_in", b - 2, TT - 1, 0] + 1)
                    act.activation(ht[:, b % 2, i, :], src, ACT.Copy).then_inc(ht_ready, 1)
                if what == "square":
                    act.wait_ge(rows_ready, n + 1)
                    if n >= 2:
                        act.wait_ge(ssq_ready, n - 1)
                    act.activation(squares[:, n % 2, :], rot[:, i, :], ACT.Square).then_inc(squares_ready, 1)
                if what == "qk":
                    src, filled = ring_view(what, b, i)
                    act.wait_ge(ring_filled, filled)
                    if n >= 2:
                        act.wait_ge(parts_saved[n % 2], 96 * (n // 2))
                    if tok:
                        act.activation(parts[:, n % 2, 0, :], src, ACT.Identity,
                                       bias=bias_qk[:, i:i + 1]).then_inc(part0_ready, 1)
                    elif rmsn:
                        act.activation(parts[:, n % 2, 0, :], src, ACT.Copy,
                                       scale=norm_w[:, i // 2:i // 2 + 1]).then_inc(part0_ready, 1)
                    else:
                        act.activation(parts[:, n % 2, 0, :], src, ACT.Copy).then_inc(part0_ready, 1)
                if what == "split":
                    act.wait_ge(left_ready, n + 1)
                    act.activation(parts[:, n % 2, 1, :], left[:, n % 2, :], ACT.Copy).then_inc(part1_ready, 1)
                if what == "scores":
                    hh = H * b + i
                    old = hh - P_SLOTS
                    if softmax:
                        for p in range(2):
                            act.wait_ge(score_filled, 2 * hh + p + 1)
                            if p == 0 and old >= 0:
                                act.wait_ge(val_filled, 2 * (old // 4) + 2)
                            act.activation(prob[:, hh % P_SLOTS, 2 * p * S:2 * (p + 1) * S],
                                           score[:, p, :, :].rearrange("p i n -> p (i n)"), ACT.Exp,
                                           scale=HD ** -0.5).then_inc(prob_ready, 1)
                    else:
                        act.wait_ge(score_filled, 2 * hh + 2)
                        if old >= 0:
                            act.wait_ge(val_filled, 2 * (old // 4) + 2)
                        act.activation(prob[:, hh % P_SLOTS, S:S + 6 * P],
                                       score[:, 1, :, :].rearrange("p i n -> p (i n)")[:, 0:6 * P],
                                       ACT.Copy).then_inc(prob_ready, 1)
                if what == "values" and i % 2:
                    act.wait_ge(val_filled, n + 1)
                    if b and i == 1:
                        act.wait_ge(out_filled, out_at["turn_o", b - 1, TT - 1] + 1)
                    act.activation(ot[:, i // 2, :], valps[:, :], ACT.Copy).then_inc(ot_ready, 1)
                if what == "values_in" and ret:
                    src, filled = ring_view(what, b, i)
                    act.wait_ge(ring_filled, filled)
                    if b and i == 0:
                        act.wait_ge(val_filled, 2 * HG * b)
                    act.activation(v[:, i, :, 0:HD], src[:, 0:D].rearrange("p (h d) -> p h d", d=HD),
                                   ACT.Copy).then_inc(v_ready, 1)
                    if b >= 2 and i == 0:
                        act.wait_ge(otok_ready, TT * (b - 1))
                    act.activation(gate[:, b % 2, i, :], src[:, D:2 * D], ACT.Silu).then_inc(gate_ready, 1)
                if what == "values_in" and rmsn:
                    act.wait_ge(graw_ready, n + 1)
                    if b >= 2 and i == 0:
                        act.wait_ge(otok_ready, TT * (b - 1))
                    act.activation(gate[:, b % 2, i, :], graw[:, :], ACT.Exp, scale=-1.0).then_inc(gexp_ready, 1)
                if what == "turn_back":
                    act.wait_ge(out_filled, out_at[what, b, i] + 1)
                    act.activation(ot2[:, i, :], outps[:, :], ACT.Copy).then_inc(ot2_ready, 1)

        @block.vector
        def _(dve):
            chain = Chain(dve, dve_step)
            if softmax:
                dve.memset(ks[SK:SK + 3, :, :, :].rearrange("p b h n -> p (b h n)").bitcast(I32),
                           0x3F803F80).then_inc(key_ones, 1)
            dve.wait_ge(weights_in, 16 * len(loads))
            heads = lambda a: a.rearrange("p (h d) -> p h d", d=HD)

            for what, b, i in order:
                n = nth[what, b, i]
                if what == "rows":
                    src, filled = ring_view(what, b, i)
                    dve.wait_ge(ring_filled, filled)
                    if rmsn:
                        if i == 0 and b:
                            dve.wait_ge(ring_filled, ring_at["qk", b - 1, 3, 0] + 1)
                        dve.tensor_tensor(rot[:, i, :], src, bias_in[:, 0:512], ALU.add).then_inc(rows_ready, 1)
                    else:
                        if n:
                            dve.wait_ge(rot_ready, n)
                        quad = lambda a: a.rearrange("p (h s r) -> p h s r", s=2, r=8)
                        both = lambda a: spread(a.rearrange("p h (s r) -> p h s r", s=1), [P, 32, 2, 8])
                        dve.tensor_tensor(quad(xcos[:, :]), quad(src), both(cos[:, i, :, :]), ALU.mult)
                        dve.tensor_tensor(quad(xsin[:, :]), quad(src), both(sin[:, i, :, :]),
                                          ALU.mult).then_inc(rows_ready, 1)
                if what == "square":
                    dve.wait_ge(squares_ready, n + 1)
                    if i == 0 and b:
                        dve.wait_ge(rms_ready, b)
                    dve.tensor_reduce(ssq[:, i, :], squares[:, n % 2, :].rearrange("p (a d) -> p a d", d=HD), AX_X,
                                      ALU.add).then_inc(ssq_ready, 1)
                if what == "norm":
                    dve.wait_ge(rms_ready, b + 1)
                    for t in range(TT):
                        r = spread(rms[:, t, :].rearrange("p (a o) -> p a o", o=1), [P, 32, HD])
                        dve.tensor_tensor(heads(rot[:, t, :]), heads(rot[:, t, :]), r, ALU.mult).then_inc(rot_ready, 1)
                if what == "qk":
                    src, filled = ring_view(what, b, i)
                    dve.wait_ge(part0_ready, n + 1)
                    if n >= 2:
                        dve.wait_ge(parts_ready, n - 1)
                    part0 = parts[:, n % 2, 0, :]
                    if tok:
                        dve.scalar_tensor_tensor(out=left[:, n % 2, :], in0=src, scalar=bias_qk[:, i:i + 1], in1=part0,
                                                 op0=ALU.add, op1=ALU.subtract).then_inc(left_ready, 1)
                    elif rmsn:
                        dve.scalar_tensor_tensor(out=left[:, n % 2, :], in0=src, scalar=norm_w[:, i // 2:i // 2 + 1],
                                                 in1=part0, op0=ALU.mult, op1=ALU.subtract).then_inc(left_ready, 1)
                    else:
                        dve.tensor_tensor(left[:, n % 2, :], src, part0, ALU.subtract).then_inc(left_ready, 1)
                if what == "row_max":
                    for t in range(TT):
                        src, filled = ring_view(what, b, i, t)
                        dve.wait_ge(ring_filled, filled)
                        dve.reduce_max(rowmax[:, TT * i + t:TT * i + t + 1], src, AX_X).then_inc(max_done, 1)
                if what == "turn_max":
                    src, filled = ring_view(what, b, i)
                    dve.wait_ge(ring_filled, filled)
                    if n:
                        dve.wait_ge(mparts_ready, n)
                    dve.tensor_scalar(negm[:, 0, :], src[0:H * TT // 2, 0:P], -1.0, None, ALU.mult).then_inc(negm_ready, 1)
                if what == "values_in" and softmax:
                    src, filled = ring_view(what, b, i)
                    dve.wait_ge(ring_filled, filled)
                    if b and i == 0:
                        dve.wait_ge(val_filled, 2 * HG * b)
                    bias = bias_v[:, :] if tok else bias_in[:, 512:512 + D]
                    dve.tensor_tensor(v[:, i, :, 0:HD], heads(src[:, 0:D]), heads(bias), ALU.add).then_inc(v_ready, 1)
                    if rmsn:
                        if n:
                            dve.wait_ge(gexp_ready, n)
                        dve.tensor_tensor(graw[:, :], src[:, D:D + H], bias_in[:, 512 + D:NW],
                                          ALU.add).then_inc(graw_ready, 1)
                if what == "scores" and ret:
                    hh = H * b + i
                    old = hh - P_SLOTS
                    dve.wait_ge(score_filled, 2 * hh + 1)
                    if old >= 0:
                        dve.wait_ge(val_filled, 2 * (old // 4) + 2)
                    dve.tensor_tensor(prob[:, hh % P_SLOTS, 0:S].rearrange("p (t n) -> p t n", n=P),
                                      score[:, 0, 0, :].rearrange("p (t n) -> p t n", n=P),
                                      spread(causal[:, :].rearrange("p (t n) -> p t n", t=1), [P, TT, P]),
                                      ALU.mult).then_inc(prob_diag, 1)
                if what == "turn_o":
                    dve.wait_ge(out_filled, out_at[what, b, i] + 1)
                    if b and i == 0:
                        dve.wait_ge(out_filled, out_at["turn_back", b - 1, KD - 1] + 1)
                    o = outps[:, :].rearrange("p (h e) -> p h e", e=32)
                    if ret:
                        dve.wait_ge(gate_ready, n + 1)
                        dve.tensor_tensor(heads(otok[:, i, :]), o[:, :, 0:HD], heads(gate[:, b % 2, i, :]),
                                          ALU.mult).then_inc(otok_ready, 1)
                        continue
                    r = rden[:, i, :]
                    if rmsn:
                        dve.wait_ge(gate_ready, n + 1)
                        chain.mark(dve.tensor_tensor(r, o[:, :, HD], gate[:, b % 2, i, :], ALU.mult))
                        chain.wait()
                        dve.reciprocal(r, r).then_inc(rden_step, 1)
                    else:
                        dve.reciprocal(r, o[:, :, HD]).then_inc(rden_step, 1)
                    dve.wait_ge(rden_step, n + 1)
                    dve.tensor_tensor(heads(otok[:, i, :]), o[:, :, 0:HD],
                                      spread(r.rearrange("p (h o) -> p h o", o=1), [P, H, HD]),
                                      ALU.mult).then_inc(otok_ready, 1)
                if what == "project_o":
                    dve.wait_ge(out_filled, out_at[what, b, i] + 1)
                    t = TT * b + 2 * i
                    y = htok[:, t:t + 2, :]
                    o = outps[:, :].rearrange("p (i d) -> p i d", d=D)
                    if tok:
                        dve.tensor_tensor(y, o, spread(bias_o[:, :].rearrange("p (i d) -> p i d", i=1), [P, 2, D]),
                                          ALU.add).then_inc(y_ready, 1)
                        continue
                    dve.tensor_tensor(y, y, o, ALU.add).then_inc(y_ready, 1)
                    dve.wait_ge(y_ready, n + 1)
                    if rmsn:
                        chain.mark(dve.tensor_tensor(
                            y, y, spread(bias_o[:, :].rearrange("p (i d) -> p i d", i=1), [P, 2, D]), ALU.add))
                        chain.wait()
                    for j in range(2):
                        chain.mark(dve.bn_stats(stats[:, :], htok[:, t + j, :]))
                        chain.wait()
                        dve.bn_aggr(mv[:, t + j, :], stats[:, :]).then_inc(stats_ready, 1)
                        dve.wait_ge(stats_ready, t + j + 1)
            if not tok:
                dve.wait_ge(rstd_ready, 1)
                for n in range(NT):
                    if n % 3 != 2:
                        dve.tensor_scalar(htok[:, n, :], htok[:, n, :], mv[:, n, 0:1], rstd[:, n:n + 1],
                                          ALU.subtract, ALU.mult)


def layernorm_rows(pool, chain, mv, veps, rstd, half, rstd_ready):
    chain.mark(pool.tensor_scalar(veps[:, :], mv[:, :, 1], 1.0, LN_EPS, ALU.mult, ALU.add))
    chain.wait()
    pool.tensor_tensor(rstd[:, :], veps[:, :], half[:, 0:NT], ALU.pow).then_inc(rstd_ready, 1)


def moe(nc, layer, env, dram):
    first = layer == 0
    htok, ident = env["htok"], env["ident"]
    rows_in, rows_out = dram[f"slots{layer}"], dram[f"results{layer}"]
    XT = F32 if first else BF16

    with ExitStack() as outer:
        def sbo(name, shape, dt=F32):
            return outer.enter_context(nc.sbuf_tensor(f"m{layer}_{name}", shape, dt))

        slot = sbo("slot", [P, NT, 2], I32)
        weight = sbo("weight", [P, NT, 2])
        expert = sbo("expert", [P, NS], I32)
        if first:
            w_gu = sbo("w_gu", [P, KD, E, 2 * FI])
            w_dn = sbo("w_dn", [P, FI // P, E, D])
            b_gu = sbo("b_gu", [P, E, 2 * FI])
            b_dn = sbo("b_dn", [P, E, D])
        else:
            w_up = sbo("w_up", [P, E, KD, HIDP], BF16)
            w_dn = sbo("w_dn", [P, E, HIDP // P, D], BF16)

        with ExitStack() as ctx:
            def sb(name, shape, dt=F32):
                return ctx.enter_context(nc.sbuf_tensor(f"r{layer}_{name}", shape, dt))

            def ps(name, shape, dt=F32):
                return ctx.enter_context(nc.psum_tensor(f"r{layer}_{name}", shape, dt))

            sem = semaphores(nc, ctx, f"r{layer}_")

            hT = sb("hT", [P, KD, NT * P])
            rw = sb("rw", [P, KD, E])
            rb = sb("rb", [P, E])
            iota = sb("iota", [P, NS])
            before = sb("before", [P, P])
            ones = sb("ones", [P, P])
            upto = sb("upto", [P, E, E])
            logit = sb("logit", [P, NT, E])
            score = sb("score", [P, NT, E])
            choice = sb("choice", [P, NT, E]) if not first else score
            top = sb("top", [P, NT])
            total = sb("total", [P, NT])
            max8 = sb("max8", [P, NT, 8])
            idx8 = sb("idx8", [P, NT, 8], U32)
            idxf = sb("idxf", [P, 2, NT])
            pick = sb("pick", [P, 2, NT, E])
            both = sb("both", [P, NT, E])
            prod = sb("prod", [P, 2, NT, E])
            count = sb("count", [P, E])
            count_i = sb("count_i", [P, E], I32)
            tiles_i = sb("tiles_i", [P, E], I32)
            tiles = sb("tiles", [P, E])
            tri = sb("tri", [P, E, E])
            upto_e = sb("upto_e", [P, E])
            base = sb("base", [P, E])
            place = sb("place", [P, NT, E])
            slotf = sb("slotf", [P, 2, NT])
            cmp = sb("cmp", [P, NS, E])
            expf = sb("expf", [P, NS])
            turned = ps("turned", [P, 2, S])
            small = ps("small", [P, S])
            places = ps("places", [P, S])
            counts = small[:, 2 * NT * E:2 * NT * E + E]
            loads = [(rw[:, :, :], dram[f"r{layer}_w"].rearrange("(k p) e -> p k e", p=P)),
                     (rb[:, :], dram[f"r{layer}_b"].partition_broadcast(P)),
                     (iota[:, :], dram["iota"].partition_broadcast(P)),
                     (before[:, :], dram["before"]),
                     (upto[:, :, :].rearrange("p a b -> p (a b)"), dram["upto"].partition_broadcast(P))]
            if first:
                late = [(w_gu[:, :, e, :], dram["m0_w_gu"][e].rearrange("(k p) n -> p k n", p=P)) for e in range(E)]
                late += [(w_dn[:, :, e, :], dram["m0_w_dn"][e].rearrange("(k p) n -> p k n", p=P)) for e in range(E)]
                late += [(b_gu[:, e, :], dram["m0_b_gu"][e].partition_broadcast(P)) for e in range(E)]
                late += [(b_dn[:, e, :], dram["m0_b_dn"][e].partition_broadcast(P)) for e in range(E)]
            else:
                s_up = sb("s_up", [P, KD, HIDP])
                s_dn = sb("s_dn", [P, HIDP // P, D])
                raw = sb("raw", [P, 2, KD * HIDP])
                hid = sb("hid", [P, 2, HIDP // P, S])
                scaled = sb("scaled", [P, NT, 2, D], BF16)
                shup = ps("shup", [P, 2, S])
                shdn = ps("shdn", [P, 2, S])
                loads += [(s_up[:, :, :], dram["s_up"].rearrange("(k p) n -> p k n", p=P)),
                          (s_dn[:, :, :], dram["s_dn"].rearrange("(k p) n -> p k n", p=P))]
                late = []

            loaded = sem("loaded")
            weights_in = sem("weights_in")
            ones_set = sem("ones_set")
            turned_filled = sem("turned_filled")
            ht_ready = sem("ht_ready")
            logits_filled = sem("logits_filled")
            logits_ready = sem("logits_ready")
            exp_ready = sem("exp_ready")
            both_ready = sem("both_ready")
            places_filled = sem("places_filled")
            slots_ready = sem("slots_ready")
            sent = sem("sent")
            dve_step = sem("dve_step")
            raw_in = [sem(f"raw_in{i}") for i in range(2)]
            cast_done = sem("cast_done")
            up_filled = sem("up_filled")
            relu_ready = sem("relu_ready")
            hid_ready = sem("hid_ready")
            dn_filled = sem("dn_filled")
            dn_read = sem("dn_read")
            scaled_ready = sem("scaled_ready")
            HC = HIDP // P

            block = ctx.enter_context(nc.Block())

            @block.sync
            def _(sp):
                for dst, src in loads:
                    sp.dma_start(dst, src).then_inc(loaded, 16)
                for dst, src in late:
                    sp.dma_start(dst, src).then_inc(weights_in, 16)
                if not first:
                    for i in range(2 * E):
                        e, up = i // 2, i % 2 == 0
                        if i >= 2:
                            sp.wait_ge(cast_done, i - 1)
                        n = KD * HIDP if up else HC * D
                        src = dram["m1_w_up" if up else "m1_w_dn"][e].rearrange("(k p) n -> p k n", p=P)
                        sp.dma_start(raw[:, i % 2, 0:n].rearrange("p (k n) -> p k n", k=KD if up else HC),
                                     src).then_inc(raw_in[i % 2], 16)
                else:
                    sp.wait_ge(weights_in, 16 * len(late))

            @block.tensor
            def _(pe):
                pe.wait_ge(loaded, 16 * len(loads))
                for b in range(B):
                    for k in range(KD):
                        u = KD * b + k
                        if u >= 2:
                            pe.wait_ge(ht_ready, u - 1)
                        for t in range(TT):
                            mm = pe.transpose(turned[:, u % 2, P * t:P * t + P], htok[:, TT * b + t, P * k:P * k + P],
                                              ident[:, :])
                        mm.then_inc(turned_filled, 1)
                    if b:
                        logits(pe, b - 1) if False else None
                pe.wait_ge(ht_ready, KD * B)
                for n in range(NT):
                    for k in range(KD):
                        mm = pe.matmul(small[:, E * n:E * n + E], hT[:, k, P * n:P * n + P], rw[:, k, :],
                                       start=(k == 0), stop=(k == KD - 1))
                mm.then_inc(logits_filled, 1)

                def shared_up(b):
                    for c in range(HC):
                        u = HC * b + c
                        if u >= 2:
                            pe.wait_ge(relu_ready, u - 1)
                        for k in range(KD):
                            mm = pe.matmul(shup[:, u % 2, :], s_up[:, k, P * c:P * c + P],
                                           hT[:, k, S * b:S * b + S], start=(k == 0), stop=(k == KD - 1))
                        mm.then_inc(up_filled, 1)

                def shared_down(b):
                    pe.wait_ge(hid_ready, HC * (b + 1))
                    for i in range(2):
                        u = 2 * b + i
                        if u >= 2:
                            pe.wait_ge(dn_read, u - 1)
                        for t in range(2):
                            for c in range(HC):
                                mm = pe.matmul(shdn[:, u % 2, D * t:D * t + D],
                                               hid[:, b % 2, c, P * (2 * i + t):P * (2 * i + t) + P],
                                               s_dn[:, c, :], start=(c == 0), stop=(c == HC - 1))
                        mm.then_inc(dn_filled, 1)

                if not first:
                    shared_up(0)
                pe.wait_ge(both_ready, 1)
                pe.wait_ge(ones_set, 1)
                flat = both[:, :, :].rearrange("p n e -> p (n e)")
                pe.matmul(places[:, 0:NT * E], before[:, :], flat, start=True, stop=False)
                for n in range(NT - 1):
                    rest = NT - 1 - n
                    pe.matmul(places[:, E * (n + 1):NT * E].rearrange("p (n e) -> p n e", e=E), ones[:, :],
                              spread(both[:, n:n + 1, :], [P, rest, E]), start=False, stop=(n == NT - 2))
                for n in range(NT):
                    mm = pe.matmul(counts, ones[:, :], both[:, n, :], start=(n == 0), stop=(n == NT - 1))
                mm.then_inc(places_filled, 1)
                if not first:
                    for b in range(B):
                        if b + 1 < B:
                            shared_up(b + 1)
                        shared_down(b)

            @block.scalar
            def _(act):
                for u in range(KD * B):
                    act.wait_ge(turned_filled, u + 1)
                    b, k = u // KD, u % KD
                    act.activation(hT[:, k, S * b:S * b + S], turned[:, u % 2, :], ACT.Copy).then_inc(ht_ready, 1)
                act.wait_ge(logits_ready, 1)
                act.activation(score[:, :, :].rearrange("p n e -> p (n e)"),
                               logit[:, :, :].rearrange("p n e -> p (n e)"),
                               ACT.Exp if first else ACT.Sigmoid).then_inc(exp_ready, 1)
                if not first:
                    def cast(i):
                        e, up = i // 2, i % 2 == 0
                        n = KD * HIDP if up else HC * D
                        act.wait_ge(raw_in[i % 2], 16 * (i // 2 + 1))
                        dst = (w_up if up else w_dn)[:, e, :, :].rearrange("p k n -> p (k n)")
                        act.activation(dst, raw[:, i % 2, 0:n], ACT.Copy).then_inc(cast_done, 1)

                    for u in range(HC * B):
                        b, c = u // HC, u % HC
                        act.wait_ge(up_filled, u + 1)
                        if b >= 2 and c == 0:
                            act.wait_ge(dn_filled, 2 * (b - 1))
                        act.activation(hid[:, b % 2, c, :], shup[:, u % 2, :], ACT.Relu).then_inc(relu_ready, 1)
                        cast(u)
                    for i in range(HC * B, 2 * E):
                        cast(i)

            @block.gpsimd
            def _(pool):
                pool.memset(ones[:, :], 1.0).then_inc(ones_set, 1)
                if not first:
                    for u in range(HC * B):
                        b, c = u // HC, u % HC
                        pool.wait_ge(relu_ready, u + 1)
                        pool.tensor_tensor(hid[:, b % 2, c, :], hid[:, b % 2, c, :], hid[:, b % 2, c, :],
                                           ALU.mult).then_inc(hid_ready, 1)
                pool.wait_ge(slots_ready, 1)
                pool.wait_ge(*env["slots_cleared"][layer])
                if not first:
                    pool.wait_ge(scaled_ready, 1)
                for n in range(NT):
                    for k in range(2):
                        src = htok[:, n, :] if first else scaled[:, n, k, :]
                        pool.indirect_dma_start(rows_in, bass.IndirectOffsetOnAxis(ap=slot[:, n, k:k + 1], axis=0),
                                                src, None).then_inc(sent, 16)
                pool.wait_ge(sent, 16 * 2 * NT)

            @block.vector
            def _(dve):
                chain = Chain(dve, dve_step)

                def then(ins):
                    chain.mark(ins)
                    chain.wait()

                def over_tiles(ap):
                    return spread(ap.rearrange("p (n e) -> p n e", n=1), [P, NT, E])

                def over_experts(ap, n=NT):
                    return spread(ap.rearrange("p (n e) -> p n e", e=1), [P, n, E])

                dve.wait_ge(loaded, 16 * len(loads))
                dve.wait_ge(logits_filled, 1)
                lg = small[:, 0:NT * E].rearrange("p (n e) -> p n e", e=E)
                if first:
                    then(dve.tensor_tensor(logit[:, :, :], lg, over_tiles(rb[:, :]), ALU.add))
                    then(dve.tensor_reduce(top[:, :], logit[:, :, :], AX_X, ALU.max))
                    dve.tensor_tensor(logit[:, :, :], logit[:, :, :], over_experts(top[:, :]),
                                      ALU.subtract).then_inc(logits_ready, 1)
                    dve.wait_ge(exp_ready, 1)
                    then(dve.tensor_reduce(total[:, :], score[:, :, :], AX_X, ALU.add))
                    then(dve.reciprocal(total[:, :], total[:, :]))
                    then(dve.tensor_tensor(score[:, :, :], score[:, :, :], over_experts(total[:, :]), ALU.mult))
                else:
                    dve.tensor_copy(logit[:, :, :], lg).then_inc(logits_ready, 1)
                    dve.wait_ge(exp_ready, 1)
                    then(dve.tensor_tensor(choice[:, :, :], score[:, :, :], over_tiles(rb[:, :]), ALU.add))
                for n in range(NT):
                    chain.mark(dve.max(max8[:, n, :], choice[:, n, :]))
                chain.wait()
                for n in range(NT):
                    chain.mark(dve.max_index(idx8[:, n, :], max8[:, n, :], choice[:, n, :]))
                chain.wait()
                for k in range(2):
                    chain.mark(dve.tensor_copy(idxf[:, k, :], idx8[:, :, k]))
                chain.wait()
                for k in range(2):
                    chain.mark(dve.tensor_tensor(pick[:, k, :, :], over_tiles(iota[:, 0:E]),
                                                 over_experts(idxf[:, k, :]), ALU.is_equal))
                chain.wait()
                dve.tensor_tensor(both[:, :, :], pick[:, 0, :, :], pick[:, 1, :, :], ALU.add).then_inc(both_ready, 1)
                for k in range(2):
                    chain.mark(dve.tensor_tensor(prod[:, k, :, :], pick[:, k, :, :], score[:, :, :], ALU.mult))
                chain.wait()
                for k in range(2):
                    chain.mark(dve.tensor_reduce(weight[:, :, k], prod[:, k, :, :], AX_X, ALU.add))
                chain.wait()
                dve.wait_ge(places_filled, 1)
                then(dve.tensor_scalar(count_i[:, :], counts, float(P - 1), None, ALU.add))
                then(dve.tensor_scalar(tiles_i[:, :], count_i[:, :], 7, None, ALU.logical_shift_right))
                then(dve.tensor_copy(tiles[:, :], tiles_i[:, :]))
                then(dve.tensor_tensor(tri[:, :, :], upto[:, :, :],
                                       spread(tiles[:, :].rearrange("p (a b) -> p a b", a=1), [P, E, E]), ALU.mult))
                then(dve.tensor_reduce(upto_e[:, :], tri[:, :, :], AX_X, ALU.add))
                then(dve.tensor_tensor(base[:, :], upto_e[:, :], tiles[:, :], ALU.subtract))
                then(dve.tensor_scalar(base[:, :], base[:, :], float(P), None, ALU.mult))
                then(dve.tensor_tensor(place[:, :, :], places[:, 0:NT * E].rearrange("p (n e) -> p n e", e=E),
                                       over_tiles(base[:, :]), ALU.add))
                for k in range(2):
                    chain.mark(dve.tensor_tensor(prod[:, k, :, :], pick[:, k, :, :], place[:, :, :], ALU.mult))
                chain.wait()
                for k in range(2):
                    chain.mark(dve.tensor_reduce(slotf[:, k, :], prod[:, k, :, :], AX_X, ALU.add))
                chain.wait()
                dve.tensor_copy(slot[:, :, :].rearrange("p n k -> p k n"), slotf[:, :, :]).then_inc(slots_ready, 1)
                if not first:
                    for n in range(NT):
                        for k in range(2):
                            last = dve.tensor_scalar(scaled[:, n, k, :], htok[:, n, :], weight[:, n, k:k + 1], None,
                                                     ALU.mult)
                    last.then_inc(scaled_ready, 1)
                then(dve.tensor_tensor(cmp[:, :, :],
                                       spread(upto_e[:, :].rearrange("p (n e) -> p n e", n=1), [P, NS, E]),
                                       over_experts(iota[:, :], NS), ALU.is_le))
                then(dve.tensor_reduce(expf[:, :], cmp[:, :, :], AX_X, ALU.add))
                then(dve.tensor_scalar(expert[:, :], expf[:, :], float(E - 1), None, ALU.min))
                if not first:
                    dve.wait_ge(scaled_ready, 1)
                    for u in range(2 * B):
                        dve.wait_ge(dn_filled, u + 1)
                        y = htok[:, 2 * u:2 * u + 2, :]
                        dve.tensor_tensor(y, y, shdn[:, u % 2, :].rearrange("p (i d) -> p i d", d=D),
                                          ALU.add).then_inc(dn_read, 1)

        with ExitStack() as ctx:
            def sb(name, shape, dt=F32):
                return ctx.enter_context(nc.sbuf_tensor(f"t{layer}_{name}", shape, dt))

            def ps(name, shape, dt=F32):
                return ctx.enter_context(nc.psum_tensor(f"t{layer}_{name}", shape, dt))

            sem = semaphores(nc, ctx, f"t{layer}_")

            (tiles_first if first else tiles_second)(nc, env, sb, ps, sem, ctx, dict(
                rows_in=rows_in, rows_out=rows_out, expert=expert, w_dn=w_dn,
                **(dict(w_gu=w_gu, b_gu=b_gu, b_dn=b_dn) if first else dict(w_up=w_up))))

        with ExitStack() as ctx:
            def sb(name, shape, dt=F32):
                return ctx.enter_context(nc.sbuf_tensor(f"c{layer}_{name}", shape, dt))

            sem = semaphores(nc, ctx, f"c{layer}_")

            got = sb("got", [P, NT, 2, D], XT)
            stats = sb("stats", [P, 6])
            mv = sb("mv", [P, NT, 2])
            veps = sb("veps", [P, NT])
            rstd = sb("rstd", [P, NT])
            half = sb("half", [P, NT])
            GRP = 4
            fetched = [sem(f"fetched{i}") for i in range(NT // GRP)]
            half_set = sem("half_set")
            pool_step = sem("pool_step")
            dve_step = sem("dve_step")
            stats_ready = sem("stats_ready")
            rstd_ready = sem("rstd_ready")
            normed = [sem(f"normed{i}") for i in range(2)]
            stored = sem("stored")
            block = ctx.enter_context(nc.Block())

            @block.gpsimd
            def _(pool):
                chain = Chain(pool, pool_step)
                pool.memset(half[:, :], -0.5).then_inc(half_set, 1)
                for n in range(NT):
                    for k in range(2):
                        pool.indirect_dma_start(got[:, n, k, :], None, rows_out,
                                                bass.IndirectOffsetOnAxis(ap=slot[:, n, k:k + 1], axis=0)
                                                ).then_inc(fetched[n // GRP], 16)
                pool.wait_ge(half_set, 1)
                pool.wait_ge(stats_ready, NT)
                layernorm_rows(pool, chain, mv, veps, rstd, half, rstd_ready)
                pool.wait_ge(rstd_ready, 1)
                for n in range(1, NT, 2):
                    pool.tensor_scalar(htok[:, n, :], htok[:, n, :], mv[:, n, 0:1], rstd[:, n:n + 1],
                                       ALU.subtract, ALU.mult).then_inc(normed[1], 1)

            @block.vector
            def _(dve):
                chain = Chain(dve, dve_step)
                for n in range(NT):
                    if n % GRP == 0:
                        dve.wait_ge(fetched[n // GRP], 16 * 2 * GRP)
                    y = htok[:, n, :]
                    for k in range(2):
                        if first:
                            chain.mark(dve.scalar_tensor_tensor(out=y, in0=got[:, n, k, :],
                                                                scalar=weight[:, n, k:k + 1], in1=y,
                                                                op0=ALU.mult, op1=ALU.add))
                        else:
                            chain.mark(dve.tensor_tensor(y, y, got[:, n, k, :], ALU.add))
                        chain.wait()
                    chain.mark(dve.bn_stats(stats[:, :], y))
                    chain.wait()
                    dve.bn_aggr(mv[:, n, :], stats[:, :]).then_inc(stats_ready, 1)
                    dve.wait_ge(stats_ready, n + 1)
                dve.wait_ge(rstd_ready, 1)
                for n in range(0, NT, 2):
                    dve.tensor_scalar(htok[:, n, :], htok[:, n, :], mv[:, n, 0:1], rstd[:, n:n + 1],
                                      ALU.subtract, ALU.mult).then_inc(normed[0], 1)

            if not first:
                @block.sync
                def _(sp):
                    out = dram["out"].rearrange("(t p) d -> p t d", p=P)
                    for n in range(0, NT, 4):
                        for s in normed:
                            sp.wait_ge(s, n // 2 + 2)
                        sp.dma_start(out[:, n:n + 4, :], htok[:, n:n + 4, :]).then_inc(stored, 16)
                    sp.wait_ge(stored, 16 * (NT // 4))


def in_steps(eng, first, last, step, unroll=2):
    turns = (last - first) // unroll
    if turns > 1:
        with eng.Fori(0, turns) as i:
            for d in range(unroll):
                step(i * unroll + (first + d), (first + d) % unroll)
    else:
        turns = 0
    for j in range(first + unroll * turns, last):
        step(j, j % unroll)


def tiles_first(nc, env, sb, ps, sem, ctx, t):
    ident, expert = env["ident"], t["expert"]
    KF = FI // P
    xin = sb("xin", [P, 2, D])
    xT = sb("xT", [P, 2, KD, P])
    g = sb("g", [P, 2, FI])
    u = sb("u", [P, 2, FI])
    sig = sb("sig", [P, 2, FI])
    act_t = sb("act", [P, 2, FI])
    aT = sb("aT", [P, 2, KF, P])
    y = sb("y", [P, 2, D])
    x_ps = ps("x_ps", [P, 2 * KD, P])
    g_ps = ps("g_ps", [P, 2, FI])
    u_ps = ps("u_ps", [P, 2, FI])
    a_ps = ps("a_ps", [P, KF, P])
    y_ps = ps("y_ps", [P, 2 * D])

    x_in = [sem(f"x_in{i}") for i in range(2)]
    x_turned = sem("x_turned")
    xT_ready = sem("xT_ready")
    g_filled = sem("g_filled")
    u_filled = sem("u_filled")
    g_ready = sem("g_ready")
    u_ready = sem("u_ready")
    g_min = sem("g_min")
    u_clip = sem("u_clip")
    sig_ready = sem("sig_ready")
    glu_ready = sem("glu_ready")
    a_ready = sem("a_ready")
    a_turned = sem("a_turned")
    aT_ready = sem("aT_ready")
    y_filled = sem("y_filled")
    y_ready = sem("y_ready")
    y_saved = [sem(f"y_saved{i}") for i in range(2)]
    block = ctx.enter_context(nc.Block())

    def of_expert(eng, j):
        return eng.value_load(expert[0:1, bass.ds(j, 1)], min_val=0, max_val=E - 1)

    @block.sync
    def _(sp):
        def rows(ap, j):
            return ap[bass.ds(j * P, P), :]

        def load(j, q):
            sp.dma_start(xin[:, q, :], rows(t["rows_in"], j)).then_inc(x_in[q], 16)

        def step(j, q):
            sp.wait_ge(x_turned, j - 1)
            load(j, q)

        load(0, 0)
        load(1, 1)
        in_steps(sp, 2, NS, step)
        for s in y_saved:
            sp.wait_ge(s, 16 * (NS // 2))

    @block.tensor
    def _(pe):
        def turn_x(j, q, early=False):
            pe.wait_ge(x_in[q], 8 * (j - q) + 16)
            if not early:
                pe.wait_ge(xT_ready, j)
            for k in range(KD):
                mm = pe.transpose(x_ps[:, k, :], xin[:, q, P * k:P * k + P], ident[:, :])
            mm.then_inc(x_turned, 1)

        def gate(j, q, early=False):
            e = of_expert(pe, j)
            pe.wait_ge(xT_ready, j + 1)
            if not early:
                pe.wait_ge(g_ready, j - 1)
            for k in range(KD):
                mm = pe.matmul(g_ps[:, q, :], xT[:, q, k, :],
                               t["w_gu"][:, k, bass.ds(e, 1), 0:FI].rearrange("p o n -> p (o n)"),
                               start=(k == 0), stop=(k == KD - 1))
            mm.then_inc(g_filled, 1)
            return e

        def up(j, q, e, early=False):
            if not early:
                pe.wait_ge(u_ready, j - 1)
            for k in range(KD):
                mm = pe.matmul(u_ps[:, q, :], xT[:, q, k, :],
                               t["w_gu"][:, k, bass.ds(e, 1), FI:2 * FI].rearrange("p o n -> p (o n)"),
                               start=(k == 0), stop=(k == KD - 1))
            mm.then_inc(u_filled, 1)

        def turn_a(j, q, early=False):
            pe.wait_ge(a_ready, j + 1)
            if not early:
                pe.wait_ge(aT_ready, j)
            for k in range(KF):
                mm = pe.transpose(a_ps[:, k, :], act_t[:, q, P * k:P * k + P], ident[:, :])
            mm.then_inc(a_turned, 1)

        def down(j, q, early=False):
            e = of_expert(pe, j)
            pe.wait_ge(aT_ready, j + 1)
            if not early:
                pe.wait_ge(y_ready, j)
            for k in range(KF):
                mm = pe.matmul(y_ps[:, 0:D], aT[:, q, k, :],
                               t["w_dn"][:, k, bass.ds(e, 1), :].rearrange("p o n -> p (o n)"),
                               start=(k == 0), stop=(k == KF - 1))
            mm.then_inc(y_filled, 1)

        def step(j, q):
            e = gate(j + 1, 1 - q)
            down(j - 1, 1 - q)
            up(j + 1, 1 - q, e)
            turn_a(j, q)
            turn_x(j + 2, q)

        turn_x(0, 0, True)
        turn_x(1, 1)
        up(0, 0, gate(0, 0, True), True)
        e = gate(1, 1, True)
        up(1, 1, e, True)
        turn_a(0, 0, True)
        turn_x(2, 0)
        for j in (1, 2):
            e = gate(j + 1, 1 - j % 2)
            down(j - 1, 1 - j % 2, j == 1)
            up(j + 1, 1 - j % 2, e)
            turn_a(j, j % 2)
            turn_x(j + 2, j % 2)
        in_steps(pe, 3, NS - 2, step)
        e = gate(NS - 1, 1)
        down(NS - 3, 1)
        up(NS - 1, 1, e)
        turn_a(NS - 2, 0)
        down(NS - 2, 0)
        turn_a(NS - 1, 1)
        down(NS - 1, 1)

    @block.scalar
    def _(act):
        def take_x(j, q):
            act.wait_ge(x_turned, j + 1)
            act.activation(xT[:, q, :, :], x_ps[:, 0:KD, :], ACT.Copy).then_inc(xT_ready, 1)

        def sigmoid(j, q):
            act.wait_ge(g_min, j + 1)
            act.activation(sig[:, q, :], g[:, q, :], ACT.Sigmoid, scale=1.702).then_inc(sig_ready, 1)

        def take_a(j, q):
            act.wait_ge(a_turned, j + 1)
            act.activation(aT[:, q, :, :], a_ps[:, :, :], ACT.Copy).then_inc(aT_ready, 1)

        def save(j, q):
            act.wait_ge(y_ready, j + 1)
            act.dma_start(t["rows_out"][bass.ds(j * P, P), :], y[:, q, :]).then_inc(y_saved[q], 16)

        def step(j, q):
            sigmoid(j, q)
            take_a(j - 1, 1 - q)
            take_x(j + 1, 1 - q)
            save(j - 3, 1 - q)

        take_x(0, 0)
        take_x(1, 1)
        sigmoid(0, 0)
        sigmoid(1, 1)
        take_a(0, 0)
        take_x(2, 0)
        sigmoid(2, 0)
        take_a(1, 1)
        take_x(3, 1)
        in_steps(act, 3, NS - 1, step)
        sigmoid(NS - 1, 1)
        take_a(NS - 2, 0)
        take_a(NS - 1, 1)
        for j in range(NS - 4, NS):
            save(j, j % 2)

    @block.gpsimd
    def _(pool):
        def step(j, q):
            pool.wait_ge(sig_ready, j + 1)
            pool.tensor_tensor(sig[:, q, :], sig[:, q, :], g[:, q, :], ALU.mult).then_inc(glu_ready, 1)

        in_steps(pool, 0, NS, step)

    @block.vector
    def _(dve):
        def hidden(j, q, early=False):
            e = of_expert(dve, j)
            dve.wait_ge(g_filled, j + 1)
            dve.tensor_tensor(g[:, q, :], g_ps[:, q, :],
                              t["b_gu"][:, bass.ds(e, 1), 0:FI].rearrange("p o n -> p (o n)"),
                              ALU.add).then_inc(g_ready, 1)
            dve.wait_ge(g_ready, j + 1)
            dve.tensor_scalar(g[:, q, :], g[:, q, :], LIMIT, None, ALU.min).then_inc(g_min, 1)
            dve.wait_ge(u_filled, j + 1)
            dve.tensor_tensor(u[:, q, :], u_ps[:, q, :],
                              t["b_gu"][:, bass.ds(e, 1), FI:2 * FI].rearrange("p o n -> p (o n)"),
                              ALU.add).then_inc(u_ready, 1)
            dve.wait_ge(u_ready, j + 1)
            dve.tensor_scalar(u[:, q, :], u[:, q, :], LIMIT, -LIMIT, ALU.min, ALU.max).then_inc(u_clip, 1)
            dve.wait_ge(u_clip, j + 1)
            dve.wait_ge(glu_ready, j + 1)
            if not early:
                dve.wait_ge(a_turned, j - 1)
            dve.scalar_tensor_tensor(out=act_t[:, q, :], in0=u[:, q, :], scalar=1.0, in1=sig[:, q, :],
                                     op0=ALU.add, op1=ALU.mult).then_inc(a_ready, 1)

        def result(j, q, early=False):
            e = of_expert(dve, j)
            dve.wait_ge(y_filled, j + 1)
            if not early:
                dve.wait_ge(y_saved[q], 8 * (j - q))
            dve.tensor_tensor(y[:, q, :], y_ps[:, 0:D],
                              t["b_dn"][:, bass.ds(e, 1), :].rearrange("p o n -> p (o n)"),
                              ALU.add).then_inc(y_ready, 1)

        def step(j, q):
            hidden(j, q)
            result(j - 2, q)

        hidden(0, 0, True)
        hidden(1, 1, True)
        for j in (2, 3):
            hidden(j, j % 2)
            result(j - 2, j % 2, True)
        in_steps(dve, 4, NS, step)
        result(NS - 2, 0)
        result(NS - 1, 1)


def tiles_second(nc, env, sb, ps, sem, ctx, t):
    expert, ident = t["expert"], env["ident_bf"]
    HC = HIDP // P
    DEEP = 4
    xin = sb("xin", [P, DEEP, D], BF16)
    xT = sb("xT", [P, 2, KD, P], BF16)
    h = sb("h", [P, 2, HC, P], BF16)
    hsq = sb("hsq", [P, 2, HC, P], BF16)
    y = sb("y", [P, DEEP, D], BF16)
    x_ps = [ps(f"x_ps{i}", [P, 2 * S], BF16) for i in range(2)]
    h_ps = [ps(f"h_ps{i}", [P, 512]) for i in range(2)]
    y_ps = [ps(f"y_ps{i}", [P, 512]) for i in range(2)]
    x_in = [sem(f"x_in{i}") for i in range(DEEP)]
    x_turned = sem("x_turned")
    xT_ready = sem("xT_ready")
    h_filled = sem("h_filled")
    h_ready = sem("h_ready")
    hsq_ready = sem("hsq_ready")
    y_filled = sem("y_filled")
    y_ready = sem("y_ready")
    y_saved = [sem(f"y_saved{i}") for i in range(DEEP)]
    block = ctx.enter_context(nc.Block())

    @block.sync
    def _(sp):
        def rows(ap, j):
            return ap[bass.ds(j * P, P), :]

        def load(j, q):
            sp.dma_start(xin[:, q, :], rows(t["rows_in"], j)).then_inc(x_in[q], 16)

        def step(j, q):
            sp.wait_ge(x_turned, j - DEEP + 1)
            load(j, q)

        for j in range(DEEP):
            load(j, j)
        in_steps(sp, DEEP, NS, step, DEEP)
        for s in y_saved:
            sp.wait_ge(s, 16 * (NS // DEEP))

    @block.tensor
    def _(pe):
        def turn_x(j, q, early=False):
            pe.wait_ge(x_in[q], 16 // DEEP * (j - q) + 16)
            if not early:
                pe.wait_ge(xT_ready, j - 1)
            for k in range(KD):
                mm = pe.transpose(x_ps[q % 2][:, P * k:P * k + P], xin[:, q, P * k:P * k + P], ident[:, :])
            mm.then_inc(x_turned, 1)

        def up(j, q, early=False):
            e = pe.value_load(expert[0:1, bass.ds(j, 1)], min_val=0, max_val=E - 1)
            pe.wait_ge(xT_ready, j + 1)
            if not early:
                pe.wait_ge(h_ready, j - 1)
            for c in range(HC):
                for k in range(KD):
                    mm = pe.matmul(h_ps[q % 2][:, P * c:P * c + P],
                                   t["w_up"][:, bass.ds(e, 1), k, P * c:P * c + P].rearrange("p o n -> p (o n)"),
                                   xT[:, q % 2, k, :], start=(k == 0), stop=(k == KD - 1))
            mm.then_inc(h_filled, 1)
            return e

        def down(j, q, early=False):
            e = pe.value_load(expert[0:1, bass.ds(j, 1)], min_val=0, max_val=E - 1)
            pe.wait_ge(hsq_ready, j + 1)
            if not early:
                pe.wait_ge(y_ready, j - 1)
            for c in range(HC):
                mm = pe.matmul(y_ps[q % 2][:, 0:D], hsq[:, q % 2, c, :],
                               t["w_dn"][:, bass.ds(e, 1), c, :].rearrange("p o n -> p (o n)"),
                               start=(c == 0), stop=(c == HC - 1))
            mm.then_inc(y_filled, 1)

        def step(j, q):
            turn_x(j + 2, (q + 2) % DEEP)
            up(j + 1, (q + 1) % DEEP)
            down(j, q)

        turn_x(0, 0, True)
        turn_x(1, 1, True)
        up(0, 0, True)
        turn_x(2, 2)
        up(1, 1, True)
        down(0, 0, True)
        turn_x(3, 3)
        up(2, 2)
        down(1, 1, True)
        in_steps(pe, 2, NS - 2, step, DEEP)
        up(NS - 1, DEEP - 1)
        down(NS - 2, DEEP - 2)
        down(NS - 1, DEEP - 1)

    @block.scalar
    def _(act):
        def take_x(j, q):
            act.wait_ge(x_turned, j + 1)
            act.activation(xT[:, q % 2, :, :], x_ps[q % 2][:, 0:D].rearrange("p (k n) -> p k n", k=KD), ACT.Copy).then_inc(xT_ready, 1)

        def relu(j, q, early=False):
            act.wait_ge(h_filled, j + 1)
            if not early:
                act.wait_ge(hsq_ready, j - 1)
            act.activation(h[:, q % 2, :, :].rearrange("p c n -> p (c n)"), h_ps[q % 2][:, 0:HIDP],
                           ACT.Relu).then_inc(h_ready, 1)

        def save(j, q):
            act.wait_ge(y_ready, j + 1)
            act.dma_start(t["rows_out"][bass.ds(j * P, P), :], y[:, q, :]).then_inc(y_saved[q], 16)

        def step(j, q):
            take_x(j, q)
            relu(j - 1, (q - 1) % DEEP)
            save(j - 3, (q - 3) % DEEP)

        take_x(0, 0)
        take_x(1, 1)
        relu(0, 0, True)
        take_x(2, 2)
        relu(1, 1, True)
        in_steps(act, 3, NS, step, DEEP)
        relu(NS - 1, DEEP - 1)
        for j in range(NS - 3, NS):
            save(j, j % DEEP)

    @block.gpsimd
    def _(pool):
        def square(j, q, early=False):
            pool.wait_ge(h_ready, j + 1)
            if not early:
                pool.wait_ge(y_filled, j - 1)
            pool.tensor_tensor(hsq[:, q % 2, :, :], h[:, q % 2, :, :], h[:, q % 2, :, :], ALU.mult).then_inc(hsq_ready, 1)

        square(0, 0, True)
        square(1, 1, True)
        in_steps(pool, 2, NS, square, DEEP)

    @block.vector
    def _(dve):
        def result(j, q, early=False):
            dve.wait_ge(y_filled, j + 1)
            if not early:
                dve.wait_ge(y_saved[q], 16 // DEEP * (j - q))
            dve.tensor_copy(y[:, q, :], y_ps[q % 2][:, 0:D]).then_inc(y_ready, 1)

        for j in range(DEEP):
            result(j, j, True)
        in_steps(dve, DEEP, NS, result, DEEP)


def rope_tables():
    inv = (1.0 / np.float32(10000.0) ** (np.arange(0, HD, 2, dtype=np.float32) / np.float32(HD))).astype(np.float32)
    angle = np.arange(S, dtype=np.float32)[:, None] * inv[None, :]
    gamma = 1.0 - 2.0 ** (-5.0 - np.arange(H))
    power = gamma[None, :] ** np.arange(S)[:, None]
    scale = np.concatenate([power, HD ** -0.5 / power], 1)
    return [(scale[:, :, None] * f(angle).astype(np.float32)[:, None, :]).astype(np.float32).reshape(S, 32 * 8)
            for f in (np.cos, np.sin)]


def vit_tower(nc, dram):
    with ExitStack() as ctx:
        htok = ctx.enter_context(nc.sbuf_tensor("htok", [P, NT, D], F32))
        ident = ctx.enter_context(nc.sbuf_tensor("ident", [P, P], F32))
        ident_bf = ctx.enter_context(nc.sbuf_tensor("ident_bf", [P, P], BF16))
        zeros = ctx.enter_context(nc.sbuf_tensor("zeros", [P, ZCOLS], F32))
        tables_in = ctx.enter_context(nc.semaphore("tables_in"))
        tables_cast = ctx.enter_context(nc.semaphore("tables_cast"))
        cleared = [ctx.enter_context(nc.semaphore(f"cleared{i}")) for i in range(2)]

        def clear_slots(sp):
            for layer, dt in ((0, F32), (1, BF16)):
                per = ZCOLS * (1 if layer == 0 else 2)
                flat = dram[f"slots{layer}"].rearrange("(p r) d -> p (r d)", p=P)
                src = zeros[:, :] if layer == 0 else zeros[:, :].bitcast(BF16)
                for c in range(NS * D // per):
                    sp.dma_start(flat[:, c * per:(c + 1) * per], src).then_inc(cleared[layer], 16)

        env = dict(htok=htok, ident=ident, ident_bf=ident_bf, ret_dmas=(clear_slots,),
                   slots_cleared=[(cleared[0], 16 * (NS * D // ZCOLS)), (cleared[1], 16 * (NS * D // (2 * ZCOLS)))])
        with nc.Block() as block:
            @block.sync
            def _(sp):
                sp.dma_start(ident[:, :], dram["ident"]).then_inc(tables_in, 16)

            @block.vector
            def _(dve):
                dve.memset(zeros[:, :], 0.0).then_inc(tables_cast, 1)
                dve.wait_ge(tables_in, 16)
                dve.tensor_copy(ident_bf[:, :], ident[:, :]).then_inc(tables_cast, 1)

        attention(nc, "tok", env, dram)
        attention(nc, "ret", env, dram)
        moe(nc, 0, env, dram)
        attention(nc, "rms", env, dram)
        moe(nc, 1, env, dram)


def kernel(**inputs):
    import numpy as _np
    import concourse.bacc as _bacc
    from concourse import mybir as _mybir
    from concourse.bass_utils import run_bass_kernel_spmd as _run

    I = {k: _np.asarray(a) for k, a in inputs.items()}
    w_qkv = I["L0_tok_w_qkv"].reshape(H, 3, HD, D).transpose(1, 0, 2, 3).reshape(3 * D, D).T
    b_qkv = I["L0_tok_b_qkv"].reshape(H, 3, HD).transpose(1, 0, 2).reshape(3 * D)
    cos, sin = rope_tables()

    def wide(a, axis):
        pad = [(0, 0)] * a.ndim
        pad[axis] = (0, HIDP - HID)
        return _np.pad(a, pad)

    arrays = {
        "x": I["x"].reshape(B * S, D).T,
        "tok_w_in": w_qkv,
        "tok_b_qk": b_qkv[:2 * D].reshape(4, P).T,
        "tok_b_v": b_qkv[2 * D:],
        "tok_w_o": I["L0_tok_w_out"].T,
        "tok_b_o": I["L0_tok_b_out"],
        "ret_w_in": _np.concatenate([I["L0_attn_wq"].T, I["L0_attn_wk"].T, I["L0_attn_wv"].T, I["L0_attn_wg"].T], 1),
        "ret_w_o": I["L0_attn_wo"].T,
        "r0_w": I["L0_ffn_router_weight"].T,
        "r0_b": I["L0_ffn_router_bias"],
        "m0_w_gu": I["L0_ffn_gate_up_proj"],
        "m0_w_dn": I["L0_ffn_down_proj"],
        "m0_b_gu": I["L0_ffn_gate_up_bias"],
        "m0_b_dn": I["L0_ffn_down_bias"],
        "rms_w_in": _np.concatenate([I["L1_attn_Wq"][:, :D], I["L1_attn_Wk"], I["L1_attn_Wv"], I["L1_attn_Wq"][:, D:]], 1),
        "rms_b_in": _np.concatenate([I["L1_attn_bq"][:D], I["L1_attn_bk"], I["L1_attn_bv"], I["L1_attn_bq"][D:]]),
        "rms_norm_w": _np.tile(_np.stack([I["L1_attn_qn_w"], I["L1_attn_kn_w"]], 1), (P // HD, 1)),
        "rms_w_o": I["L1_attn_Wo"],
        "rms_b_o": I["L1_attn_bo"],
        "r1_w": I["L1_ffn_gate_w"].T,
        "r1_b": I["L1_ffn_expert_bias"],
        "m1_w_up": wide(I["L1_ffn_w_up"].transpose(0, 2, 1), 2),
        "m1_w_dn": wide(I["L1_ffn_w_down"].transpose(0, 2, 1), 1),
        "s_up": wide(I["L1_ffn_shared_w_up"].T, 1),
        "s_dn": wide(I["L1_ffn_shared_w_down"].T, 0),
        "cos": cos,
        "sin": sin,
        "causal": _np.triu(_np.ones((P, P), _np.float32)),
        "ident": _np.eye(P, dtype=_np.float32),
        "iota": _np.arange(NS, dtype=_np.float32),
        "before": _np.triu(_np.ones((P, P), _np.float32), 1),
        "upto": _np.tril(_np.ones((E, E), _np.float32)).reshape(E * E),
    }
    nc = _bacc.Bacc("TRN2", target_bir_lowering=False, num_devices=1)
    arrays = {f"in_{k}": _np.ascontiguousarray(a) for k, a in arrays.items()}
    dram = {k[3:]: nc.dram_tensor(k, a.shape, _mybir.dt.from_np(a.dtype), kind="ExternalInput").ap()
            for k, a in arrays.items()}
    dram["out"] = nc.dram_tensor("out_0", (B * S, D), F32, kind="ExternalOutput").ap()
    dram["scratch"] = nc.dram_tensor("scratch", (B, 2, SK, H, S), BF16, kind="Internal").ap()
    for layer, dt in ((0, F32), (1, BF16)):
        dram[f"slots{layer}"] = nc.dram_tensor(f"slots{layer}", (NS * P, D), dt, kind="Internal").ap()
        dram[f"results{layer}"] = nc.dram_tensor(f"results{layer}", (NS * P, D), dt, kind="Internal").ap()
    vit_tower(nc, dram)
    r = _run(nc, [arrays], core_ids=[0])
    return r.results[0]["out_0"].reshape(B, S, D)
```

```python
from contextlib import ExitStack

import numpy as np

import concourse.bass as bass
from concourse import mybir

F32 = mybir.dt.float32
BF16 = mybir.dt.bfloat16
I32 = mybir.dt.int32
U32 = mybir.dt.uint32
ALU = mybir.AluOpType
ACT = mybir.ActivationFunctionType
AX_X = mybir.AxisListType.X

P = 128
B = 4
S = 512
D = 256
H = 16
HD = D // H
KD = D // P
TT = S // P
NT = B * TT
HG = H // 4
Q_PART = (0, 0, 0, 1, 1, 2)
K_PART = (0, 1, 2, 0, 1, 0)
SK = HD * len(Q_PART)
E = 8
FI = 512
LIMIT = 7.0
HID = 352
HIDP = 384
NU = (2 * B * S + E * (P - 1)) // P
NS = NU + NU % 2
NI = 4 * -(-NU // 4) + 4
RING = 3
LEAD = 11
ZCOLS = 1024
PROJECTED = {"tok": 3 * D, "ret": 4 * D, "rms": 3 * D + H}
LN_EPS = 1e-5
RMS_EPS = 1e-6


class Chain:

    def __init__(self, eng, sem):
        self.eng, self.sem, self.n = eng, sem, 0

    def mark(self, ins):
        ins.then_inc(self.sem, 1)
        self.n += 1
        return self.n

    def wait(self, n=None):
        self.eng.wait_ge(self.sem, self.n if n is None else n)


def semaphores(nc, ctx, prefix):
    taken = []

    def sem(name):
        taken.append(nc.alloc_semaphore(prefix + name))
        return taken[-1]

    def give_back():
        nc.clear_and_free_semaphores(taken)
        nc.all_engine_barrier()

    ctx.callback(give_back)
    return sem


def spread(ap, shape):
    return ap.broadcast_to(shape)


def attention_order(kind):
    softmax = kind != "ret"
    if kind == "tok":
        prepare = [(3, "qk", 0), (5, "qk", 2), (7, "qk", 1), (9, "qk", 3)]
    elif kind == "ret":
        prepare = [(0, "turn_h", 0), (0, "turn_h", 1)] + [(1 + t, "rows", t) for t in range(TT)]
        prepare += [(6 + i, "qk", f) for i, f in enumerate((0, 2, 1, 3))]
    else:
        prepare = [(t, "combine", t) for t in range(TT)] + [(4, "deviation_in", 0)]
        prepare += [(5 + t // 2, "normalise_in", t) for t in range(TT)] + [(7, "fetch", t) for t in range(TT)]
        prepare += [(7, "turn_h", 0), (7, "turn_h", 1)] + [(8 + t, "rows", t) for t in range(TT)]
        prepare += [(9 + t, "square", t) for t in range(TT)] + [(12, "root", 0)]
        prepare += [(13, "invert", 0)] + [(13, "norm", t) for t in range(TT)]
        prepare += [(15 + i, "qk", f) for i, f in enumerate((0, 2, 1, 3))]
    prepare += [(h + 1, "split", f) for h, what, f in prepare if what == "qk"]
    prepare = sorted(prepare, key=lambda x: (x[0], x[1] != "split"))
    length = prepare[-1][0] + 1
    finish = [(2 + t, "turn_o", t) for t in range(TT)] + [(7 + k, "turn_back", k) for k in range(KD)]
    if kind == "rms":
        finish += [(8 + u, "add_bias", u) for u in range(2)]
    finish += [(10 + u, "project_o", u) for u in range(2)]
    if kind != "tok":
        finish += [(12 + t // 2, "stats", t) for t in range(TT)] + [(14, "deviation", 0)]
        finish += [(15 + t // 2, "layernorm", t) for t in range(TT)]
        finish += [(17, "turn_r", k) for k in range(KD)] + [(18, "route", 0)]
    lead = LEAD if softmax else 0
    ahead = 2 if softmax else 1

    items = [("fetch", -1, t) for t in range(TT)] if kind == "rms" else []
    items += [(what, 0, i) for _, what, i in prepare]
    if not softmax:
        items += [("values_in", 0, t) for t in range(TT)]
    for u in range(-lead, B * H):
        b, h = u // H, u % H
        score = [("scores", b, 2 * h + p) for p in range(2)] if u >= 0 else []
        row_max = []
        if softmax and u + lead < B * H:
            bb_max, hh = (u + lead) // H, (u + lead) % H
            row_max = [("row_max", bb_max, TT * hh + t) for t in range(TT)]
        fill = [("values_in", 0, t) for t in (2 * u + 4, 2 * u + 5)] if u in (-2, -1) else []
        if b > 0:
            fill += [(what, bb, i) for bb in (b - 2, b - 1) for at, what, i in finish
                     if bb >= 0 and at == h + H * (b - 1 - bb)]
        if u >= 4 and h % 4 < 2:
            g = u // 4 - 1
            fill += [("values", g // HG, TT * (g % HG) + 2 * (h % 4) + i) for i in range(2)]
        if b > 0 and h in (1, 2):
            fill += [("values_in", b, t) for t in (2 * h - 2, 2 * h - 1)]
        if u < 0:
            fill += [(what, 1, i) for at, what, i in prepare if at * lead // length == u + lead]
        fill += [(what, bb, i) for bb in range(ahead, B) for at, what, i in prepare if at == u - H * (bb - ahead)]
        gaps = [[], [], [], []]
        for n, x in enumerate(fill):
            gaps[int((n + 0.5) * 4 / len(fill))].append(x)
        items += score[0:1] + row_max[0:1] + gaps[0] + score[1:2] + row_max[1:2] + gaps[1]
        items += row_max[2:3] + gaps[2] + row_max[3:4] + gaps[3]
        if row_max and hh % 8 == 7:
            items.append(("turn_max", bb_max, hh // 8))
    items += [("values", B - 1, TT * (HG - 1) + i) for i in range(TT)]
    items += [(what, B - 2, i) for at, what, i in finish if at >= H]
    items += [(what, B - 1, i) for _, what, i in finish]
    return items


def attention_weights(nc, kind, ctx, dram, sem):
    w = {}

    def room(name, shape, src):
        t = ctx.enter_context(nc.sbuf_tensor(f"{kind}_{name}", shape, F32))
        w[name] = t
        return t[tuple(slice(None) for _ in shape)], src

    nw = PROJECTED[kind]
    w["first"] = [room("w_in", [P, KD, nw], dram[f"{kind}_w_in"].rearrange("(k p) n -> p k n", p=P))]
    w["rest"] = [room("w_o", [P, KD, D], dram[f"{kind}_w_o"].rearrange("(k p) n -> p k n", p=P))]
    if kind == "tok":
        w["first"].append(room("bias_qk", [P, 4], dram["tok_b_qk"]))
        w["rest"].append(room("bias_v", [P, D], dram["tok_b_v"].partition_broadcast(P)))
    if kind == "rms":
        w["first"] += [room("bias_in", [P, nw], dram["rms_b_in"].partition_broadcast(P)),
                       room("norm_w", [P, 2], dram["rms_norm_w"])]
    if kind == "ret":
        w["first"] += [room(x, [P, TT, 32 * 8], dram[x].rearrange("(t p) r -> p t r", p=P)) for x in ("cos", "sin")]
        w["rest"].append(room("causal", [P, P], dram["causal"]))
    else:
        w["rest"].append(room("bias_o", [P, D], dram[f"{kind}_b_o"].partition_broadcast(P)))
    if kind != "tok":
        w["rest"].append(room("router", [P, KD, E], dram[f"{kind}_router"].rearrange("(k p) e -> p k e", p=P)))
    w["first_in"], w["rest_in"] = sem("first_in"), sem("rest_in")
    return w


def load_weights(eng, w, which):
    for dst, src in w[which]:
        eng.dma_start(dst, src).then_inc(w[f"{which}_in"], 16)


def attention(nc, kind, env, dram):
    tok, ret, rmsn = kind == "tok", kind == "ret", kind == "rms"
    softmax = not ret
    htok, ident = env["htok"], env["ident"]
    scratch = dram["scratch"]
    NW = PROJECTED[kind]
    WV = NW - 512
    P_SLOTS = 6
    PCOLS = TT * S if softmax else TT * S - P * (1 + 2 + 3)
    order = attention_order(kind)

    ring_items = [x for x in order if x[0] in ("turn_h", "rows", "qk", "row_max", "turn_max", "values_in", "turn_o",
                                               "turn_back", "project_o", "turn_r", "route")]
    ring_at = {use: n for n, use in enumerate(ring_items)}
    counts = {}
    nth = {}
    for x in order:
        nth[x] = counts.get(x[0], 0)
        counts[x[0]] = nth[x] + 1

    with ExitStack() as ctx:
        def sb(name, shape, dt=F32):
            return ctx.enter_context(nc.sbuf_tensor(f"{kind}_{name}", shape, dt))

        def ps(name, shape, dt=F32):
            return ctx.enter_context(nc.psum_tensor(f"{kind}_{name}", shape, dt))

        sem = semaphores(nc, ctx, f"{kind}_")

        w = env[f"{kind}_weights"] if f"{kind}_weights" in env else attention_weights(nc, kind, ctx, dram, sem)
        w_in, w_o = w["w_in"], w["w_o"]
        if softmax:
            bias_o = w["bias_o"]
            rowmax = sb("rowmax", [P, H * TT])
            negm = sb("negm", [H * TT // 2, 2, P])
            mparts = sb("mparts", [H * TT // 2, 3, P], BF16)
            rden = sb("rden", [P, TT, H])
        if tok:
            bias_qk, bias_v = w["bias_qk"], w["bias_v"]
        if rmsn:
            bias_in, norm_w = w["bias_in"], w["norm_w"]
            ssq = sb("ssq", [P, TT, 32])
            rms = sb("rms", [P, 2, TT, 32])
            eps = sb("eps", [P, 1])
            squares = sb("squares", [P, S])
            gate = sb("gate", [P, 2, TT, H])
            graw = sb("graw", [P, H])
        if ret:
            causal, cos, sin = w["causal"], w["cos"], w["sin"]
            gate = sb("gate", [P, 2, TT, D])
            xcos = sb("xcos", [P, S])
            xsin = sb("xsin", [P, S])
        if not tok:
            router = w["router"]
            stats = sb("stats", [P, 6])
            if rmsn:
                back = env["experts_rows"]
                got = sb("got", [P, TT, 2, D])
                mv_in = sb("mv_in", [P, TT, 2])
                rstd_in = sb("rstd_in", [P, TT])
            mv = sb("mv", [P, NT, 2])
            rstd = sb("rstd", [P, NT])
            half = sb("half", [P, NT])
            rot = sb("rot", [P, TT, S])
        ht = sb("ht", [P, 2, KD, S])
        left = sb("left", [P, 2, S])
        parts = sb("parts", [P, 2, 3, S], BF16)
        qs = sb("qs", [SK + 3, 2, H, S], BF16)
        ks = sb("ks", [SK + 3, 2, H, S], BF16)
        v = sb("v", [P, TT, H, 32])
        prob = sb("prob", [P, P_SLOTS, PCOLS])
        ot = sb("ot", [P, HG, S])
        otok = sb("otok", [P, TT, D])
        ot2 = sb("ot2", [P, KD, S])

        ring = ps("ring", [P, RING, S])
        score = ps("score", [P, 2, 2, S])
        valps = ps("valps", [P, S])

        first_in = w["first_in"], 16 * len(w["first"])
        rest_in = w["rest_in"], 16 * len(w["rest"])
        x_in = [sem(f"x_in{i}") for i in range(2)]
        fetched = [sem(f"fetched{t}") for t in range(TT)] if rmsn else []
        bias_added = sem("bias_added")
        combined = sem("combined")
        rstd_in_ready = sem("rstd_in_ready")
        rows_in = sem("rows_in")
        ones_set = sem("ones_set")
        half_set = sem("half_set")
        key_ones = sem("key_ones")
        ring_filled = sem("ring_filled")
        ht_ready = sem("ht_ready")
        rows_ready = sem("rows_ready")
        squares_ready = sem("squares_ready")
        ssq_ready = sem("ssq_ready")
        inverse_ready = sem("inverse_ready")
        roots_ready = sem("roots_ready")
        rot_ready = sem("rot_ready")
        part0_ready = sem("part0_ready")
        left_ready = sem("left_ready")
        part1_ready = sem("part1_ready")
        parts_ready = sem("parts_ready")
        parts_saved = [sem(f"parts_saved{i}") for i in range(2)]
        stacked = [sem(f"stacked{i}") for i in range(4)]
        max_done = sem("max_done")
        negm_ready = sem("negm_ready")
        mparts_ready = sem("mparts_ready")
        maxrows_in = [sem(f"maxrows_in{i}") for i in range(2)]
        score_filled = sem("score_filled")
        prob_ready = sem("prob_ready")
        prob_diag = sem("prob_diag")
        v_ready = sem("v_ready")
        graw_ready = sem("graw_ready")
        gexp_ready = sem("gexp_ready")
        gate_ready = sem("gate_ready")
        val_filled = sem("val_filled")
        ot_ready = sem("ot_ready")
        rden_step = sem("rden_step")
        otok_ready = sem("otok_ready")
        ot2_ready = sem("ot2_ready")
        y_ready = sem("y_ready")
        stats_ready = sem("stats_ready")
        normed = sem("normed")
        router_turned = sem("router_turned")
        logits_ready = sem("logits_ready")
        rstd_ready = sem("rstd_ready")
        pool_step = sem("pool_step")
        dve_step = sem("dve_step")

        def ring_release(use):
            what = use[0]
            n = nth[use]
            if what == "values_in":
                return (graw_ready if rmsn else gate_ready if ret else v_ready), n + 1
            return {"turn_h": ht_ready, "rows": rows_ready, "qk": left_ready, "row_max": max_done,
                    "turn_max": negm_ready, "turn_o": otok_ready, "turn_back": ot2_ready, "project_o": y_ready,
                    "turn_r": router_turned, "route": logits_ready}[what], n + 1

        def ring_view(what, b, i):
            n = ring_at[what, b, i]
            return ring[:, n % RING, :], n + 1

        def stack_ready(b, h):
            return stacked[2 * (b % 2) + h // 8], 32 * (b // 2 + 1)

        DIAG = [(kt, kt, 1, P * kt) for kt in range(TT)]
        OFF = [(0, 1, 3, 0), (2, 3, 1, 3 * P), (1, 2, 2, 0)]

        block = ctx.enter_context(nc.Block())

        @block.sync
        def _(sp):
            def load_x(b):
                if b >= 2:
                    sp.wait_ge(ring_filled, ring_at["values_in", b - 2, TT - 1] + 1)
                sp.dma_start(ht[:, b % 2, :, :],
                             dram["x"].rearrange("(k p) n -> p k n", p=P)[:, :, b * S:(b + 1) * S]).then_inc(x_in[b % 2], 16)

            def save_parts(b, f):
                n = nth["split", b, f]
                heads = slice(8 * (f % 2), 8 * (f % 2) + 8)
                sp.wait_ge(parts_ready, n + 1)
                for g, part in enumerate(K_PART if f // 2 else Q_PART):
                    sp.dma_start(scratch[b, f // 2, HD * g:HD * g + HD, heads, :].rearrange("d h n -> h d n"),
                                 parts[:, n % 2, part, :]).then_inc(parts_saved[n % 2], 16)

            def stack(b, f):
                n = nth["split", b, f]
                heads = slice(8 * (f % 2), 8 * (f % 2) + 8)
                sp.wait_ge(parts_saved[n % 2], 96 * (n // 2 + 1))
                if b >= 2:
                    sp.wait_ge(score_filled, 2 * (H * (b - 2) + 8 * (f % 2) + 8))
                sp.dma_start((ks if f // 2 else qs)[0:SK, b % 2, heads, :].rearrange("p h n -> p (h n)"),
                             scratch[b, f // 2, :, heads, :].rearrange("p h n -> p (h n)")
                             ).then_inc(stacked[2 * (b % 2) + f % 2], 16)

            def max_rows(b, i):
                sp.wait_ge(mparts_ready, 2 * b + i + 1)
                for j in range(3):
                    sp.dma_start(qs[SK + j:SK + j + 1, b % 2, 8 * i:8 * i + 8, :].rearrange("o h (t q) -> o (h t) q", q=P),
                                 mparts[:, j, :]).then_inc(maxrows_in[i], 16)

            ours = f"{kind}_weights" not in env
            if ours:
                load_weights(sp, w, "first")
            if tok:
                load_x(0)
                load_x(1)
            if ours:
                load_weights(sp, w, "rest")

            spare = list(env.get(f"{kind}_spare", ()))
            assert len(spare) <= B * H
            begun = set()
            late = []
            for what, b, i in order:
                if what == "scores" and i % 2 and spare:
                    sp.wait_ge(score_filled, nth[what, b, i] + 1)
                    dst, src, landed = spare.pop(0)
                    sp.dma_start(dst, src).then_inc(landed, 16)
                if what == "values_in" and tok and i == TT - 1 and b + 2 < B:
                    load_x(b + 2)
                if what == "split":
                    save_parts(b, i)
                    if i == 2:
                        stack(b, 0)
                        stack(b, 2)
                    if i == 3:
                        if b < 2 or b - 1 in begun:
                            stack(b, 1)
                            stack(b, 3)
                        else:
                            late.append(b)
                if what == "turn_max":
                    max_rows(b, i)
                if what == "scores" and i == 0:
                    begun.add(b)
                    for bb in late:
                        stack(bb, 1)
                        stack(bb, 3)
                    late = []

        @block.gpsimd
        def _(pool):
            chain = Chain(pool, pool_step)
            pool.memset(v[:, :, :, HD:32], 1.0).then_inc(ones_set, 1)
            if rmsn:
                pool.memset(eps[:, :], RMS_EPS).then_inc(half_set, 1)
            if not tok:
                pool.memset(half[:, :], -0.5).then_inc(half_set, 1)
                pool.wait_ge(half_set, 2 if rmsn else 1)
            for what, b, i in order:
                n = nth[what, b, i]
                if what == "norm":
                    pool.wait_ge(inverse_ready, b + 1)
                    x = rot[:, i, :].rearrange("p (h d) -> p h d", d=HD)
                    r = spread(rms[:, 1, i, :].rearrange("p (a o) -> p a o", o=1), [P, 32, HD])
                    pool.tensor_tensor(x, x, r, ALU.mult).then_inc(rot_ready, 1)
                if what == "fetch" and b + 1 < B:
                    if b >= 0:
                        pool.wait_ge(combined, TT * b + i + 1)
                    for k in range(2):
                        pool.indirect_dma_start(
                            got[:, i, k, :], None, back["rows"],
                            bass.IndirectOffsetOnAxis(ap=back["slot"][:, TT * (b + 1) + i, k:k + 1], axis=0)
                        ).then_inc(fetched[i], 16)
                if what == "deviation_in":
                    pool.wait_ge(combined, TT * (b + 1))
                    if b:
                        pool.wait_ge(rows_in, TT * b)
                    chain.mark(pool.tensor_scalar(rstd_in[:, :], mv_in[:, :, 1], 1.0, LN_EPS, ALU.mult, ALU.add))
                    chain.wait()
                    pool.tensor_tensor(rstd_in[:, :], rstd_in[:, :], half[:, 0:TT], ALU.pow).then_inc(rstd_in_ready, 1)
                if what == "rows" and ret:
                    pool.wait_ge(rows_ready, n + 1)
                    if i == 0 and b:
                        pool.wait_ge(ring_filled, ring_at["qk", b - 1, 3] + 1)
                    halves = lambda a: a.rearrange("p (h s r) -> p h s r", s=2, r=8)
                    a, z, r = halves(xcos[:, :]), halves(xsin[:, :]), halves(rot[:, i, :])
                    chain.mark(pool.tensor_tensor(r[:, :, 0, :], a[:, :, 0, :], z[:, :, 1, :], ALU.subtract))
                    pool.tensor_tensor(r[:, :, 1, :], a[:, :, 1, :], z[:, :, 0, :], ALU.add).then_inc(rot_ready, 1)
                    chain.wait()
                    pool.wait_ge(rot_ready, n + 1)
                if what == "split":
                    pool.wait_ge(part1_ready, n + 1)
                    pool.tensor_tensor(parts[:, n % 2, 2, :], left[:, n % 2, :], parts[:, n % 2, 1, :],
                                       ALU.subtract).then_inc(parts_ready, 1)
                if what == "turn_max":
                    pool.wait_ge(negm_ready, n + 1)
                    if n:
                        pool.wait_ge(maxrows_in[(n - 1) % 2], 48 * ((n - 1) // 2 + 1))
                    a, r = negm[:, 0, :], negm[:, 1, :]
                    chain.mark(pool.tensor_copy(mparts[:, 0, :], a))
                    chain.wait()
                    chain.mark(pool.tensor_tensor(r, a, mparts[:, 0, :], ALU.subtract))
                    chain.wait()
                    chain.mark(pool.tensor_copy(mparts[:, 1, :], r))
                    chain.wait()
                    pool.tensor_tensor(mparts[:, 2, :], r, mparts[:, 1, :], ALU.subtract).then_inc(mparts_ready, 1)
                    pool.wait_ge(mparts_ready, n + 1)
                if what == "values_in" and rmsn:
                    pool.wait_ge(gexp_ready, n + 1)
                    pool.tensor_scalar(gate[:, b % 2, i, :], gate[:, b % 2, i, :], 1.0, None,
                                       ALU.add).then_inc(gate_ready, 1)
                if what == "add_bias":
                    y = htok[:, TT * b + 2 * i:TT * b + 2 * i + 2, :]
                    if n == 0:
                        pool.wait_ge(*rest_in)
                    pool.wait_ge(ring_filled, ring_at["turn_h", b, KD - 1] + 1)
                    pool.tensor_tensor(y, y, spread(bias_o[:, :].rearrange("p (i d) -> p i d", i=1), [P, 2, D]),
                                       ALU.add).then_inc(bias_added, 1)
                if what == "deviation":
                    t = TT * b
                    pool.wait_ge(stats_ready, t + TT)
                    chain.mark(pool.tensor_scalar(rstd[:, t:t + TT], mv[:, t:t + TT, 1], 1.0, LN_EPS,
                                                  ALU.mult, ALU.add))
                    chain.wait()
                    pool.tensor_tensor(rstd[:, t:t + TT], rstd[:, t:t + TT], half[:, 0:TT],
                                       ALU.pow).then_inc(rstd_ready, 1)

        @block.tensor
        def _(pe):
            pe.wait_ge(*first_in)

            def use_ring(what, b, i):
                n = ring_at[what, b, i]
                if n >= RING:
                    pe.wait_ge(*ring_release(ring_items[n - RING]))
                return ring[:, n % RING, :]

            def turn_h(b, k):
                if rmsn and k == 0:
                    pe.wait_ge(rows_in, TT * (b + 1))
                dst = use_ring("turn_h", b, k)
                for t in range(TT):
                    mm = pe.transpose(dst[:, P * t:P * t + P], htok[:, TT * b + t, P * k:P * k + P], ident[:, :])
                mm.then_inc(ring_filled, 1)

            def rows(b, t):
                if t == 0:
                    pe.wait_ge(ht_ready, KD * (b + 1))
                dst = use_ring("rows", b, t)
                for k in range(KD):
                    mm = pe.matmul(dst, ht[:, b % 2, k, P * t:P * t + P], w_in[:, k, 0:512],
                                   start=(k == 0), stop=(k == KD - 1))
                mm.then_inc(ring_filled, 1)

            def qk(b, f):
                if tok:
                    if f == 0:
                        pe.wait_ge(x_in[b % 2], 16 * (b // 2 + 1))
                    dst = use_ring("qk", b, f)
                    for k in range(KD):
                        mm = pe.matmul(dst, w_in[:, k, P * f:P * f + P], ht[:, b % 2, k, :],
                                       start=(k == 0), stop=(k == KD - 1))
                else:
                    if f == 0:
                        pe.wait_ge(rot_ready, TT * (b + 1))
                    dst = use_ring("qk", b, f)
                    for t in range(TT):
                        mm = pe.transpose(dst[:, P * t:P * t + P], rot[:, t, P * f:P * f + P], ident[:, :])
                mm.then_inc(ring_filled, 1)

            def values_in(b, t):
                if b + t == 0:
                    pe.wait_ge(*rest_in)
                dst = use_ring("values_in", b, t)
                for k in range(KD):
                    mm = pe.matmul(dst[:, 0:WV], ht[:, b % 2, k, P * t:P * t + P], w_in[:, k, 512:NW],
                                   start=(k == 0), stop=(k == KD - 1))
                mm.then_inc(ring_filled, 1)

            def row_max(b, i):
                h, t = i // TT, i % TT
                if h % 8 == 0 and t == 0:
                    pe.wait_ge(*stack_ready(b, h))
                dst = use_ring("row_max", b, i)
                pe.matmul(dst, qs[0:SK, b % 2, h, P * t:P * t + P], ks[0:SK, b % 2, h, :],
                          start=True, stop=True).then_inc(ring_filled, 1)

            def turn_max(b, i):
                dst = use_ring("turn_max", b, i)
                pe.wait_ge(max_done, TT * (H * b + 8 * i + 8))
                pe.transpose(dst[0:H * TT // 2, 0:P], rowmax[:, 8 * TT * i:8 * TT * i + 8 * TT],
                             ident[:, :]).then_inc(ring_filled, 1)

            def scores(b, i):
                h, p = i // 2, i % 2
                hh, n = H * b + h, 2 * H * b + i
                if i % 16 == 0:
                    pe.wait_ge(*stack_ready(b, h))
                    if softmax:
                        pe.wait_ge(maxrows_in[h // 8], 48 * (b + 1))
                        if n == 0:
                            pe.wait_ge(key_ones, 1)
                if softmax:
                    if n >= 2:
                        pe.wait_ge(prob_ready, n - 1)
                    for d in range(2):
                        kt = 2 * p + d
                        mm = pe.matmul(score[:, p, d, :], ks[0:SK + 3, b % 2, h, P * kt:P * kt + P],
                                       qs[0:SK + 3, b % 2, h, :], start=True, stop=True)
                elif p == 0:
                    if hh >= 2:
                        pe.wait_ge(prob_diag, hh - 1)
                    for kt, qt, nq, at in DIAG:
                        mm = pe.matmul(score[:, 0, hh % 2, at:at + P * nq], ks[0:SK, b % 2, h, P * kt:P * kt + P],
                                       qs[0:SK, b % 2, h, P * qt:P * (qt + nq)], start=True, stop=True)
                else:
                    if hh:
                        pe.wait_ge(prob_ready, hh)
                    for j, (kt, qt, nq, at) in enumerate(OFF):
                        mm = pe.matmul(score[:, 1, j // 2, at:at + P * nq], ks[0:SK, b % 2, h, P * kt:P * kt + P],
                                       qs[0:SK, b % 2, h, P * qt:P * (qt + nq)], start=True, stop=True)
                mm.then_inc(score_filled, 1)

            def values(b, i):
                g, kt = i // TT, i % TT
                if kt == 0:
                    hh = H * b + 4 * g + 4
                    pe.wait_ge(prob_ready, 2 * hh if softmax else hh)
                    if ret:
                        pe.wait_ge(prob_diag, hh)
                    if b + g:
                        pe.wait_ge(ot_ready, HG * b + g)
                    if g == 0:
                        pe.wait_ge(v_ready, TT * (b + 1))
                        pe.wait_ge(ones_set, 1)
                if softmax:
                    blocks = [(0, TT, S * kt)]
                else:
                    blocks = [(qt, nq, S + S * (j // 2) + at) for j, (k, qt, nq, at) in enumerate(OFF) if k == kt]
                    blocks.append((kt, 1, P * kt))
                for n, (qt, nq, at) in enumerate(blocks):
                    for j in range(4):
                        h = 4 * g + j
                        mm = pe.matmul(valps[32 * j:32 * j + 32, P * qt:P * (qt + nq)], v[:, kt, h, :],
                                       prob[:, (H * b + h) % P_SLOTS, at:at + P * nq],
                                       start=(kt == 0 and n == 0), stop=(kt == TT - 1 and n == len(blocks) - 1),
                                       tile_position=(0, 32 * j), skip_group_check=not softmax)
                mm.then_inc(val_filled, 1)

            def turn_o(b, t):
                if t == 0:
                    pe.wait_ge(ot_ready, HG * (b + 1))
                dst = use_ring("turn_o", b, t)
                for g in range(HG):
                    mm = pe.transpose(dst[:, P * g:P * g + P], ot[:, g, P * t:P * t + P], ident[:, :])
                mm.then_inc(ring_filled, 1)

            def turn_back(b, k):
                if k == 0:
                    pe.wait_ge(otok_ready, TT * (b + 1))
                dst = use_ring("turn_back", b, k)
                for t in range(TT):
                    mm = pe.transpose(dst[:, P * t:P * t + P], otok[:, t, P * k:P * k + P], ident[:, :])
                mm.then_inc(ring_filled, 1)

            def project_o(b, u):
                if u == 0:
                    pe.wait_ge(ot2_ready, KD * (b + 1))
                dst = use_ring("project_o", b, u)
                for i in range(2):
                    t = 2 * u + i
                    for k in range(KD):
                        mm = pe.matmul(dst[:, D * i:D * i + D], ot2[:, k, P * t:P * t + P], w_o[:, k, :],
                                       start=(k == 0), stop=(k == KD - 1))
                mm.then_inc(ring_filled, 1)

            def turn_r(b, k):
                if k == 0:
                    pe.wait_ge(normed, TT * (b + 1))
                dst = use_ring("turn_r", b, k)
                for t in range(TT):
                    mm = pe.transpose(dst[:, P * t:P * t + P], htok[:, TT * b + t, P * k:P * k + P], ident[:, :])
                mm.then_inc(ring_filled, 1)

            def route(b, i):
                pe.wait_ge(router_turned, KD * (b + 1))
                dst = use_ring("route", b, i)
                for t in range(TT):
                    for k in range(KD):
                        mm = pe.matmul(dst[:, E * t:E * t + E], ot2[:, k, P * t:P * t + P], router[:, k, :],
                                       start=(k == 0), stop=(k == KD - 1))
                mm.then_inc(ring_filled, 1)

            work = dict(turn_r=turn_r, route=route, turn_h=turn_h, rows=rows, qk=qk, values_in=values_in, row_max=row_max, turn_max=turn_max,
                        scores=scores, values=values, turn_o=turn_o, turn_back=turn_back, project_o=project_o)
            for what, b, i in order:
                if what in work:
                    work[what](b, i)

        @block.scalar
        def _(act):
            act.wait_ge(*first_in)
            for what, b, i in order:
                n = nth[what, b, i]
                if what == "turn_h":
                    src, filled = ring_view(what, b, i)
                    act.wait_ge(ring_filled, filled)
                    if b >= 2 and i == 0:
                        act.wait_ge(ring_filled, ring_at["values_in", b - 2, TT - 1] + 1)
                    act.activation(ht[:, b % 2, i, :], src, ACT.Copy).then_inc(ht_ready, 1)
                if what == "square":
                    act.wait_ge(rows_ready, n + 1)
                    if n:
                        act.wait_ge(ssq_ready, n)
                    act.activation(squares[:, :], rot[:, i, :], ACT.Square,
                                   scale=HD ** -0.5).then_inc(squares_ready, 1)
                if what == "root":
                    act.wait_ge(ssq_ready, TT * (n + 1))
                    act.wait_ge(half_set, 2)
                    if n:
                        act.wait_ge(rot_ready, TT * n)
                    act.activation(rms[:, 0, :, :].rearrange("p t a -> p (t a)"),
                                   ssq[:, :, :].rearrange("p t a -> p (t a)"), ACT.Sqrt,
                                   bias=eps[:, 0:1]).then_inc(roots_ready, 1)
                if what == "qk":
                    src, filled = ring_view(what, b, i)
                    act.wait_ge(ring_filled, filled)
                    if n >= 2:
                        act.wait_ge(parts_saved[n % 2], 96 * (n // 2))
                    if tok:
                        act.activation(parts[:, n % 2, 0, :], src, ACT.Identity,
                                       bias=bias_qk[:, i:i + 1]).then_inc(part0_ready, 1)
                    elif rmsn:
                        act.activation(parts[:, n % 2, 0, :], src, ACT.Copy,
                                       scale=norm_w[:, i // 2:i // 2 + 1]).then_inc(part0_ready, 1)
                    else:
                        act.activation(parts[:, n % 2, 0, :], src, ACT.Copy).then_inc(part0_ready, 1)
                if what == "split":
                    act.wait_ge(left_ready, n + 1)
                    act.activation(parts[:, n % 2, 1, :], left[:, n % 2, :], ACT.Copy).then_inc(part1_ready, 1)
                if what == "scores" and (softmax or i % 2):
                    hh, p = H * b + i // 2, i % 2
                    old = hh - P_SLOTS
                    act.wait_ge(score_filled, n + 1)
                    if old >= 0 and (p == 0 or ret):
                        act.wait_ge(val_filled, TT * (old // 4) + TT)
                    if softmax:
                        act.activation(prob[:, hh % P_SLOTS, 2 * p * S:2 * (p + 1) * S],
                                       score[:, p, :, :].rearrange("p i n -> p (i n)"), ACT.Exp,
                                       scale=HD ** -0.5).then_inc(prob_ready, 1)
                    else:
                        act.activation(prob[:, hh % P_SLOTS, S:S + 6 * P],
                                       score[:, 1, :, :].rearrange("p i n -> p (i n)")[:, 0:6 * P],
                                       ACT.Copy).then_inc(prob_ready, 1)
                if what == "values" and i % TT == TT - 1:
                    act.wait_ge(val_filled, n + 1)
                    if b and i == TT - 1:
                        act.wait_ge(ring_filled, ring_at["turn_o", b - 1, TT - 1] + 1)
                    act.activation(ot[:, i // TT, :], valps[:, :], ACT.Copy).then_inc(ot_ready, 1)
                if what == "values_in" and ret:
                    src, filled = ring_view(what, b, i)
                    act.wait_ge(ring_filled, filled)
                    if b and i == 0:
                        act.wait_ge(val_filled, TT * HG * b)
                    act.activation(v[:, i, :, 0:HD], src[:, 0:D].rearrange("p (h d) -> p h d", d=HD),
                                   ACT.Copy).then_inc(v_ready, 1)
                    if b >= 2 and i == 0:
                        act.wait_ge(otok_ready, TT * (b - 1))
                    act.activation(gate[:, b % 2, i, :], src[:, D:2 * D], ACT.Silu).then_inc(gate_ready, 1)
                if what == "values_in" and rmsn:
                    act.wait_ge(graw_ready, n + 1)
                    if b >= 2 and i == 0:
                        act.wait_ge(otok_ready, TT * (b - 1))
                    act.activation(gate[:, b % 2, i, :], graw[:, :], ACT.Exp, scale=-1.0).then_inc(gexp_ready, 1)
                if what == "turn_r":
                    act.wait_ge(ring_filled, ring_at[what, b, i] + 1)
                    act.activation(ot2[:, i, :], ring_view(what, b, i)[0], ACT.Copy).then_inc(router_turned, 1)
                if what == "turn_back":
                    act.wait_ge(ring_filled, ring_at[what, b, i] + 1)
                    act.activation(ot2[:, i, :], ring_view(what, b, i)[0], ACT.Copy).then_inc(ot2_ready, 1)

        @block.vector
        def _(dve):
            chain = Chain(dve, dve_step)
            dve.wait_ge(*first_in)
            heads = lambda a: a.rearrange("p (h d) -> p h d", d=HD)

            for what, b, i in order:
                n = nth[what, b, i]
                if what == "combine":
                    dve.wait_ge(fetched[i], 16 * 2 * (b + 1))
                    y = htok[:, TT * b + i, :]
                    for k in range(2):
                        chain.mark(dve.scalar_tensor_tensor(out=y, in0=got[:, i, k, :],
                                                            scalar=back["weight"][:, TT * b + i, k:k + 1], in1=y,
                                                            op0=ALU.mult, op1=ALU.add))
                        chain.wait()
                    chain.mark(dve.bn_stats(stats[:, :], y))
                    chain.wait()
                    dve.bn_aggr(mv_in[:, i, :], stats[:, :]).then_inc(combined, 1)
                    dve.wait_ge(combined, n + 1)
                if what == "normalise_in":
                    dve.wait_ge(rstd_in_ready, b + 1)
                    y = htok[:, TT * b + i, :]
                    dve.tensor_scalar(y, y, mv_in[:, i, 0:1], rstd_in[:, i:i + 1], ALU.subtract,
                                      ALU.mult).then_inc(rows_in, 1)
                if what == "values_in" and n == 0:
                    dve.wait_ge(*rest_in)
                if what == "rows":
                    src, filled = ring_view(what, b, i)
                    dve.wait_ge(ring_filled, filled)
                    if rmsn:
                        if i == 0 and b:
                            dve.wait_ge(ring_filled, ring_at["qk", b - 1, 3] + 1)
                        dve.tensor_tensor(rot[:, i, :], src, bias_in[:, 0:512], ALU.add).then_inc(rows_ready, 1)
                    else:
                        if n:
                            dve.wait_ge(rot_ready, n)
                        quad = lambda a: a.rearrange("p (h s r) -> p h s r", s=2, r=8)
                        both = lambda a: spread(a.rearrange("p (h s r) -> p h s r", s=1, r=8), [P, 32, 2, 8])
                        dve.tensor_tensor(quad(xcos[:, :]), quad(src), both(cos[:, i, :]), ALU.mult)
                        dve.tensor_tensor(quad(xsin[:, :]), quad(src), both(sin[:, i, :]),
                                          ALU.mult).then_inc(rows_ready, 1)
                if what == "square":
                    dve.wait_ge(squares_ready, n + 1)
                    if i == 0 and b:
                        dve.wait_ge(roots_ready, b)
                    dve.tensor_reduce(ssq[:, i, :], squares[:, :].rearrange("p (a d) -> p a d", d=HD), AX_X,
                                      ALU.add).then_inc(ssq_ready, 1)
                if what == "invert":
                    dve.wait_ge(roots_ready, n + 1)
                    if n:
                        dve.wait_ge(rot_ready, TT * n)
                    dve.reciprocal(rms[:, 1, :, :], rms[:, 0, :, :]).then_inc(inverse_ready, 1)
                if what == "qk":
                    src, filled = ring_view(what, b, i)
                    dve.wait_ge(part0_ready, n + 1)
                    if n >= 2:
                        dve.wait_ge(parts_ready, n - 1)
                    part0 = parts[:, n % 2, 0, :]
                    if tok:
                        dve.scalar_tensor_tensor(out=left[:, n % 2, :], in0=src, scalar=bias_qk[:, i:i + 1], in1=part0,
                                                 op0=ALU.add, op1=ALU.subtract).then_inc(left_ready, 1)
                    elif rmsn:
                        dve.scalar_tensor_tensor(out=left[:, n % 2, :], in0=src, scalar=norm_w[:, i // 2:i // 2 + 1],
                                                 in1=part0, op0=ALU.mult, op1=ALU.subtract).then_inc(left_ready, 1)
                    else:
                        dve.tensor_tensor(left[:, n % 2, :], src, part0, ALU.subtract).then_inc(left_ready, 1)
                if what == "row_max" and n == 0:
                    dve.memset(ks[SK:SK + 3, :, :, :].rearrange("p b h n -> p (b h n)").bitcast(I32),
                               0x3F803F80).then_inc(key_ones, 1)
                if what == "row_max":
                    src, filled = ring_view(what, b, i)
                    dve.wait_ge(ring_filled, filled)
                    dve.reduce_max(rowmax[:, i:i + 1], src, AX_X).then_inc(max_done, 1)
                if what == "turn_max":
                    src, filled = ring_view(what, b, i)
                    dve.wait_ge(ring_filled, filled)
                    if n:
                        dve.wait_ge(mparts_ready, n)
                    dve.tensor_scalar(negm[:, 0, :], src[0:H * TT // 2, 0:P], -1.0, None, ALU.mult).then_inc(negm_ready, 1)
                if what == "values_in" and softmax:
                    src, filled = ring_view(what, b, i)
                    dve.wait_ge(ring_filled, filled)
                    if b and i == 0:
                        dve.wait_ge(val_filled, TT * HG * b)
                    bias = bias_v[:, :] if tok else bias_in[:, 512:512 + D]
                    dve.tensor_tensor(v[:, i, :, 0:HD], heads(src[:, 0:D]), heads(bias), ALU.add).then_inc(v_ready, 1)
                    if rmsn:
                        if n:
                            dve.wait_ge(gexp_ready, n)
                        dve.tensor_tensor(graw[:, :], src[:, D:D + H], bias_in[:, 512 + D:NW],
                                          ALU.add).then_inc(graw_ready, 1)
                if what == "scores" and ret and i % 2 == 0:
                    hh = H * b + i // 2
                    old = hh - P_SLOTS
                    dve.wait_ge(score_filled, 2 * hh + 1)
                    if old >= 0:
                        dve.wait_ge(val_filled, TT * (old // 4) + TT)
                    dve.tensor_tensor(prob[:, hh % P_SLOTS, 0:S].rearrange("p (t n) -> p t n", n=P),
                                      score[:, 0, hh % 2, :].rearrange("p (t n) -> p t n", n=P),
                                      spread(causal[:, :].rearrange("p (t n) -> p t n", t=1), [P, TT, P]),
                                      ALU.mult).then_inc(prob_diag, 1)
                if what == "turn_o":
                    dve.wait_ge(ring_filled, ring_at[what, b, i] + 1)
                    if b and i == 0:
                        dve.wait_ge(ring_filled, ring_at["turn_back", b - 1, KD - 1] + 1)
                    o = ring_view(what, b, i)[0].rearrange("p (h e) -> p h e", e=32)
                    if ret:
                        dve.wait_ge(gate_ready, n + 1)
                        dve.tensor_tensor(heads(otok[:, i, :]), o[:, :, 0:HD], heads(gate[:, b % 2, i, :]),
                                          ALU.mult).then_inc(otok_ready, 1)
                        continue
                    r = rden[:, i, :]
                    if rmsn:
                        dve.wait_ge(gate_ready, n + 1)
                        chain.mark(dve.tensor_tensor(r, o[:, :, HD], gate[:, b % 2, i, :], ALU.mult))
                        chain.wait()
                        dve.reciprocal(r, r).then_inc(rden_step, 1)
                    else:
                        dve.reciprocal(r, o[:, :, HD]).then_inc(rden_step, 1)
                    dve.wait_ge(rden_step, n + 1)
                    dve.tensor_tensor(heads(otok[:, i, :]), o[:, :, 0:HD],
                                      spread(r.rearrange("p (h o) -> p h o", o=1), [P, H, HD]),
                                      ALU.mult).then_inc(otok_ready, 1)
                if what == "project_o":
                    dve.wait_ge(ring_filled, ring_at[what, b, i] + 1)
                    t = TT * b + 2 * i
                    y = htok[:, t:t + 2, :]
                    o = ring_view(what, b, i)[0].rearrange("p (i d) -> p i d", d=D)
                    if tok:
                        dve.tensor_tensor(y, o, spread(bias_o[:, :].rearrange("p (i d) -> p i d", i=1), [P, 2, D]),
                                          ALU.add).then_inc(y_ready, 1)
                        continue
                    if rmsn:
                        dve.wait_ge(bias_added, n + 1)
                    dve.tensor_tensor(y, y, o, ALU.add).then_inc(y_ready, 1)
                if what == "stats":
                    dve.wait_ge(y_ready, 2 * b + i // 2 + 1)
                    chain.mark(dve.bn_stats(stats[:, :], htok[:, TT * b + i, :]))
                    chain.wait()
                    dve.bn_aggr(mv[:, TT * b + i, :], stats[:, :]).then_inc(stats_ready, 1)
                    dve.wait_ge(stats_ready, n + 1)
                if what == "layernorm":
                    t = TT * b + i
                    dve.wait_ge(rstd_ready, b + 1)
                    dve.tensor_scalar(htok[:, t, :], htok[:, t, :], mv[:, t, 0:1], rstd[:, t:t + 1],
                                      ALU.subtract, ALU.mult).then_inc(normed, 1)
                if what == "route":
                    dve.wait_ge(ring_filled, ring_at[what, b, i] + 1)
                    dve.tensor_copy(env["logits"][:, TT * b:TT * b + TT, :].rearrange("p t e -> p (t e)"),
                                    ring_view(what, b, i)[0][:, 0:TT * E]).then_inc(logits_ready, 1)


def moe(nc, layer, env, dram):
    first = layer == 0
    htok, ident = env["htok"], env["ident"]
    rows_in, rows_out = dram[f"slots{layer}"], dram[f"results{layer}"]
    XT = F32 if first else BF16

    with ExitStack() as outer:
        def sbo(name, shape, dt=F32):
            return outer.enter_context(nc.sbuf_tensor(f"m{layer}_{name}", shape, dt))

        slot, weight = env["slot"], env["weight"]
        expert = sbo("expert", [P, NI], I32)
        packed = sbo("packed", [P, NI // 4 - 1], I32)
        if first:
            w_gu = sbo("w_gu", [P, KD, E, 2 * FI])
            w_dn = sbo("w_dn", [P, FI // P, E, D])
            b_gu = sbo("b_gu", [P, E, 2 * FI])
            b_dn = sbo("b_dn", [P, E, D])
            down_in = outer.enter_context(nc.semaphore("down_in"))
        else:
            w_up = sbo("w_up", [P, E, KD, HIDP], BF16)
            w_dn = sbo("w_dn", [P, E, HIDP // P, D], BF16)

        with ExitStack() as ctx:
            def sb(name, shape, dt=F32):
                return ctx.enter_context(nc.sbuf_tensor(f"r{layer}_{name}", shape, dt))

            def ps(name, shape, dt=F32):
                return ctx.enter_context(nc.psum_tensor(f"r{layer}_{name}", shape, dt))

            sem = semaphores(nc, ctx, f"r{layer}_")

            rb = env[f"r{layer}_b"]
            iota = env["iota"]
            before = env["before"]
            ones = sb("ones", [P, P])
            upto = env["upto"]
            logit = env["logits"]
            score = sb("score", [P, NT, E])
            choice = sb("choice", [P, NT, E]) if not first else score
            top = sb("top", [P, NT])
            total = sb("total", [P, NT])
            max8 = sb("max8", [P, NT, 8])
            idx8 = sb("idx8", [P, NT, 8], U32)
            idxf = sb("idxf", [P, 2, NT])
            pick = sb("pick", [P, 2, NT, E])
            both = sb("both", [P, NT, E])
            prod = sb("prod", [P, 2, NT, E])
            count = sb("count", [P, E])
            count_i = sb("count_i", [P, E], I32)
            tiles_i = sb("tiles_i", [P, E], I32)
            tiles = sb("tiles", [P, E])
            tri = sb("tri", [P, E, E])
            upto_e = sb("upto_e", [P, E])
            base = sb("base", [P, E])
            place = sb("place", [P, NT, E])
            slotf = sb("slotf", [P, 2, NT])
            cmp = sb("cmp", [P, NI, E])
            expf = sb("expf", [P, NI])
            packf = sb("packf", [P, 2, NI // 4 - 1])
            places = ps("places", [P, S])
            counts = ps("counts", [P, S])[:, 0:E]
            sofar = sb("sofar", [P, 2, NT, E])
            if first:
                late = [(w_gu[:, :, e, :], dram["m0_w_gu"][e].rearrange("(k p) n -> p k n", p=P)) for e in range(E)]
                down = [(w_dn[:, :, e, :], dram["m0_w_dn"][e].rearrange("(k p) n -> p k n", p=P)) for e in range(E)]
                brows = sb("brows", [E, 2 * FI + D])
                biases = [(brows[:, 0:2 * FI], dram["m0_b_gu"]), (brows[:, 2 * FI:2 * FI + D], dram["m0_b_dn"])]
                bcast = ps("bcast", [P, 2, S])
                biases_in = sem("biases_in")
                bcast_filled = sem("bcast_filled")
                bcast_read = sem("bcast_read")
                spans = [(e, at, min(S, 2 * FI + D - at)) for e in range(E) for at in range(0, 2 * FI + D, S)]
            else:
                hT = sb("hT", [P, KD, NT * P])
                turned = ps("turned", [P, 2, S])
                s_up = sb("s_up", [P, KD, HIDP])
                s_dn = sb("s_dn", [P, HIDP // P, D])
                raw = sb("raw", [P, 2, KD * HIDP])
                hid = sb("hid", [P, 2, HIDP // P, S])
                scaled = sb("scaled", [P, NT, 2, D], BF16)
                shup = ps("shup", [P, 2, S])
                shdn = ps("shdn", [P, 2, S])
                late = [(s_up[:, :, :], dram["s_up"].rearrange("(k p) n -> p k n", p=P)),
                        (s_dn[:, :, :], dram["s_dn"].rearrange("(k p) n -> p k n", p=P))]

            weights_in = sem("weights_in")
            ones_set = sem("ones_set")
            turned_filled = sem("turned_filled")
            ht_ready = sem("ht_ready")
            logits_ready = sem("logits_ready")
            exp_ready = sem("exp_ready")
            both_ready = sem("both_ready")
            sofar_ready = sem("sofar_ready")
            places_filled = sem("places_filled")
            slots_ready = sem("slots_ready")
            sent = sem("sent")
            dve_step = sem("dve_step")
            raw_in = [sem(f"raw_in{i}") for i in range(2)]
            cast_done = sem("cast_done")
            up_filled = sem("up_filled")
            relu_ready = sem("relu_ready")
            hid_ready = sem("hid_ready")
            dn_filled = sem("dn_filled")
            dn_read = sem("dn_read")
            scaled_ready = sem("scaled_ready")
            HC = HIDP // P

            block = ctx.enter_context(nc.Block())

            @block.sync
            def _(sp):
                if first:
                    for dst, src in biases:
                        sp.dma_start(dst, src).then_inc(biases_in, 16)
                for dst, src in late:
                    sp.dma_start(dst, src).then_inc(weights_in, 16)
                if not first:
                    for i in range(2 * E):
                        e, up = i // 2, i % 2 == 0
                        if i >= 2:
                            sp.wait_ge(cast_done, i - 1)
                        n = KD * HIDP if up else HC * D
                        src = dram["m1_w_up" if up else "m1_w_dn"][e].rearrange("(k p) n -> p k n", p=P)
                        sp.dma_start(raw[:, i % 2, 0:n].rearrange("p (k n) -> p k n", k=KD if up else HC),
                                     src).then_inc(raw_in[i % 2], 16)
                else:
                    for dst, src in down:
                        sp.dma_start(dst, src).then_inc(down_in, 16)
                    sp.wait_ge(weights_in, 16 * len(late))

            @block.tensor
            def _(pe):
                def turn(b):
                    for k in range(KD):
                        u = KD * b + k
                        if u >= 2:
                            pe.wait_ge(ht_ready, u - 1)
                        for t in range(TT):
                            mm = pe.transpose(turned[:, u % 2, P * t:P * t + P], htok[:, TT * b + t, P * k:P * k + P],
                                              ident[:, :])
                        mm.then_inc(turned_filled, 1)

                def shared_up(b):
                    pe.wait_ge(ht_ready, KD * (b + 1))
                    if b == 0:
                        pe.wait_ge(weights_in, 16 * len(late))
                    for c in range(HC):
                        u = HC * b + c
                        if u >= 2:
                            pe.wait_ge(relu_ready, u - 1)
                        for k in range(KD):
                            mm = pe.matmul(shup[:, u % 2, :], s_up[:, k, P * c:P * c + P],
                                           hT[:, k, S * b:S * b + S], start=(k == 0), stop=(k == KD - 1))
                        mm.then_inc(up_filled, 1)

                def shared_down(b):
                    pe.wait_ge(hid_ready, HC * (b + 1))
                    for i in range(2):
                        u = 2 * b + i
                        if u >= 2:
                            pe.wait_ge(dn_read, u - 1)
                        for t in range(2):
                            for c in range(HC):
                                mm = pe.matmul(shdn[:, u % 2, D * t:D * t + D],
                                               hid[:, b % 2, c, P * (2 * i + t):P * (2 * i + t) + P],
                                               s_dn[:, c, :], start=(c == 0), stop=(c == HC - 1))
                        mm.then_inc(dn_filled, 1)

                if not first:
                    turn(0)
                    turn(1)
                pe.wait_ge(*env["tables_in"])
                pe.wait_ge(both_ready, 1)
                pe.wait_ge(ones_set, 1)
                flat = lambda a: a.rearrange("p n e -> p (n e)")
                pe.matmul(places[:, 0:NT * E], before[:, :], flat(both[:, :, :]), start=True, stop=False)
                pe.wait_ge(sofar_ready, 1)
                pe.matmul(places[:, 0:NT * E], ones[:, :], flat(sofar[:, 1, :, :]), start=False, stop=True)
                pe.matmul(counts, ones[:, :], sofar[:, 1, NT - 1, :], start=True, stop=False)
                pe.matmul(counts, ones[:, :], both[:, NT - 1, :], start=False, stop=True).then_inc(places_filled, 1)
                if not first:
                    shared_up(0)
                if first:
                    pe.wait_ge(biases_in, 16 * len(biases))
                    for n, (e, at, width) in enumerate(spans):
                        if n >= 2:
                            pe.wait_ge(bcast_read, n - 1)
                        pe.matmul(bcast[:, n % 2, 0:width], spread(ident[0:E, e:e + 1], [E, P]),
                                  brows[:, at:at + width], start=True, stop=True).then_inc(bcast_filled, 1)
                if not first:
                    for b in range(B):
                        if b + 1 < B:
                            shared_up(b + 1)
                        if b + 2 < B:
                            turn(b + 2)
                        shared_down(b)

            @block.scalar
            def _(act):
                if first:
                    act.wait_ge(logits_ready, 1)
                act.activation(score[:, :, :].rearrange("p n e -> p (n e)"),
                               logit[:, :, :].rearrange("p n e -> p (n e)"),
                               ACT.Exp if first else ACT.Sigmoid).then_inc(exp_ready, 1)
                if first:
                    for n, (e, at, width) in enumerate(spans):
                        dst = b_gu[:, e, at:at + width] if at < 2 * FI else b_dn[:, e, :]
                        act.wait_ge(bcast_filled, n + 1)
                        act.activation(dst, bcast[:, n % 2, 0:width], ACT.Copy).then_inc(bcast_read, 1)
                if not first:
                    def take(u):
                        act.wait_ge(turned_filled, u + 1)
                        b, k = u // KD, u % KD
                        act.activation(hT[:, k, S * b:S * b + S], turned[:, u % 2, :], ACT.Copy).then_inc(ht_ready, 1)

                    def cast(i):
                        e, up = i // 2, i % 2 == 0
                        n = KD * HIDP if up else HC * D
                        act.wait_ge(raw_in[i % 2], 16 * (i // 2 + 1))
                        dst = (w_up if up else w_dn)[:, e, :, :].rearrange("p k n -> p (k n)")
                        act.activation(dst, raw[:, i % 2, 0:n], ACT.Copy).then_inc(cast_done, 1)

                    def relu(b):
                        for c in range(HC):
                            act.wait_ge(up_filled, HC * b + c + 1)
                            if b >= 2 and c == 0:
                                act.wait_ge(dn_filled, 2 * (b - 1))
                            act.activation(hid[:, b % 2, c, :], shup[:, (HC * b + c) % 2, :],
                                           ACT.Relu).then_inc(relu_ready, 1)

                    for u in range(2 * KD):
                        take(u)
                    relu(0)
                    for b in range(B):
                        if b + 1 < B:
                            relu(b + 1)
                        if b + 2 < B:
                            take(KD * (b + 2))
                            take(KD * (b + 2) + 1)
                        for i in range(4 * b, 4 * b + 4):
                            cast(i)

            @block.gpsimd
            def _(pool):
                pool.memset(ones[:, :], 1.0).then_inc(ones_set, 1)
                pool.wait_ge(slots_ready, 1)
                pool.wait_ge(*env["slots_cleared"][layer])
                for n in range(NT):
                    if not first:
                        pool.wait_ge(scaled_ready, n + 1)
                    for k in range(2):
                        src = htok[:, n, :] if first else scaled[:, n, k, :]
                        pool.indirect_dma_start(rows_in, bass.IndirectOffsetOnAxis(ap=slot[:, n, k:k + 1], axis=0),
                                                src, None).then_inc(sent, 16)
                pool.wait_ge(sent, 16 * 2 * NT)

            @block.vector
            def _(dve):
                chain = Chain(dve, dve_step)

                def then(ins):
                    chain.mark(ins)
                    chain.wait()

                def over_tiles(ap):
                    return spread(ap.rearrange("p (n e) -> p n e", n=1), [P, NT, E])

                def over_experts(ap, n=NT):
                    return spread(ap.rearrange("p (n e) -> p n e", e=1), [P, n, E])

                dve.wait_ge(*env["tables_in"])
                if first:
                    then(dve.tensor_tensor(logit[:, :, :], logit[:, :, :], over_tiles(rb[:, :]), ALU.add))
                    then(dve.tensor_reduce(top[:, :], logit[:, :, :], AX_X, ALU.max))
                    dve.tensor_tensor(logit[:, :, :], logit[:, :, :], over_experts(top[:, :]),
                                      ALU.subtract).then_inc(logits_ready, 1)
                    dve.wait_ge(exp_ready, 1)
                    then(dve.tensor_reduce(total[:, :], score[:, :, :], AX_X, ALU.add))
                    then(dve.reciprocal(total[:, :], total[:, :]))
                    then(dve.tensor_tensor(score[:, :, :], score[:, :, :], over_experts(total[:, :]), ALU.mult))
                else:
                    dve.wait_ge(exp_ready, 1)
                    then(dve.tensor_tensor(choice[:, :, :], score[:, :, :], over_tiles(rb[:, :]), ALU.add))
                for n in range(NT):
                    chain.mark(dve.max(max8[:, n, :], choice[:, n, :]))
                chain.wait()
                for n in range(NT):
                    chain.mark(dve.max_index(idx8[:, n, :], max8[:, n, :], choice[:, n, :]))
                chain.wait()
                for k in range(2):
                    chain.mark(dve.tensor_copy(idxf[:, k, :], idx8[:, :, k]))
                chain.wait()
                for k in range(2):
                    chain.mark(dve.tensor_tensor(pick[:, k, :, :], over_tiles(iota[:, 0:E]),
                                                 over_experts(idxf[:, k, :]), ALU.is_equal))
                chain.wait()
                dve.tensor_tensor(both[:, :, :], pick[:, 0, :, :], pick[:, 1, :, :], ALU.add).then_inc(both_ready, 1)
                dve.wait_ge(both_ready, 1)
                dve.memset(sofar[:, 0, 0:1, :], 0.0)
                then(dve.tensor_copy(sofar[:, 0, 1:NT, :], both[:, 0:NT - 1, :]))
                step, at = 1, 0
                while step < NT:
                    dve.tensor_copy(sofar[:, 1 - at, 0:step, :], sofar[:, at, 0:step, :])
                    then(dve.tensor_tensor(sofar[:, 1 - at, step:NT, :], sofar[:, at, step:NT, :],
                                           sofar[:, at, 0:NT - step, :], ALU.add))
                    step, at = 2 * step, 1 - at
                dve.tensor_copy(sofar[:, 1, :, :], sofar[:, 0, :, :]).then_inc(sofar_ready, 1)
                for k in range(2):
                    chain.mark(dve.tensor_tensor(prod[:, k, :, :], pick[:, k, :, :], score[:, :, :], ALU.mult))
                chain.wait()
                for k in range(2):
                    chain.mark(dve.tensor_reduce(weight[:, :, k], prod[:, k, :, :], AX_X, ALU.add))
                chain.wait()
                dve.wait_ge(places_filled, 1)
                then(dve.tensor_scalar(count_i[:, :], counts, float(P - 1), None, ALU.add))
                then(dve.tensor_scalar(tiles_i[:, :], count_i[:, :], 7, None, ALU.logical_shift_right))
                then(dve.tensor_copy(tiles[:, :], tiles_i[:, :]))
                then(dve.tensor_tensor(tri[:, :, :], upto[:, :, :],
                                       spread(tiles[:, :].rearrange("p (a b) -> p a b", a=1), [P, E, E]), ALU.mult))
                then(dve.tensor_reduce(upto_e[:, :], tri[:, :, :], AX_X, ALU.add))
                then(dve.tensor_tensor(base[:, :], upto_e[:, :], tiles[:, :], ALU.subtract))
                then(dve.tensor_scalar(base[:, :], base[:, :], float(P), None, ALU.mult))
                then(dve.tensor_tensor(place[:, :, :], places[:, 0:NT * E].rearrange("p (n e) -> p n e", e=E),
                                       over_tiles(base[:, :]), ALU.add))
                for k in range(2):
                    chain.mark(dve.tensor_tensor(prod[:, k, :, :], pick[:, k, :, :], place[:, :, :], ALU.mult))
                chain.wait()
                for k in range(2):
                    chain.mark(dve.tensor_reduce(slotf[:, k, :], prod[:, k, :, :], AX_X, ALU.add))
                chain.wait()
                dve.tensor_copy(slot[:, :, :].rearrange("p n k -> p k n"), slotf[:, :, :]).then_inc(slots_ready, 1)
                if not first:
                    def square(b):
                        for u in range(HC * b, HC * b + HC):
                            dve.wait_ge(relu_ready, u + 1)
                            x = hid[:, b % 2, u % HC, :]
                            dve.tensor_tensor(x, x, x, ALU.mult).then_inc(hid_ready, 1)

                    def scale(n):
                        dve.tensor_scalar(scaled[:, n, 0, :], htok[:, n, :], weight[:, n, 0:1], None, ALU.mult)
                        dve.tensor_scalar(scaled[:, n, 1, :], htok[:, n, :], weight[:, n, 1:2], None,
                                          ALU.mult).then_inc(scaled_ready, 1)

                    def join(u):
                        dve.wait_ge(dn_filled, u + 1)
                        y = htok[:, 2 * u:2 * u + 2, :]
                        dve.tensor_tensor(y, y, shdn[:, u % 2, :].rearrange("p (i d) -> p i d", d=D),
                                          ALU.add).then_inc(dn_read, 1)

                    for n in range(TT):
                        scale(n)
                    square(0)
                then(dve.tensor_tensor(cmp[:, :, :],
                                       spread(upto_e[:, :].rearrange("p (n e) -> p n e", n=1), [P, NI, E]),
                                       over_experts(iota[:, :], NI), ALU.is_le))
                then(dve.tensor_reduce(expf[:, :], cmp[:, :, :], AX_X, ALU.add))
                then(dve.tensor_scalar(expf[:, :], expf[:, :], float(E - 1), None, ALU.min))
                then(dve.tensor_copy(expert[:, :], expf[:, :]))
                if not first:
                    def every4(k):
                        return expf[:, k // 4 * 4:NI - 4 + k // 4 * 4].rearrange("p (i o) -> p i o", o=4)[:, :, k % 4]

                    then(dve.tensor_copy(packf[:, 0, :], every4(0)))
                    for k in range(1, 6):
                        dst = packf[:, k % 2, :] if k < 5 else packed[:, :]
                        then(dve.scalar_tensor_tensor(out=dst, in0=every4(k), scalar=float(E ** k),
                                                      in1=packf[:, 1 - k % 2, :], op0=ALU.mult, op1=ALU.add))
                if not first:
                    for b in range(B):
                        if b + 1 < B:
                            square(b + 1)
                            for n in range(TT * (b + 1), TT * (b + 2)):
                                scale(n)
                        dve.wait_ge(scaled_ready, TT * (b + 1))
                        dve.wait_ge(turned_filled, KD * (b + 1))
                        join(2 * b)
                        join(2 * b + 1)

        with ExitStack() as ctx:
            def sb(name, shape, dt=F32):
                return ctx.enter_context(nc.sbuf_tensor(f"t{layer}_{name}", shape, dt))

            def ps(name, shape, dt=F32):
                return ctx.enter_context(nc.psum_tensor(f"t{layer}_{name}", shape, dt))

            sem = semaphores(nc, ctx, f"t{layer}_")

            (tiles_first if first else tiles_second)(nc, env, sb, ps, sem, ctx, dict(
                rows_in=rows_in, rows_out=rows_out, expert=expert, packed=packed, w_dn=w_dn,
                **(dict(w_gu=w_gu, b_gu=b_gu, b_dn=b_dn, down_in=(down_in, 16 * E)) if first else dict(w_up=w_up))))

        if first:
            return

        with ExitStack() as ctx:
            def sb(name, shape, dt=F32):
                return ctx.enter_context(nc.sbuf_tensor(f"c{layer}_{name}", shape, dt))

            sem = semaphores(nc, ctx, f"c{layer}_")

            got = sb("got", [P, NT, 2, D], BF16)
            stats = sb("stats", [P, 6])
            mv = sb("mv", [P, NT, 2])
            root = sb("root", [P, NT])
            rstd = sb("rstd", [P, NT])
            eps = sb("eps", [P, 1])
            fetched = [sem(f"fetched{n}") for n in range(NT)]
            eps_set = sem("eps_set")
            dve_step = sem("dve_step")
            stats_ready = sem("stats_ready")
            root_ready = sem("root_ready")
            normed = sem("normed")
            stored = sem("stored")
            block = ctx.enter_context(nc.Block())

            @block.gpsimd
            def _(pool):
                pool.memset(eps[:, :], LN_EPS).then_inc(eps_set, 1)
                for n in range(NT):
                    for k in range(2):
                        pool.indirect_dma_start(got[:, n, k, :], None, rows_out,
                                                bass.IndirectOffsetOnAxis(ap=slot[:, n, k:k + 1], axis=0)
                                                ).then_inc(fetched[n], 16)

            @block.scalar
            def _(act):
                act.wait_ge(eps_set, 1)
                for n in range(NT):
                    act.wait_ge(stats_ready, n + 1)
                    act.activation(root[:, n:n + 1], mv[:, n, 1:2], ACT.Sqrt,
                                   bias=eps[:, 0:1]).then_inc(root_ready, 1)

            @block.vector
            def _(dve):
                chain = Chain(dve, dve_step)

                def combine(n):
                    dve.wait_ge(fetched[n], 16 * 2)
                    y = htok[:, n, :]
                    for k in range(2):
                        chain.mark(dve.tensor_tensor(y, y, got[:, n, k, :], ALU.add))
                        chain.wait()
                    chain.mark(dve.bn_stats(stats[:, :], y))
                    chain.wait()
                    dve.bn_aggr(mv[:, n, :], stats[:, :]).then_inc(stats_ready, 1)
                    dve.wait_ge(stats_ready, n + 1)

                def normalise(n):
                    dve.wait_ge(root_ready, n + 1)
                    chain.mark(dve.reciprocal(rstd[:, n:n + 1], root[:, n:n + 1]))
                    chain.wait()
                    dve.tensor_scalar(htok[:, n, :], htok[:, n, :], mv[:, n, 0:1], rstd[:, n:n + 1],
                                      ALU.subtract, ALU.mult).then_inc(normed, 1)

                for n in range(NT + 1):
                    if n < NT:
                        combine(n)
                    if n:
                        normalise(n - 1)

            @block.sync
            def _(sp):
                out = dram["out"].rearrange("(t p) d -> p t d", p=P)
                for n in range(0, NT, 2):
                    sp.wait_ge(normed, n + 2)
                    sp.dma_start(out[:, n:n + 2, :], htok[:, n:n + 2, :]).then_inc(stored, 16)
                sp.wait_ge(stored, 16 * (NT // 2))


def in_steps(eng, first, last, step, unroll=2):
    turns = (last - first) // unroll
    if turns > 1:
        with eng.Fori(0, turns) as i:
            for d in range(unroll):
                step(i * unroll + (first + d), (first + d) % unroll)
    else:
        turns = 0
    for j in range(first + unroll * turns, last):
        step(j, j % unroll)


def tiles_first(nc, env, sb, ps, sem, ctx, t):
    ident, expert = env["ident"], t["expert"]
    KF = FI // P
    xin = sb("xin", [P, 2, D])
    xT = sb("xT", [P, 2, KD, P])
    g = sb("g", [P, 2, FI])
    u = sb("u", [P, 2, FI])
    sig = sb("sig", [P, 2, FI])
    act_t = sb("act", [P, 2, FI])
    aT = sb("aT", [P, 2, KF, P])
    y = sb("y", [P, 2, D])
    x_ps = ps("x_ps", [P, 2 * KD, P])
    g_ps = ps("g_ps", [P, 2, FI])
    u_ps = ps("u_ps", [P, 2, FI])
    a_ps = ps("a_ps", [P, KF, P])
    y_ps = ps("y_ps", [P, 2 * D])

    x_in = [sem(f"x_in{i}") for i in range(2)]
    x_turned = sem("x_turned")
    xT_ready = sem("xT_ready")
    g_filled = sem("g_filled")
    u_filled = sem("u_filled")
    g_ready = sem("g_ready")
    u_ready = sem("u_ready")
    g_min = sem("g_min")
    u_clip = sem("u_clip")
    sig_ready = sem("sig_ready")
    glu_ready = sem("glu_ready")
    a_ready = sem("a_ready")
    a_turned = sem("a_turned")
    aT_ready = sem("aT_ready")
    y_filled = sem("y_filled")
    y_ready = sem("y_ready")
    y_saved = [sem(f"y_saved{i}") for i in range(2)]
    block = ctx.enter_context(nc.Block())

    def of_expert(eng, j):
        return eng.value_load(expert[0:1, bass.ds(j, 1)], min_val=0, max_val=E - 1)

    @block.sync
    def _(sp):
        def rows(ap, j):
            return ap[bass.ds(j * P, P), :]

        def load(j, q):
            sp.dma_start(xin[:, q, :], rows(t["rows_in"], j)).then_inc(x_in[q], 16)

        def step(j, q):
            sp.wait_ge(x_turned, j - 1)
            load(j, q)

        load(0, 0)
        load(1, 1)
        in_steps(sp, 2, NU, step)
        for q, s in enumerate(y_saved):
            sp.wait_ge(s, 16 * len(range(q, NU, 2)))

    @block.tensor
    def _(pe):
        def turn_x(j, q, early=False):
            pe.wait_ge(x_in[q], 8 * (j - q) + 16)
            if not early:
                pe.wait_ge(xT_ready, j)
            for k in range(KD):
                mm = pe.transpose(x_ps[:, k, :], xin[:, q, P * k:P * k + P], ident[:, :])
            mm.then_inc(x_turned, 1)

        def gate(j, q, early=False):
            e = of_expert(pe, j)
            pe.wait_ge(xT_ready, j + 1)
            if not early:
                pe.wait_ge(g_ready, j - 1)
            for k in range(KD):
                mm = pe.matmul(g_ps[:, q, :], xT[:, q, k, :],
                               t["w_gu"][:, k, bass.ds(e, 1), 0:FI].rearrange("p o n -> p (o n)"),
                               start=(k == 0), stop=(k == KD - 1))
            mm.then_inc(g_filled, 1)
            return e

        def up(j, q, e, early=False):
            if not early:
                pe.wait_ge(u_ready, j - 1)
            for k in range(KD):
                mm = pe.matmul(u_ps[:, q, :], xT[:, q, k, :],
                               t["w_gu"][:, k, bass.ds(e, 1), FI:2 * FI].rearrange("p o n -> p (o n)"),
                               start=(k == 0), stop=(k == KD - 1))
            mm.then_inc(u_filled, 1)

        def turn_a(j, q, early=False):
            pe.wait_ge(a_ready, j + 1)
            if not early:
                pe.wait_ge(aT_ready, j)
            for k in range(KF):
                mm = pe.transpose(a_ps[:, k, :], act_t[:, q, P * k:P * k + P], ident[:, :])
            mm.then_inc(a_turned, 1)

        def down(j, q, early=False):
            e = of_expert(pe, j)
            pe.wait_ge(aT_ready, j + 1)
            if not early:
                pe.wait_ge(y_ready, j)
            for k in range(KF):
                mm = pe.matmul(y_ps[:, 0:D], aT[:, q, k, :],
                               t["w_dn"][:, k, bass.ds(e, 1), :].rearrange("p o n -> p (o n)"),
                               start=(k == 0), stop=(k == KF - 1))
            mm.then_inc(y_filled, 1)

        def step(j, q):
            e = gate(j + 1, 1 - q)
            turn_x(j + 2, q)
            down(j - 2, q)
            up(j + 1, 1 - q, e)
            turn_a(j - 1, 1 - q)

        turn_x(0, 0, True)
        turn_x(1, 1)
        for j in (0, 1):
            e = gate(j, j, True)
            up(j, j, e, True)
        turn_x(2, 0)
        for j in (1, 2, 3):
            e = gate(j + 1, 1 - j % 2)
            turn_x(j + 2, j % 2)
            if j == 2:
                pe.wait_ge(*t["down_in"])
            if j > 1:
                down(j - 2, j % 2, j == 2)
            up(j + 1, 1 - j % 2, e)
            turn_a(j - 1, 1 - j % 2, j == 1)
        in_steps(pe, 4, NU - 2, step)
        last = NU - 2
        e = gate(last + 1, 1 - last % 2)
        down(last - 2, last % 2)
        up(last + 1, 1 - last % 2, e)
        turn_a(last - 1, 1 - last % 2)
        down(last - 1, 1 - last % 2)
        turn_a(last, last % 2)
        down(last, last % 2)
        turn_a(last + 1, 1 - last % 2)
        down(last + 1, 1 - last % 2)

    @block.scalar
    def _(act):
        def take_x(j, q):
            act.wait_ge(x_turned, j + 1)
            act.activation(xT[:, q, :, :], x_ps[:, 0:KD, :], ACT.Copy).then_inc(xT_ready, 1)

        def sigmoid(j, q):
            act.wait_ge(g_min, j + 1)
            act.activation(sig[:, q, :], g[:, q, :], ACT.Sigmoid, scale=1.702).then_inc(sig_ready, 1)

        def take_a(j, q):
            act.wait_ge(a_turned, j + 1)
            act.activation(aT[:, q, :, :], a_ps[:, :, :], ACT.Copy).then_inc(aT_ready, 1)

        def save(j, q):
            act.wait_ge(y_ready, j + 1)
            act.dma_start(t["rows_out"][bass.ds(j * P, P), :], y[:, q, :]).then_inc(y_saved[q], 16)

        def step(j, q):
            take_x(j + 1, 1 - q)
            take_a(j - 2, q)
            sigmoid(j, q)
            save(j - 4, q)

        take_x(0, 0)
        take_x(1, 1)
        sigmoid(0, 0)
        sigmoid(1, 1)
        take_x(2, 0)
        for j in (2, 3):
            take_x(j + 1, 1 - j % 2)
            take_a(j - 2, j % 2)
            sigmoid(j, j % 2)
        in_steps(act, 4, NU - 1, step)
        last = NU - 1
        take_a(last - 2, last % 2)
        sigmoid(last, last % 2)
        save(last - 4, last % 2)
        take_a(last - 1, 1 - last % 2)
        save(last - 3, 1 - last % 2)
        take_a(last, last % 2)
        for j in range(last - 2, NU):
            save(j, j % 2)

    @block.gpsimd
    def _(pool):
        def step(j, q):
            pool.wait_ge(sig_ready, j + 1)
            pool.tensor_tensor(sig[:, q, :], sig[:, q, :], g[:, q, :], ALU.mult).then_inc(glu_ready, 1)

        in_steps(pool, 0, NU, step)

    @block.vector
    def _(dve):
        def hidden(j, q, early=False):
            e = of_expert(dve, j)
            dve.wait_ge(g_filled, j + 1)
            dve.tensor_tensor(g[:, q, :], g_ps[:, q, :],
                              t["b_gu"][:, bass.ds(e, 1), 0:FI].rearrange("p o n -> p (o n)"),
                              ALU.add).then_inc(g_ready, 1)
            dve.wait_ge(g_ready, j + 1)
            dve.tensor_scalar(g[:, q, :], g[:, q, :], LIMIT, None, ALU.min).then_inc(g_min, 1)
            dve.wait_ge(u_filled, j + 1)
            dve.tensor_tensor(u[:, q, :], u_ps[:, q, :],
                              t["b_gu"][:, bass.ds(e, 1), FI:2 * FI].rearrange("p o n -> p (o n)"),
                              ALU.add).then_inc(u_ready, 1)
            dve.wait_ge(u_ready, j + 1)
            dve.tensor_scalar(u[:, q, :], u[:, q, :], LIMIT, -LIMIT, ALU.min, ALU.max).then_inc(u_clip, 1)
            dve.wait_ge(u_clip, j + 1)
            dve.wait_ge(glu_ready, j + 1)
            if not early:
                dve.wait_ge(a_turned, j - 1)
            dve.scalar_tensor_tensor(out=act_t[:, q, :], in0=u[:, q, :], scalar=1.0, in1=sig[:, q, :],
                                     op0=ALU.add, op1=ALU.mult).then_inc(a_ready, 1)

        def result(j, q, early=False):
            e = of_expert(dve, j)
            dve.wait_ge(y_filled, j + 1)
            if not early:
                dve.wait_ge(y_saved[q], 8 * (j - q))
            dve.tensor_tensor(y[:, q, :], y_ps[:, 0:D],
                              t["b_dn"][:, bass.ds(e, 1), :].rearrange("p o n -> p (o n)"),
                              ALU.add).then_inc(y_ready, 1)

        def step(j, q):
            result(j - 3, 1 - q)
            hidden(j, q)

        hidden(0, 0, True)
        hidden(1, 1, True)
        hidden(2, 0)
        for j in (3, 4):
            result(j - 3, 1 - j % 2, True)
            hidden(j, j % 2)
        in_steps(dve, 5, NU, step)
        for j in range(NU - 3, NU):
            result(j, j % 2)


def tiles_second(nc, env, sb, ps, sem, ctx, t):
    packed, ident = t["packed"], env["ident_bf"]
    HC = HIDP // P
    DEEP = 4
    xin = sb("xin", [P, DEEP, D], BF16)
    xT = sb("xT", [P, 2, KD, P], BF16)
    h = sb("h", [P, 2, HC, P], BF16)
    hsq = sb("hsq", [P, 2, HC, P], BF16)
    y = sb("y", [P, DEEP, D], BF16)
    x_ps = [ps(f"x_ps{i}", [P, 2 * S], BF16) for i in range(2)]
    h_ps = [ps(f"h_ps{i}", [P, 512]) for i in range(2)]
    y_ps = [ps(f"y_ps{i}", [P, 512]) for i in range(2)]
    x_in = [sem(f"x_in{i}") for i in range(DEEP)]
    x_turned = sem("x_turned")
    xT_ready = sem("xT_ready")
    h_filled = sem("h_filled")
    h_ready = sem("h_ready")
    hsq_ready = sem("hsq_ready")
    y_filled = sem("y_filled")
    y_ready = sem("y_ready")
    y_saved = [sem(f"y_saved{i}") for i in range(DEEP)]
    block = ctx.enter_context(nc.Block())

    @block.sync
    def _(sp):
        def rows(ap, j):
            return ap[bass.ds(j * P, P), :]

        def load(j, q):
            sp.dma_start(xin[:, q, :], rows(t["rows_in"], j)).then_inc(x_in[q], 16)

        def step(j, q):
            sp.wait_ge(x_turned, j - DEEP + 1)
            load(j, q)

        for j in range(DEEP):
            load(j, j)
        in_steps(sp, DEEP, NU, step, DEEP)
        for q, s in enumerate(y_saved):
            sp.wait_ge(s, 16 * len(range(q, NU, DEEP)))

    @block.tensor
    def _(pe):
        def turn_x(j, q, early=False):
            pe.wait_ge(x_in[q], 16 // DEEP * (j - q) + 16)
            if not early:
                pe.wait_ge(xT_ready, j - 1)
            for k in range(KD):
                mm = pe.transpose(x_ps[q % 2][:, P * k:P * k + P], xin[:, q, P * k:P * k + P], ident[:, :])
            mm.then_inc(x_turned, 1)

        def of_experts(i):
            word = pe.value_load(packed[0:1, bass.ds(i, 1)], min_val=0, max_val=E ** 6 - 1)
            return [(word // E ** k) % E for k in range(6)]

        def up(j, q, e, early=False):
            pe.wait_ge(xT_ready, j + 1)
            if not early:
                pe.wait_ge(h_ready, j - 1)
            for c in range(HC):
                for k in range(KD):
                    mm = pe.matmul(h_ps[q % 2][:, P * c:P * c + P],
                                   t["w_up"][:, bass.ds(e, 1), k, P * c:P * c + P].rearrange("p o n -> p (o n)"),
                                   xT[:, q % 2, k, :], start=(k == 0), stop=(k == KD - 1))
            mm.then_inc(h_filled, 1)

        def down(j, q, e, early=False):
            pe.wait_ge(hsq_ready, j + 1)
            if not early:
                pe.wait_ge(y_ready, j - 1)
            for c in range(HC):
                mm = pe.matmul(y_ps[q % 2][:, 0:D], hsq[:, q % 2, c, :],
                               t["w_dn"][:, bass.ds(e, 1), c, :].rearrange("p o n -> p (o n)"),
                               start=(c == 0), stop=(c == HC - 1))
            mm.then_inc(y_filled, 1)

        def steps(i, e, places, early=False):
            for d in places:
                j = i * DEEP + (d + 1)
                turn_x(j + 2, (d + 3) % DEEP)
                up(j + 1, (d + 2) % DEEP, e[d + 2])
                down(j - 1, d, e[d], early and d < 2)

        turn_x(0, 0, True)
        turn_x(1, 1, True)
        e = of_experts(0)
        up(0, 0, e[0], True)
        turn_x(2, 2)
        up(1, 1, e[1], True)
        steps(0, e, range(DEEP), True)
        last = (NU - 2 - DEEP) // DEEP
        assert last % 2 == 0
        with pe.Fori(0, last // 2) as i:
            e = of_experts(i * 2 + 1)
            steps(i * 2 + 1, e, range(DEEP - 1))
            later = of_experts(i * 2 + 2)
            steps(i * 2 + 1, e, [DEEP - 1])
            steps(i * 2 + 2, later, range(DEEP))
        e = of_experts(last + 1)
        done = DEEP * (last + 1)
        for j in range(done + 1, NU + 1):
            if j + 2 < NU:
                turn_x(j + 2, (j + 2) % DEEP)
            if j + 1 < NU:
                up(j + 1, (j + 1) % DEEP, e[j + 1 - done])
            down(j - 1, (j - 1) % DEEP, e[j - 1 - done])

    @block.scalar
    def _(act):
        def take_x(j, q):
            act.wait_ge(x_turned, j + 1)
            act.activation(xT[:, q % 2, :, :], x_ps[q % 2][:, 0:D].rearrange("p (k n) -> p k n", k=KD), ACT.Copy).then_inc(xT_ready, 1)

        def relu(j, q, early=False):
            act.wait_ge(h_filled, j + 1)
            if not early:
                act.wait_ge(hsq_ready, j - 1)
            act.activation(h[:, q % 2, :, :].rearrange("p c n -> p (c n)"), h_ps[q % 2][:, 0:HIDP],
                           ACT.Relu).then_inc(h_ready, 1)

        def save(j, q):
            act.wait_ge(y_ready, j + 1)
            act.dma_start(t["rows_out"][bass.ds(j * P, P), :], y[:, q, :]).then_inc(y_saved[q], 16)

        def step(j, q):
            take_x(j, q)
            relu(j - 1, (q - 1) % DEEP)
            save(j - 4, q)

        take_x(0, 0)
        take_x(1, 1)
        relu(0, 0, True)
        take_x(2, 2)
        relu(1, 1, True)
        take_x(3, 3)
        relu(2, 2)
        in_steps(act, 4, NU, step, DEEP)
        relu(NU - 1, (NU - 1) % DEEP)
        for j in range(NU - 4, NU):
            save(j, j % DEEP)

    @block.vector
    def _(dve):
        def square(j, q, early=False):
            dve.wait_ge(h_ready, j + 1)
            if not early:
                dve.wait_ge(y_filled, j - 1)
            x = h[:, q % 2, :, :]
            dve.tensor_tensor(hsq[:, q % 2, :, :], x, x, ALU.mult).then_inc(hsq_ready, 1)

        def result(j, q, early=False):
            dve.wait_ge(y_filled, j + 1)
            if not early:
                dve.wait_ge(y_saved[q], 16 // DEEP * (j - q))
            dve.tensor_copy(y[:, q, :], y_ps[q % 2][:, 0:D]).then_inc(y_ready, 1)

        def step(j, q):
            square(j, q)
            result(j - 2, (q - 2) % DEEP)

        for j in range(DEEP + 2):
            square(j, j % DEEP, j < 2)
            if j >= 2:
                result(j - 2, j - 2, True)
        in_steps(dve, DEEP + 2, NU, step, DEEP)
        for j in (NU - 2, NU - 1):
            result(j, j % DEEP)


def rope_tables():
    inv = (1.0 / np.float32(10000.0) ** (np.arange(0, HD, 2, dtype=np.float32) / np.float32(HD))).astype(np.float32)
    angle = np.arange(S, dtype=np.float32)[:, None] * inv[None, :]
    gamma = 1.0 - 2.0 ** (-5.0 - np.arange(H))
    power = gamma[None, :] ** np.arange(S)[:, None]
    scale = np.concatenate([power, HD ** -0.5 / power], 1)
    return [(scale[:, :, None] * f(angle).astype(np.float32)[:, None, :]).astype(np.float32).reshape(S, 32 * 8)
            for f in (np.cos, np.sin)]


def vit_tower(nc, dram):
    with ExitStack() as ctx:
        htok = ctx.enter_context(nc.sbuf_tensor("htok", [P, NT, D], F32))
        ident = ctx.enter_context(nc.sbuf_tensor("ident", [P, P], F32))
        ident_bf = ctx.enter_context(nc.sbuf_tensor("ident_bf", [P, P], BF16))
        logits = ctx.enter_context(nc.sbuf_tensor("logits", [P, NT, E], F32))
        slot = ctx.enter_context(nc.sbuf_tensor("slot", [P, NT, 2], I32))
        weight = ctx.enter_context(nc.sbuf_tensor("weight", [P, NT, 2], F32))
        tables = {}

        def table(name, shape, src):
            tables[name] = ctx.enter_context(nc.sbuf_tensor(name, shape, F32))
            return tables[name][tuple(slice(None) for _ in shape)], src

        loads = [table("before", [P, P], dram["before"]),
                 table("iota", [P, NI], dram["iota"].partition_broadcast(P)),
                 table("upto", [P, E, E], dram["upto"].partition_broadcast(P)),
                 table("r0_b", [P, E], dram["r0_b"].partition_broadcast(P)),
                 table("r1_b", [P, E], dram["r1_b"].partition_broadcast(P))]
        ident_in = ctx.enter_context(nc.semaphore("ident_in"))
        tables_in = ctx.enter_context(nc.semaphore("tables_in"))
        set_up = ctx.enter_context(nc.semaphore("set_up"))
        cleared = [ctx.enter_context(nc.semaphore(f"cleared{i}")) for i in range(2)]
        clears = [NS * D // (ZCOLS * n) for n in (1, 2)]
        env = dict(htok=htok, logits=logits, ident=ident, ident_bf=ident_bf, tables_in=(tables_in, 16 * len(loads)),
                   slots_cleared=[(s, 16 * n) for s, n in zip(cleared, clears)], slot=slot, weight=weight,
                   experts_rows=dict(rows=dram["results0"], slot=slot, weight=weight), **tables)

        with ExitStack() as early:
            zeros = early.enter_context(nc.sbuf_tensor("zeros", [P, ZCOLS], F32))
            env["ret_weights"] = attention_weights(
                nc, "ret", early, dram, lambda name: ctx.enter_context(nc.semaphore(f"ret_{name}")))

            later = [(dst, src, tables_in) for dst, src in loads]
            w = env["ret_weights"]
            later += [(dst, src, w[f"{which}_in"]) for which in ("first", "rest") for dst, src in w[which]]
            for layer, zero in enumerate((zeros[:, :], zeros[:, :].bitcast(BF16))):
                flat = dram[f"slots{layer}"].rearrange("(p r) d -> p (r d)", p=P)
                per = ZCOLS * (layer + 1)
                later += [(flat[:, c * per:(c + 1) * per], zero, cleared[layer]) for c in range(clears[layer])]
            env["tok_spare"] = later
            with nc.Block() as block:
                @block.sync
                def _(sp):
                    sp.dma_start(ident[:, :], dram["ident"]).then_inc(ident_in, 16)

                @block.vector
                def _(dve):
                    dve.memset(zeros[:, :], 0.0).then_inc(set_up, 1)
                    dve.wait_ge(ident_in, 16)
                    dve.tensor_copy(ident_bf[:, :], ident[:, :]).then_inc(set_up, 1)

            attention(nc, "tok", env, dram)
            attention(nc, "ret", env, dram)
        moe(nc, 0, env, dram)
        attention(nc, "rms", env, dram)
        moe(nc, 1, env, dram)


def kernel(**inputs):
    import numpy as _np
    import concourse.bacc as _bacc
    from concourse import mybir as _mybir
    from concourse.bass_utils import run_bass_kernel_spmd as _run

    I = {k: _np.asarray(a) for k, a in inputs.items()}
    w_qkv = I["L0_tok_w_qkv"].reshape(H, 3, HD, D).transpose(1, 0, 2, 3).reshape(3 * D, D).T
    b_qkv = I["L0_tok_b_qkv"].reshape(H, 3, HD).transpose(1, 0, 2).reshape(3 * D)
    cos, sin = rope_tables()

    def wide(a, axis):
        pad = [(0, 0)] * a.ndim
        pad[axis] = (0, HIDP - HID)
        return _np.pad(a, pad)

    arrays = {
        "x": I["x"].reshape(B * S, D).T,
        "tok_w_in": w_qkv,
        "tok_b_qk": b_qkv[:2 * D].reshape(4, P).T,
        "tok_b_v": b_qkv[2 * D:],
        "tok_w_o": I["L0_tok_w_out"].T,
        "tok_b_o": I["L0_tok_b_out"],
        "ret_w_in": _np.concatenate([I["L0_attn_wq"].T, I["L0_attn_wk"].T, I["L0_attn_wv"].T, I["L0_attn_wg"].T], 1),
        "ret_w_o": I["L0_attn_wo"].T,
        "ret_router": I["L0_ffn_router_weight"].T,
        "r0_b": I["L0_ffn_router_bias"],
        "m0_w_gu": I["L0_ffn_gate_up_proj"],
        "m0_w_dn": I["L0_ffn_down_proj"],
        "m0_b_gu": I["L0_ffn_gate_up_bias"],
        "m0_b_dn": I["L0_ffn_down_bias"],
        "rms_w_in": _np.concatenate([I["L1_attn_Wq"][:, :D], I["L1_attn_Wk"], I["L1_attn_Wv"], I["L1_attn_Wq"][:, D:]], 1),
        "rms_b_in": _np.concatenate([I["L1_attn_bq"][:D], I["L1_attn_bk"], I["L1_attn_bv"], I["L1_attn_bq"][D:]]),
        "rms_norm_w": _np.tile(_np.stack([I["L1_attn_qn_w"], I["L1_attn_kn_w"]], 1), (P // HD, 1)),
        "rms_w_o": I["L1_attn_Wo"],
        "rms_b_o": I["L1_attn_bo"],
        "rms_router": I["L1_ffn_gate_w"].T,
        "r1_b": I["L1_ffn_expert_bias"],
        "m1_w_up": wide(I["L1_ffn_w_up"].transpose(0, 2, 1), 2),
        "m1_w_dn": wide(I["L1_ffn_w_down"].transpose(0, 2, 1), 1),
        "s_up": wide(I["L1_ffn_shared_w_up"].T, 1),
        "s_dn": wide(I["L1_ffn_shared_w_down"].T, 0),
        "cos": cos,
        "sin": sin,
        "causal": _np.triu(_np.ones((P, P), _np.float32)),
        "ident": _np.eye(P, dtype=_np.float32),
        "iota": _np.arange(NI, dtype=_np.float32),
        "before": _np.triu(_np.ones((P, P), _np.float32), 1),
        "upto": _np.tril(_np.ones((E, E), _np.float32)).reshape(E * E),
    }
    nc = _bacc.Bacc("TRN2", target_bir_lowering=False, num_devices=1)
    arrays = {f"in_{k}": _np.ascontiguousarray(a) for k, a in arrays.items()}
    dram = {k[3:]: nc.dram_tensor(k, a.shape, _mybir.dt.from_np(a.dtype), kind="ExternalInput").ap()
            for k, a in arrays.items()}
    dram["out"] = nc.dram_tensor("out_0", (B * S, D), F32, kind="ExternalOutput").ap()
    dram["scratch"] = nc.dram_tensor("scratch", (B, 2, SK, H, S), BF16, kind="Internal").ap()
    for layer, dt in ((0, F32), (1, BF16)):
        dram[f"slots{layer}"] = nc.dram_tensor(f"slots{layer}", (NS * P, D), dt, kind="Internal").ap()
        dram[f"results{layer}"] = nc.dram_tensor(f"results{layer}", (NU * P, D), dt, kind="Internal").ap()
    vit_tower(nc, dram)
    r = _run(nc, [arrays], core_ids=[0])
    return r.results[0]["out_0"].reshape(B, S, D)
```
